# Optimizing a Trainium2 kernel written in Bass

```python
import numpy as np
import jax
import jax.numpy as jnp

def _softmax(x, axis=-1):
    return jax.nn.softmax(x, axis=axis)

def _gelu(x):
    return jax.nn.gelu(x, approximate=True)

def _silu(x):
    return jax.nn.silu(x)

def _sigmoid(x):
    return jax.nn.sigmoid(x)

def _layernorm(x, axis=-1, eps=1e-05):
    m = jnp.mean(x, axis=axis, keepdims=True)
    v = jnp.var(x, axis=axis, keepdims=True)
    return (x - m) / jnp.sqrt(v + eps)

def _scatter_add(tgt, idx, src, axis=0):
    return tgt.at[idx].add(src)

def _segment_sum(src, seg, n):
    return jax.ops.segment_sum(src, seg, n)
kernel_name = 'mk_vit_tower_cls_d4_tok_img768_r4_6d49c2'

def setup_inputs(seed: int=0):
    np.random.seed(seed)
    _w = jnp.asarray

    def _rec_inputs():
        import jax
        import jax.numpy as jnp
        _rk = jax.random.key(seed)
        x = -0.000356955 + 1 * jax.random.normal(jax.random.fold_in(_rk, 1), (32, 3, 64, 64), jnp.float32)
        cls_tok = 0.02 * jax.random.normal(jax.random.fold_in(_rk, 5), (1, 1, 192), jnp.float32)
        return (x, cls_tok)
    x, cls_tok = _rec_inputs()

    def _L0_tok_setup():
        import jax, jax.numpy as jnp
        import numpy as np
        PATCH = 16
        EMBED = 192
        IN_DIM = PATCH * PATCH * 3

        def extract_patches(x, p):
            B, C, H, Wd = x.shape
            h, w = (H // p, Wd // p)
            xr = x.reshape(B, C, h, p, w, p)
            xr = xr.transpose(0, 2, 4, 3, 5, 1)
            return xr.reshape(B, h * w, p * p * C)
        key = jax.random.key(seed)
        kx, kw, kb = jax.random.split(key, 3)
        x = jax.random.normal(kx, (128, 3, 224, 224), dtype=jnp.float32)
        bound = 1.0 / np.sqrt(IN_DIM)
        W = jax.random.uniform(kw, (EMBED, IN_DIM), jnp.float32, -bound, bound)
        b = jax.random.uniform(kb, (EMBED,), jnp.float32, -bound, bound)
        return {'x': x, 'W': W, 'b': b}
    _L0_tok_all = _L0_tok_setup()
    _L0_tok_in = {k: v for k, v in _L0_tok_all.items() if k in ('W', 'b')}
    del _L0_tok_all

    def _L0_attn_setup():
        import jax, jax.numpy as jnp
        import numpy as np
        EMBED_DIM = 192
        NUM_HEADS = 12
        HEAD_DIM = EMBED_DIM // NUM_HEADS
        MAX_WAVELENGTH = 10000.0
        ROPE_PERCENT = 0.5

        def p_rope(x, positions):
            rope_angles = int(ROPE_PERCENT * HEAD_DIM) // 2
            nope_angles = HEAD_DIM // 2 - rope_angles
            fraction = 2.0 * jnp.arange(rope_angles, dtype=x.dtype) / HEAD_DIM
            timescale = MAX_WAVELENGTH ** fraction
            timescale = jnp.concatenate([timescale, jnp.full((nope_angles,), jnp.inf, dtype=x.dtype)])
            sinusoid = positions[:, None] / timescale[None, :]
            sin, cos = (jnp.sin(sinusoid), jnp.cos(sinusoid))
            x1, x2 = jnp.split(x, 2, axis=-1)
            return jnp.concatenate([x1 * cos - x2 * sin, x2 * cos + x1 * sin], axis=-1)

        def _shape(x, B, S):
            return x.reshape(B, S, NUM_HEADS, HEAD_DIM).transpose(0, 2, 1, 3).reshape(B * NUM_HEADS, S, HEAD_DIM)
        key = jax.random.key(seed)
        ks = jax.random.split(key, 9)
        B, T, E = (16, 256, EMBED_DIM)
        s = 0.02
        return {'hidden_states': jax.random.normal(ks[0], (B, T, E), jnp.float32), 'wq': jax.random.normal(ks[1], (E, E), jnp.float32) * s, 'bq': jax.random.normal(ks[2], (E,), jnp.float32) * s, 'wk': jax.random.normal(ks[3], (E, E), jnp.float32) * s, 'bk': jax.random.normal(ks[4], (E,), jnp.float32) * s, 'wv': jax.random.normal(ks[5], (E, E), jnp.float32) * s, 'bv': jax.random.normal(ks[6], (E,), jnp.float32) * s, 'wo': jax.random.normal(ks[7], (E, E), jnp.float32) * s, 'bo': jax.random.normal(ks[8], (E,), jnp.float32) * s}
    _L0_attn_all = _L0_attn_setup()
    _L0_attn_in = {k: v for k, v in _L0_attn_all.items() if k in ('wq', 'bq', 'wk', 'bk', 'wv', 'bv', 'wo', 'bo')}
    del _L0_attn_all

    def _L0_ffn_setup():
        import jax, jax.numpy as jnp
        import numpy as np
        DIM = 192
        HID = 128
        E = 16
        G = 8
        TOPK_G = 4
        TOPK_E = 4
        SCALE = 2.5
        B, S = (2, 512)
        key = jax.random.key(seed)
        ks = jax.random.split(key, 9)
        init = lambda k, shape: jax.random.normal(k, shape, dtype=jnp.float32) * 0.02
        z = lambda shape: jnp.zeros(shape, jnp.float32)
        return {'x': jax.random.normal(ks[0], (B, S, DIM), dtype=jnp.float32), 'gate_w': init(ks[1], (DIM, E)), 'gate_b': z((E,)), 'bias': z((E,)), 'Wu': init(ks[2], (E, DIM, HID)), 'bu': z((E, HID)), 'Wg': init(ks[3], (E, DIM, HID)), 'bg': z((E, HID)), 'Wd': init(ks[4], (E, HID, DIM)), 'bd': z((E, DIM)), 'sWu': init(ks[5], (DIM, HID)), 'sbu': z((HID,)), 'sWg': init(ks[6], (DIM, HID)), 'sbg': z((HID,)), 'sWd': init(ks[7], (HID, DIM)), 'sbd': z((DIM,))}
    _L0_ffn_all = _L0_ffn_setup()
    _L0_ffn_in = {k: v for k, v in _L0_ffn_all.items() if k in ('gate_w', 'gate_b', 'bias', 'Wu', 'bu', 'Wg', 'bg', 'Wd', 'bd', 'sWu', 'sbu', 'sWg', 'sbg', 'sWd', 'sbd')}
    del _L0_ffn_all

    def _L1_attn_setup():
        import jax, jax.numpy as jnp
        import numpy as np
        B, P, D = (16, 256, 192)
        key = jax.random.key(seed)
        k1, k2 = jax.random.split(key)
        p = jax.random.normal(k1, (B, P, D), dtype=jnp.float32)
        w = jax.random.normal(k2, (1, 3 * D), dtype=jnp.float32) * 0.05
        return {'p': p, 'w': w}
    _L1_attn_all = _L1_attn_setup()
    _L1_attn_in = {k: v for k, v in _L1_attn_all.items() if k in ('w',)}
    del _L1_attn_all

    def _L1_ffn_setup():
        import jax, jax.numpy as jnp
        import numpy as np
        from jax import lax
        DIM = 192
        INTER = 128
        E = 8
        G = 4
        TOPK_G = 2
        TOPK = 2
        ROUTE_SCALE = 1.0

        def _gate(x2, gate_weight, gate_bias):
            T = x2.shape[0]
            scores = jax.nn.sigmoid(x2 @ gate_weight.T)
            s = scores + gate_bias
            sv = s.reshape(T, G, E // G)
            top2, _ = lax.top_k(sv, 2)
            group_scores = top2.sum(-1)
            _, gidx = lax.top_k(group_scores, TOPK_G)
            gmask = jnp.zeros((T, G), bool).at[jnp.arange(T)[:, None], gidx].set(True)
            masked = jnp.where(gmask[:, :, None], sv, -jnp.inf).reshape(T, E)
            _, idx = lax.top_k(masked, TOPK)
            w = jnp.take_along_axis(scores, idx, axis=1)
            w = w / (w.sum(-1, keepdims=True) + 1e-06) * ROUTE_SCALE
            return (w, idx)
        key = jax.random.key(seed)
        ks = jax.random.split(key, 9)
        s = 1.0 / np.sqrt(DIM)
        si = 1.0 / np.sqrt(INTER)
        return {'x': jax.random.normal(ks[0], (4, 1024, DIM), jnp.float32), 'gate_weight': jax.random.uniform(ks[1], (E, DIM), jnp.float32, -s, s), 'gate_bias': jnp.zeros((E,), jnp.float32), 'w1': jax.random.uniform(ks[2], (E, INTER, DIM), jnp.float32, -s, s), 'w2': jax.random.uniform(ks[3], (E, DIM, INTER), jnp.float32, -si, si), 'w3': jax.random.uniform(ks[4], (E, INTER, DIM), jnp.float32, -s, s), 'sw1': jax.random.uniform(ks[5], (INTER, DIM), jnp.float32, -s, s), 'sw2': jax.random.uniform(ks[6], (DIM, INTER), jnp.float32, -si, si), 'sw3': jax.random.uniform(ks[7], (INTER, DIM), jnp.float32, -s, s)}
    _L1_ffn_all = _L1_ffn_setup()
    _L1_ffn_in = {k: v for k, v in _L1_ffn_all.items() if k in ('gate_weight', 'gate_bias', 'w1', 'w2', 'w3', 'sw1', 'sw2', 'sw3')}
    del _L1_ffn_all

    def _L2_attn_setup():
        import jax, jax.numpy as jnp
        import numpy as np
        B, N, C = (2, 1024, 192)
        H = 12
        HD = C // H
        THETA = 10000.0

        def _rope_tables(n, hd, dtype):
            inv = 1.0 / THETA ** (jnp.arange(0, hd, 2, dtype=jnp.float32) / hd)
            freqs = jnp.arange(n, dtype=jnp.float32)[:, None] * inv[None, :]
            cos = jnp.concatenate([jnp.cos(freqs), jnp.cos(freqs)], axis=-1).astype(dtype)
            sin = jnp.concatenate([jnp.sin(freqs), jnp.sin(freqs)], axis=-1).astype(dtype)
            return (cos, sin)

        def _rotate_half(x):
            x1, x2 = (x[..., :x.shape[-1] // 2], x[..., x.shape[-1] // 2:])
            return jnp.concatenate([-x2, x1], axis=-1)
        key = jax.random.key(seed)
        k1, k2, k3 = jax.random.split(key, 3)
        x = jax.random.normal(k1, (B, N, C), dtype=jnp.float32)
        w_qkv = jax.random.normal(k2, (3 * C, C), dtype=jnp.float32) * C ** (-0.5)
        b_qkv = jnp.zeros((3 * C,), dtype=jnp.float32)
        w_proj = jax.random.normal(k3, (C, C), dtype=jnp.float32) * C ** (-0.5)
        b_proj = jnp.zeros((C,), dtype=jnp.float32)
        return {'x': x, 'w_qkv': w_qkv, 'b_qkv': b_qkv, 'w_proj': w_proj, 'b_proj': b_proj}
    _L2_attn_all = _L2_attn_setup()
    _L2_attn_in = {k: v for k, v in _L2_attn_all.items() if k in ('w_qkv', 'b_qkv', 'w_proj', 'b_proj')}
    del _L2_attn_all

    def _L2_ffn_setup():
        import jax, jax.numpy as jnp
        import numpy as np
        E = 16
        K = 4
        H = 192
        I = 384
        LIMIT = 7.0
        ALPHA = 1.702
        EPS = 1e-05

        def rmsnorm(x, scale):
            xf = x.astype(jnp.float32)
            inv = jax.lax.rsqrt(jnp.mean(xf * xf, axis=-1, keepdims=True) + EPS)
            return (xf * inv).astype(x.dtype) * scale

        def swiglu(x, limit=LIMIT, alpha=ALPHA):
            x_glu = x[..., ::2]
            x_lin = x[..., 1::2]
            x_glu = jnp.minimum(x_glu, limit)
            x_lin = jnp.clip(x_lin, -limit, limit)
            return x_glu * jax.nn.sigmoid(alpha * x_glu) * (x_lin + 1.0)
        key = jax.random.key(seed)
        ks = jax.random.split(key, 7)
        s = 0.02
        return {'x': jax.random.normal(ks[0], (2, 256, H), dtype=jnp.float32), 'norm_scale': jnp.ones((H,), dtype=jnp.float32), 'gate_w': jax.random.normal(ks[1], (E, H), dtype=jnp.float32) * s, 'gate_b': jnp.zeros((E,), dtype=jnp.float32), 'mlp1_w': jax.random.normal(ks[2], (E, 2 * I, H), dtype=jnp.float32) * s, 'mlp1_b': jax.random.normal(ks[3], (E, 2 * I), dtype=jnp.float32) * s, 'mlp2_w': jax.random.normal(ks[4], (E, H, I), dtype=jnp.float32) * s, 'mlp2_b': jax.random.normal(ks[5], (E, H), dtype=jnp.float32) * s}
    _L2_ffn_all = _L2_ffn_setup()
    _L2_ffn_in = {k: v for k, v in _L2_ffn_all.items() if k in ('norm_scale', 'gate_w', 'gate_b', 'mlp1_w', 'mlp1_b', 'mlp2_w', 'mlp2_b')}
    del _L2_ffn_all

    def _L3_attn_setup():
        import jax, jax.numpy as jnp
        import numpy as np
        B, L, D = (4, 512, 192)
        H, K = (12, 9)
        IPG = D // H
        PAD = (K - 1) // 2

        def _sdconv(query, dw_w, pw_w, pw_b, ak_w, ak_b, pt_w, pt_b):
            b, l, d = query.shape
            x = query.transpose(0, 2, 1)
            dw = jax.lax.conv_general_dilated(x, dw_w, window_strides=(1,), padding=[(PAD, PAD)], feature_group_count=d, dimension_numbers=('NCH', 'OIH', 'NCH'))
            dwg = dw.reshape(b, H, IPG, l)
            pw = jnp.einsum('bhil,hoi->bhol', dwg, pw_w).reshape(b, d, l) + pw_b[None, :, None]
            key_conv_attn = pw.transpose(0, 2, 1)
            conv_attn = key_conv_attn * query
            ca = conv_attn.reshape(b, l, H, IPG)
            kern = jnp.einsum('blhi,hki->blhk', ca, ak_w) + ak_b.reshape(H, K)
            w = jax.nn.softmax(kern, axis=-1)
            v = query @ pt_w.T + pt_b
            vp = jnp.pad(v, ((0, 0), (PAD, PAD), (0, 0)))
            idx = jnp.arange(l)[:, None] + jnp.arange(K)[None, :]
            win = vp[:, idx]
            winh = win.reshape(b, l, K, H, IPG)
            out = jnp.einsum('blkhd,blhk->blhd', winh, w).reshape(b, l, d)
            return out
        key = jax.random.key(seed)
        ks = jax.random.split(key, 8)
        s = lambda k, shape, scale: jax.random.normal(k, shape, dtype=jnp.float32) * scale
        return {'query': s(ks[0], (B, L, D), 1.0), 'dw_w': s(ks[1], (D, 1, K), 0.1), 'pw_w': s(ks[2], (H, IPG, IPG), 0.05), 'pw_b': s(ks[3], (D,), 0.02), 'ak_w': s(ks[4], (H, K, IPG), 0.05), 'ak_b': s(ks[5], (H * K,), 0.02), 'pt_w': s(ks[6], (D, D), 0.02), 'pt_b': s(ks[7], (D,), 0.02)}
    _L3_attn_all = _L3_attn_setup()
    _L3_attn_in = {k: v for k, v in _L3_attn_all.items() if k in ('dw_w', 'pw_w', 'pw_b', 'ak_w', 'ak_b', 'pt_w', 'pt_b')}
    del _L3_attn_all

    def _L3_ffn_setup():
        import jax, jax.numpy as jnp
        import numpy as np
        E = 8
        K = 2
        D = 192
        F = 4 * D
        key = jax.random.key(seed)
        ks = jax.random.split(key, 10)
        s_exp = 0.02
        return {'x': jax.random.normal(ks[0], (4, 256, D), jnp.float32), 'W1': jax.random.normal(ks[1], (E, F, D), jnp.float32) * s_exp, 'b1': jax.random.normal(ks[2], (E, F), jnp.float32) * s_exp, 'W2': jax.random.normal(ks[3], (E, D, F), jnp.float32) * s_exp, 'b2': jax.random.normal(ks[4], (E, D), jnp.float32) * s_exp, 'Wr1': jax.random.normal(ks[5], (D, D), jnp.float32) * s_exp, 'br1': jax.random.normal(ks[6], (D,), jnp.float32) * s_exp, 'Wr2': jax.random.normal(ks[7], (E, D), jnp.float32) * s_exp, 'br2': jax.random.normal(ks[8], (E,), jnp.float32) * s_exp}
    _L3_ffn_all = _L3_ffn_setup()
    _L3_ffn_in = {k: v for k, v in _L3_ffn_all.items() if k in ('W1', 'b1', 'W2', 'b2', 'Wr1', 'br1', 'Wr2', 'br2')}
    del _L3_ffn_all
    return {'x': x, 'cls_tok': cls_tok, 'L0_tok_W': _L0_tok_in['W'], 'L0_tok_b': _L0_tok_in['b'], 'L0_attn_wq': _L0_attn_in['wq'], 'L0_attn_bq': _L0_attn_in['bq'], 'L0_attn_wk': _L0_attn_in['wk'], 'L0_attn_bk': _L0_attn_in['bk'], 'L0_attn_wv': _L0_attn_in['wv'], 'L0_attn_bv': _L0_attn_in['bv'], 'L0_attn_wo': _L0_attn_in['wo'], 'L0_attn_bo': _L0_attn_in['bo'], 'L0_ffn_gate_w': _L0_ffn_in['gate_w'], 'L0_ffn_gate_b': _L0_ffn_in['gate_b'], 'L0_ffn_bias': _L0_ffn_in['bias'], 'L0_ffn_Wu': _L0_ffn_in['Wu'], 'L0_ffn_bu': _L0_ffn_in['bu'], 'L0_ffn_Wg': _L0_ffn_in['Wg'], 'L0_ffn_bg': _L0_ffn_in['bg'], 'L0_ffn_Wd': _L0_ffn_in['Wd'], 'L0_ffn_bd': _L0_ffn_in['bd'], 'L0_ffn_sWu': _L0_ffn_in['sWu'], 'L0_ffn_sbu': _L0_ffn_in['sbu'], 'L0_ffn_sWg': _L0_ffn_in['sWg'], 'L0_ffn_sbg': _L0_ffn_in['sbg'], 'L0_ffn_sWd': _L0_ffn_in['sWd'], 'L0_ffn_sbd': _L0_ffn_in['sbd'], 'L1_attn_w': _L1_attn_in['w'], 'L1_ffn_gate_weight': _L1_ffn_in['gate_weight'], 'L1_ffn_gate_bias': _L1_ffn_in['gate_bias'], 'L1_ffn_w1': _L1_ffn_in['w1'], 'L1_ffn_w2': _L1_ffn_in['w2'], 'L1_ffn_w3': _L1_ffn_in['w3'], 'L1_ffn_sw1': _L1_ffn_in['sw1'], 'L1_ffn_sw2': _L1_ffn_in['sw2'], 'L1_ffn_sw3': _L1_ffn_in['sw3'], 'L2_attn_w_qkv': _L2_attn_in['w_qkv'], 'L2_attn_b_qkv': _L2_attn_in['b_qkv'], 'L2_attn_w_proj': _L2_attn_in['w_proj'], 'L2_attn_b_proj': _L2_attn_in['b_proj'], 'L2_ffn_norm_scale': _L2_ffn_in['norm_scale'], 'L2_ffn_gate_w': _L2_ffn_in['gate_w'], 'L2_ffn_gate_b': _L2_ffn_in['gate_b'], 'L2_ffn_mlp1_w': _L2_ffn_in['mlp1_w'], 'L2_ffn_mlp1_b': _L2_ffn_in['mlp1_b'], 'L2_ffn_mlp2_w': _L2_ffn_in['mlp2_w'], 'L2_ffn_mlp2_b': _L2_ffn_in['mlp2_b'], 'L3_attn_dw_w': _L3_attn_in['dw_w'], 'L3_attn_pw_w': _L3_attn_in['pw_w'], 'L3_attn_pw_b': _L3_attn_in['pw_b'], 'L3_attn_ak_w': _L3_attn_in['ak_w'], 'L3_attn_ak_b': _L3_attn_in['ak_b'], 'L3_attn_pt_w': _L3_attn_in['pt_w'], 'L3_attn_pt_b': _L3_attn_in['pt_b'], 'L3_ffn_W1': _L3_ffn_in['W1'], 'L3_ffn_b1': _L3_ffn_in['b1'], 'L3_ffn_W2': _L3_ffn_in['W2'], 'L3_ffn_b2': _L3_ffn_in['b2'], 'L3_ffn_Wr1': _L3_ffn_in['Wr1'], 'L3_ffn_br1': _L3_ffn_in['br1'], 'L3_ffn_Wr2': _L3_ffn_in['Wr2'], 'L3_ffn_br2': _L3_ffn_in['br2']}

def reference(x, cls_tok, L0_tok_W, L0_tok_b, L0_attn_wq, L0_attn_bq, L0_attn_wk, L0_attn_bk, L0_attn_wv, L0_attn_bv, L0_attn_wo, L0_attn_bo, L0_ffn_gate_w, L0_ffn_gate_b, L0_ffn_bias, L0_ffn_Wu, L0_ffn_bu, L0_ffn_Wg, L0_ffn_bg, L0_ffn_Wd, L0_ffn_bd, L0_ffn_sWu, L0_ffn_sbu, L0_ffn_sWg, L0_ffn_sbg, L0_ffn_sWd, L0_ffn_sbd, L1_attn_w, L1_ffn_gate_weight, L1_ffn_gate_bias, L1_ffn_w1, L1_ffn_w2, L1_ffn_w3, L1_ffn_sw1, L1_ffn_sw2, L1_ffn_sw3, L2_attn_w_qkv, L2_attn_b_qkv, L2_attn_w_proj, L2_attn_b_proj, L2_ffn_norm_scale, L2_ffn_gate_w, L2_ffn_gate_b, L2_ffn_mlp1_w, L2_ffn_mlp1_b, L2_ffn_mlp2_w, L2_ffn_mlp2_b, L3_attn_dw_w, L3_attn_pw_w, L3_attn_pw_b, L3_attn_ak_w, L3_attn_ak_b, L3_attn_pt_w, L3_attn_pt_b, L3_ffn_W1, L3_ffn_b1, L3_ffn_W2, L3_ffn_b2, L3_ffn_Wr1, L3_ffn_br1, L3_ffn_Wr2, L3_ffn_br2):
    import jax
    import jax.numpy as jnp

    def _L0_tok_ref(x, W, b):
        import jax, jax.numpy as jnp
        import numpy as np
        PATCH = 16
        EMBED = 192
        IN_DIM = PATCH * PATCH * 3

        def extract_patches(x, p):
            B, C, H, Wd = x.shape
            h, w = (H // p, Wd // p)
            xr = x.reshape(B, C, h, p, w, p)
            xr = xr.transpose(0, 2, 4, 3, 5, 1)
            return xr.reshape(B, h * w, p * p * C)
        patches = extract_patches(x, PATCH)
        return jnp.einsum('bnd,ed->bne', patches, W) + b

    def _L0_attn_ref(hidden_states, wq, bq, wk, bk, wv, bv, wo, bo):
        import jax, jax.numpy as jnp
        import numpy as np
        EMBED_DIM = 192
        NUM_HEADS = 12
        HEAD_DIM = EMBED_DIM // NUM_HEADS
        MAX_WAVELENGTH = 10000.0
        ROPE_PERCENT = 0.5

        def p_rope(x, positions):
            rope_angles = int(ROPE_PERCENT * HEAD_DIM) // 2
            nope_angles = HEAD_DIM // 2 - rope_angles
            fraction = 2.0 * jnp.arange(rope_angles, dtype=x.dtype) / HEAD_DIM
            timescale = MAX_WAVELENGTH ** fraction
            timescale = jnp.concatenate([timescale, jnp.full((nope_angles,), jnp.inf, dtype=x.dtype)])
            sinusoid = positions[:, None] / timescale[None, :]
            sin, cos = (jnp.sin(sinusoid), jnp.cos(sinusoid))
            x1, x2 = jnp.split(x, 2, axis=-1)
            return jnp.concatenate([x1 * cos - x2 * sin, x2 * cos + x1 * sin], axis=-1)

        def _shape(x, B, S):
            return x.reshape(B, S, NUM_HEADS, HEAD_DIM).transpose(0, 2, 1, 3).reshape(B * NUM_HEADS, S, HEAD_DIM)
        B, T, E = hidden_states.shape
        scaling = HEAD_DIM ** (-0.5)
        q = (hidden_states @ wq.T + bq) * scaling
        k = hidden_states @ wk.T + bk
        v = hidden_states @ wv.T + bv
        q = _shape(q, B, T)
        k = _shape(k, B, T)
        v = _shape(v, B, T)
        positions = jnp.arange(T, dtype=hidden_states.dtype)
        k = p_rope(k, positions)
        q = p_rope(q, positions)
        attn = jnp.einsum('bqd,bkd->bqk', q, k)
        attn = jax.nn.softmax(attn, axis=-1)
        out = jnp.einsum('bqk,bkd->bqd', attn, v)
        out = out.reshape(B, NUM_HEADS, T, HEAD_DIM).transpose(0, 2, 1, 3).reshape(B, T, E)
        return out @ wo.T + bo

    def _L0_ffn_ref(x, gate_w, gate_b, bias, Wu, bu, Wg, bg, Wd, bd, sWu, sbu, sWg, sbg, sWd, sbd):
        import jax, jax.numpy as jnp
        import numpy as np
        DIM = 192
        HID = 128
        E = 16
        G = 8
        TOPK_G = 4
        TOPK_E = 4
        SCALE = 2.5
        B, S = (2, 512)
        orig_shape = x.shape
        xt = x.reshape(-1, DIM)
        T = xt.shape[0]
        scores = jax.nn.softmax(xt @ gate_w + gate_b, axis=-1)
        orig_scores = jax.lax.stop_gradient(scores)
        s = scores + bias[None, :]
        s3 = s.reshape(T, G, E // G)
        group_scores = jax.lax.top_k(s3, 2)[0].sum(-1)
        gidx = jax.lax.top_k(group_scores, TOPK_G)[1]
        gmask = jnp.any(jnp.arange(G)[None, None, :] == gidx[:, :, None], axis=1)
        s_masked = jnp.where(gmask[:, :, None], s3, -jnp.inf).reshape(T, E)
        _, idx = jax.lax.top_k(s_masked, TOPK_E)
        w = jnp.take_along_axis(orig_scores, idx, axis=1) * SCALE
        w_full = jnp.zeros((T, E), xt.dtype).at[jnp.arange(T)[:, None], idx].add(w)
        up = jax.nn.silu(jnp.einsum('td,edh->teh', xt, Wu) + bu)
        gt = jnp.einsum('td,edh->teh', xt, Wg) + bg
        act = up * gt * w_full[:, :, None]
        y = jnp.einsum('teh,ehd->td', act, Wd) + w_full @ bd
        sh = jax.nn.silu(xt @ sWu + sbu) * (xt @ sWg + sbg)
        y = y + sh @ sWd + sbd
        return y.reshape(orig_shape)

    def _L1_attn_ref(p, w):
        import jax, jax.numpy as jnp
        import numpy as np
        B, P, D = (16, 256, 192)
        d = p.shape[-1]
        w1 = w[0, :d]
        w2 = w[0, d:2 * d]
        w3 = w[0, 2 * d:]
        a_j = p @ w1
        a_i = p @ w2
        a_ij = jnp.einsum('bid,bjd->bij', p * w3, p)
        A = a_ij + a_i[:, :, None] + a_j[:, None, :]
        sA = jax.nn.softmax(A, axis=2)
        return jnp.einsum('bij,bjd->bid', sA, p)

    def _L1_ffn_ref(x, gate_weight, gate_bias, w1, w2, w3, sw1, sw2, sw3):
        import jax, jax.numpy as jnp
        import numpy as np
        from jax import lax
        DIM = 192
        INTER = 128
        E = 8
        G = 4
        TOPK_G = 2
        TOPK = 2
        ROUTE_SCALE = 1.0

        def _gate(x2, gate_weight, gate_bias):
            T = x2.shape[0]
            scores = jax.nn.sigmoid(x2 @ gate_weight.T)
            s = scores + gate_bias
            sv = s.reshape(T, G, E // G)
            top2, _ = lax.top_k(sv, 2)
            group_scores = top2.sum(-1)
            _, gidx = lax.top_k(group_scores, TOPK_G)
            gmask = jnp.zeros((T, G), bool).at[jnp.arange(T)[:, None], gidx].set(True)
            masked = jnp.where(gmask[:, :, None], sv, -jnp.inf).reshape(T, E)
            _, idx = lax.top_k(masked, TOPK)
            w = jnp.take_along_axis(scores, idx, axis=1)
            w = w / (w.sum(-1, keepdims=True) + 1e-06) * ROUTE_SCALE
            return (w, idx)
        B, S, D = x.shape
        x2 = x.reshape(-1, D)
        T = x2.shape[0]
        weights, indices = _gate(x2, gate_weight, gate_bias)
        cw = jnp.zeros((T, E), x.dtype).at[jnp.arange(T)[:, None], indices].add(weights)
        h1 = jnp.einsum('td,eid->tei', x2, w1)
        h3 = jnp.einsum('td,eid->tei', x2, w3)
        h = jax.nn.silu(h1) * h3
        y = jnp.einsum('tei,edi,te->td', h, w2, cw)
        z = jax.nn.silu(x2 @ sw1.T) * (x2 @ sw3.T) @ sw2.T
        return (y + z).reshape(B, S, D)

    def _L2_attn_ref(x, w_qkv, b_qkv, w_proj, b_proj):
        import jax, jax.numpy as jnp
        import numpy as np
        B, N, C = (2, 1024, 192)
        H = 12
        HD = C // H
        THETA = 10000.0

        def _rope_tables(n, hd, dtype):
            inv = 1.0 / THETA ** (jnp.arange(0, hd, 2, dtype=jnp.float32) / hd)
            freqs = jnp.arange(n, dtype=jnp.float32)[:, None] * inv[None, :]
            cos = jnp.concatenate([jnp.cos(freqs), jnp.cos(freqs)], axis=-1).astype(dtype)
            sin = jnp.concatenate([jnp.sin(freqs), jnp.sin(freqs)], axis=-1).astype(dtype)
            return (cos, sin)

        def _rotate_half(x):
            x1, x2 = (x[..., :x.shape[-1] // 2], x[..., x.shape[-1] // 2:])
            return jnp.concatenate([-x2, x1], axis=-1)
        b, n, c = x.shape
        scale = HD ** (-0.5)
        qkv = jnp.einsum('bnc,dc->bnd', x, w_qkv) + b_qkv
        qkv = qkv.reshape(b, n, 3, H, HD).transpose(2, 0, 3, 1, 4)
        q, k, v = (qkv[0], qkv[1], qkv[2])
        cos, sin = _rope_tables(n, HD, x.dtype)
        q = q * cos + _rotate_half(q) * sin
        k = k * cos + _rotate_half(k) * sin
        attn = jnp.einsum('bhqd,bhkd->bhqk', q, k) * scale
        attn = jax.nn.softmax(attn, axis=-1)
        out = jnp.einsum('bhqk,bhkd->bhqd', attn, v)
        out = out.transpose(0, 2, 1, 3).reshape(b, n, c)
        return jnp.einsum('bnc,dc->bnd', out, w_proj) + b_proj

    def _L2_ffn_ref(x, norm_scale, gate_w, gate_b, mlp1_w, mlp1_b, mlp2_w, mlp2_b):
        import jax, jax.numpy as jnp
        import numpy as np
        E = 16
        K = 4
        H = 192
        I = 384
        LIMIT = 7.0
        ALPHA = 1.702
        EPS = 1e-05

        def rmsnorm(x, scale):
            xf = x.astype(jnp.float32)
            inv = jax.lax.rsqrt(jnp.mean(xf * xf, axis=-1, keepdims=True) + EPS)
            return (xf * inv).astype(x.dtype) * scale

        def swiglu(x, limit=LIMIT, alpha=ALPHA):
            x_glu = x[..., ::2]
            x_lin = x[..., 1::2]
            x_glu = jnp.minimum(x_glu, limit)
            x_lin = jnp.clip(x_lin, -limit, limit)
            return x_glu * jax.nn.sigmoid(alpha * x_glu) * (x_lin + 1.0)
        B, T, _ = x.shape
        t = rmsnorm(x, norm_scale)
        g = jnp.einsum('bth,eh->bte', t, gate_w) + gate_b
        top_vals, top_idx = jax.lax.top_k(g, K)
        route_w = jax.nn.softmax(top_vals, axis=-1)
        t_flat = t.reshape(B * T, H)
        idx_flat = top_idx.reshape(B * T, K)
        w_flat = route_w.reshape(B * T, K)
        onehot = jax.nn.one_hot(idx_flat, E, dtype=t_flat.dtype)
        comb = jnp.einsum('nke,nk->ne', onehot, w_flat)
        h = jnp.einsum('nh,ech->nec', t_flat, mlp1_w) + mlp1_b
        a = swiglu(h)
        y = jnp.einsum('nec,ehc->neh', a, mlp2_w) + mlp2_b
        out_flat = jnp.einsum('neh,ne->nh', y, comb)
        return x + out_flat.reshape(B, T, H)

    def _L3_attn_ref(query, dw_w, pw_w, pw_b, ak_w, ak_b, pt_w, pt_b):
        import jax, jax.numpy as jnp
        import numpy as np
        B, L, D = (4, 512, 192)
        H, K = (12, 9)
        IPG = D // H
        PAD = (K - 1) // 2

        def _sdconv(query, dw_w, pw_w, pw_b, ak_w, ak_b, pt_w, pt_b):
            b, l, d = query.shape
            x = query.transpose(0, 2, 1)
            dw = jax.lax.conv_general_dilated(x, dw_w, window_strides=(1,), padding=[(PAD, PAD)], feature_group_count=d, dimension_numbers=('NCH', 'OIH', 'NCH'))
            dwg = dw.reshape(b, H, IPG, l)
            pw = jnp.einsum('bhil,hoi->bhol', dwg, pw_w).reshape(b, d, l) + pw_b[None, :, None]
            key_conv_attn = pw.transpose(0, 2, 1)
            conv_attn = key_conv_attn * query
            ca = conv_attn.reshape(b, l, H, IPG)
            kern = jnp.einsum('blhi,hki->blhk', ca, ak_w) + ak_b.reshape(H, K)
            w = jax.nn.softmax(kern, axis=-1)
            v = query @ pt_w.T + pt_b
            vp = jnp.pad(v, ((0, 0), (PAD, PAD), (0, 0)))
            idx = jnp.arange(l)[:, None] + jnp.arange(K)[None, :]
            win = vp[:, idx]
            winh = win.reshape(b, l, K, H, IPG)
            out = jnp.einsum('blkhd,blhk->blhd', winh, w).reshape(b, l, d)
            return out
        return _sdconv(query, dw_w, pw_w, pw_b, ak_w, ak_b, pt_w, pt_b)

    def _L3_ffn_ref(x, W1, b1, W2, b2, Wr1, br1, Wr2, br2):
        import jax, jax.numpy as jnp
        import numpy as np
        E = 8
        K = 2
        D = 192
        F = 4 * D
        h = jax.nn.relu(jnp.einsum('bsd,hd->bsh', x, Wr1) + br1)
        score = jnp.einsum('bsd,ed->bse', h, Wr2) + br2
        _, idx = jax.lax.top_k(score, K)
        mask = (jax.nn.one_hot(idx, E) > 0).any(axis=-2)
        w = jax.nn.softmax(jnp.where(mask, score, -jnp.inf), axis=-1)
        out = jnp.zeros_like(x)
        for e in range(E):
            mid = jax.nn.relu(jnp.einsum('bsd,fd->bsf', x, W1[e]) + b1[e])
            ye = jnp.einsum('bsf,df->bsd', mid, W2[e]) + b2[e]
            out = out + w[..., e:e + 1] * ye
        return out
    h = _L0_tok_ref(x, L0_tok_W, L0_tok_b)
    h = jnp.concatenate([jnp.broadcast_to(cls_tok, (h.shape[0], 1, h.shape[2])), h], axis=1)
    h = h + _L0_attn_ref(_layernorm(h, axis=-1), L0_attn_wq, L0_attn_bq, L0_attn_wk, L0_attn_bk, L0_attn_wv, L0_attn_bv, L0_attn_wo, L0_attn_bo)
    h = h + _L0_ffn_ref(_layernorm(h, axis=-1), L0_ffn_gate_w, L0_ffn_gate_b, L0_ffn_bias, L0_ffn_Wu, L0_ffn_bu, L0_ffn_Wg, L0_ffn_bg, L0_ffn_Wd, L0_ffn_bd, L0_ffn_sWu, L0_ffn_sbu, L0_ffn_sWg, L0_ffn_sbg, L0_ffn_sWd, L0_ffn_sbd)
    h = h + _L1_attn_ref(_layernorm(h, axis=-1), L1_attn_w)
    h = h + _L1_ffn_ref(_layernorm(h, axis=-1), L1_ffn_gate_weight, L1_ffn_gate_bias, L1_ffn_w1, L1_ffn_w2, L1_ffn_w3, L1_ffn_sw1, L1_ffn_sw2, L1_ffn_sw3)
    h = h + _L2_attn_ref(_layernorm(h, axis=-1), L2_attn_w_qkv, L2_attn_b_qkv, L2_attn_w_proj, L2_attn_b_proj)
    h = h + _L2_ffn_ref(_layernorm(h, axis=-1), L2_ffn_norm_scale, L2_ffn_gate_w, L2_ffn_gate_b, L2_ffn_mlp1_w, L2_ffn_mlp1_b, L2_ffn_mlp2_w, L2_ffn_mlp2_b)
    h = h + _L3_attn_ref(_layernorm(h, axis=-1), L3_attn_dw_w, L3_attn_pw_w, L3_attn_pw_b, L3_attn_ak_w, L3_attn_ak_b, L3_attn_pt_w, L3_attn_pt_b)
    h = h + _L3_ffn_ref(_layernorm(h, axis=-1), L3_ffn_W1, L3_ffn_b1, L3_ffn_W2, L3_ffn_b2, L3_ffn_Wr1, L3_ffn_br1, L3_ffn_Wr2, L3_ffn_br2)
    return h

_drawn_inputs = setup_inputs


def setup_inputs(seed=0):
    import zlib

    import numpy as np

    out = dict(_drawn_inputs(seed))
    spreads = {'L0_ffn_gate_b': (0.0, 0.1),
     'L0_ffn_bias': (0.0, 0.1),
     'L0_ffn_bu': (0.0, 0.8),
     'L0_ffn_bg': (0.0, 0.8),
     'L0_ffn_bd': (0.0, 0.1),
     'L0_ffn_sbu': (0.0, 0.645),
     'L0_ffn_sbg': (0.0, 0.704),
     'L0_ffn_sbd': (0.0, 0.1),
     'L1_ffn_gate_bias': (0.0, 0.1),
     'L2_attn_b_qkv': (0.0, 0.1),
     'L2_attn_b_proj': (0.0, 0.1),
     'L2_ffn_norm_scale': (1.0, 0.6),
     'L2_ffn_gate_b': (0.0, 0.735)}
    factors = {'L0_attn_wq': 7.244,
     'L0_attn_bq': 8.0,
     'L0_attn_wk': 6.678,
     'L0_attn_bk': 8.0,
     'L0_ffn_Wu': 6.071,
     'L0_ffn_Wg': 6.823,
     'L0_ffn_Wd': 5.624,
     'L2_ffn_gate_w': 4.034,
     'L2_ffn_mlp1_w': 3.723,
     'L2_ffn_mlp1_b': 8.0,
     'L2_ffn_mlp2_w': 3.577,
     'L2_ffn_mlp2_b': 8.0,
     'L3_attn_dw_w': 8.0,
     'L3_attn_pw_w': 8.0,
     'L3_attn_pw_b': 64.0,
     'L3_attn_ak_w': 8.0,
     'L3_attn_ak_b': 64.0,
     'L3_attn_pt_b': 6.36,
     'L3_ffn_b1': 34.209,
     'L3_ffn_b2': 8.0,
     'L3_ffn_br1': 8.0,
     'L3_ffn_br2': 4.698,
     'L3_ffn_W1': 2.875}
    for name, (base, spread) in spreads.items():
        noise = np.random.default_rng([zlib.crc32(name.encode()), seed]).standard_normal(out[name].shape)
        drawn = base * np.exp(spread * noise) if base else spread * noise
        out[name] = jnp.asarray(drawn.astype(out[name].dtype))
    for name, factor in factors.items():
        out[name] = (out[name] * factor).astype(out[name].dtype)
    return out
```

```python
from contextlib import ExitStack

import numpy as np

import concourse.bass as bass
from concourse import mybir

F32 = mybir.dt.float32
F32R = mybir.dt.float32r
BF16 = mybir.dt.bfloat16
I32 = mybir.dt.int32
ALU = mybir.AluOpType
ACT = mybir.ActivationFunctionType
AX = mybir.AxisListType.X

IMAGES, PATCHES = 32, 16
SEQ = PATCHES + 1
TOKENS = IMAGES * SEQ
D = 192
KC = 96
CH = D // KC
PER_TILE = 7
TR = PER_TILE * SEQ
TILES = -(-IMAGES // PER_TILE)
TPAD = TILES * TR
LAST = TOKENS - (TILES - 1) * TR
HALF = TOKENS // 2
HEADS, HD = 12, 16
HPC = HEADS // CH
TAPS = 9
PAD = (TAPS - 1) // 2
LPAD = SEQ + TAPS - 1
IN_CH = 768 // 128
EPS = 1e-5
BIG = 2.0 ** 60
GMAX = 17

MOE = [
    dict(kind="silu", n=17, pairs=1, routed=16, top=4, groups=8, top_groups=4, shared=1, bias=True),
    dict(kind="silu", n=9, pairs=1, routed=8, top=2, groups=4, top_groups=2, shared=1, bias=False),
    dict(kind="swiglu", n=16, pairs=3, routed=16, top=4, groups=0, top_groups=0, shared=0, bias=True),
    dict(kind="relu", n=8, pairs=3, routed=8, top=2, groups=0, top_groups=0, shared=0, bias=True),
]
for _m in MOE:
    _m["units"] = 2 * _m["pairs"]
    _m["blocks"] = _m["pairs"] * (2 if _m["kind"] == "relu" else 1)
    _m["tail"] = _m["n"] % 2 == 0
    _m["loops"] = (_m["n"] - 1) // 2
MAXP, MAXB = 3, 6

PACKS = {
    "p_tok": [("tokw", 128, IN_CH * D), ("ind", 128, TPAD), ("tokb", 128, D), ("ident", 128, 128)],
    "p_l0": [("wqkv0", 97, CH * 3 * D), ("wo0", 97, CH * D), ("cos0", 128, HD), ("sin0", 128, HD),
             ("same_q", 128, TR), ("same_k", 128, 4 * TR), ("hmask", KC, HPC), ("onespad", TR, HPC * KC), ("gw0", 97, CH * 16), ("gb0", 128, 16),
             ("tri16", 128, 256), ("tri8", 128, 64), ("tri4", 128, 16), ("b2_0", 17, D)],
    "p_l1": [("w1v", KC, CH), ("w2v", KC, CH), ("w3v", KC, CH), ("ones", KC, TR), ("gw1", 97, CH * 8), ("gb1", 128, 8)],
    "p_l2": [("wqkv1", 97, CH * 3 * D), ("wo1", 97, CH * D), ("cos1", 128, HD), ("sin1", 128, HD),
             ("nscale", KC, CH), ("gw2", 97, CH * 16), ("b2_2", 16, D)],
    "p_l3": [("dww", KC, CH * TAPS), ("pww", KC, CH * KC), ("pwb", KC, CH), ("akw", 97, CH * TAPS * HPC),
             ("ptw", 97, CH * D), ("shift", TR, TAPS * TR), ("wr1", KC, CH * D), ("br1", KC, CH),
             ("gw3", 97, CH * 8), ("b2_3", 8, D)],
}


def vit_tower(nc, A, out):
    with ExitStack() as ctx:
        def sb(name, shape, dt=F32):
            return ctx.enter_context(nc.sbuf_tensor(name, shape, dt))

        def sem(name):
            return ctx.enter_context(nc.semaphore(name))

        V = {}
        packs = {}
        for p, items in PACKS.items():
            packs[p] = sb(p, [128, sum(c for _, _, c in items)])
            at = 0
            for name, rows, cols in items:
                V[name] = packs[p][:, at:at + cols]
                at += cols

        def v3(name, a):
            return V[name].rearrange("p (a b) -> p a b", a=a)

        maskA = sb("maskA", [128, TR], BF16)
        maskB = sb("maskB", [128, 4 * TR], BF16)
        h = sb("h", [128, TILES, D])
        xhat = sb("xhat", [128, TILES, D])
        xrms = sb("xrms", [128, TILES, D])
        xT = sb("xT", [128, CH, TPAD])
        st = sb("st", [128, TILES, 6])
        mv = sb("mv", [128, TILES, 2])
        nt = sb("nt", [128, 4, TILES])
        nti = sb("nti", [128, TILES], I32)
        rope = sb("rope", [128, 2, 2 * D])
        qk = sb("qk", [128, 2, 2 * D])
        qkT = sb("qkT", [128, 2, 2 * CH, TR])
        hidden_or_scores = sb("hidden_or_scores", [128, 2 * MAXB * TOKENS])
        patches = hidden_or_scores[:, 0:IN_CH * TPAD].rearrange("p (c r) -> p c r", c=IN_CH)
        n = 2 * HEADS * TR
        kmask = hidden_or_scores[:, 0:n].rearrange("p (b h r) -> p b h r", b=2, h=HEADS)
        prob = hidden_or_scores[:, n:2 * n].rearrange("p (b h r) -> p b h r", b=2, h=HEADS)
        probT_or_cmp = sb("probT_or_cmp", [128, n])
        probT = probT_or_cmp[:, :].rearrange("p (b h r) -> p b h r", b=2, h=HEADS)
        w = TILES * 256
        cmpg = probT_or_cmp[:, 0:w].rearrange("p (t a b) -> p t a b", t=TILES, a=16)
        cmpe = probT_or_cmp[:, w:2 * w].rearrange("p (t a b) -> p t a b", t=TILES, a=16)
        prod = probT_or_cmp[:, 0:TAPS * D].rearrange("p (k d) -> p k d", k=TAPS)
        vpad = sb("vpad", [128, 2, HEADS, KC])
        smax = sb("smax", [128, HEADS])
        rden = sb("rden", [128, CH, TR])
        oT = sb("oT", [128, CH, TR])
        uT = sb("uT", [128, CH, TPAD])
        aT = sb("aT", [128, CH, TPAD])
        nmax = sb("nmax", [128, TILES])
        psumr = sb("psumr", [128, TILES])
        rsum = sb("rsum", [128, TILES])
        xpad = sb("xpad", [128, CH, TILES * PER_TILE, LPAD])
        dwc = uT
        ca = sb("ca", [128, CH, TPAD])
        kern = sb("kern", [128, TILES, TAPS * HEADS])
        kexp = sb("kexp", [128, TILES, TAPS * HEADS])
        kmx = sb("kmx", [128, TILES, HEADS])
        vtok = sb("vtok", [128, TILES, D])
        conv = sb("conv", [128, D])
        W1 = sb("W1", [128, 2, CH, MAXP * 256])
        W1h = sb("W1h", [128, 2, CH, MAXP * 256], F32R)
        W1l = sb("W1l", [128, 2, CH, MAXP * 256], F32R)
        xh = sb("xh", [128, CH, TOKENS], F32R)
        xl = sb("xl", [128, CH, TOKENS], F32R)
        W2 = sb("W2", [128, 2, MAXB, D])
        act = hidden_or_scores[:, :].rearrange("p (b q r) -> p b q r", b=2, q=MAXB)
        gate = sb("gate", [128, 2, HALF])
        gsig = sb("gsig", [128, 2, HALF])
        lin = sb("lin", [128, 2, HALF])
        cw = sb("cw", [128, TILES, GMAX])
        lg = sb("lg", [128, TILES, 16])
        sc = sb("sc", [128, TILES, 16])
        sr = sb("sr", [128, TILES, 16])
        gsum = sb("gsum", [128, TILES, 8])
        pick = sb("pick", [128, TILES, 16])
        gpick = sb("gpick", [128, TILES, 8])
        rank = sb("rank", [128, TILES, 16])
        s5 = sb("s5", [128, 2, TILES])
        biases = sb("biases", [128, 2, 2 * MAXP])
        lin_bias = sb("lin_bias", [128, 2, MAXP])
        rT = aT
        cwT = sb("cwT", [128, TPAD])

        ps = ctx.enter_context(nc.psum_tensor("ps", [128, 8, 512], F32))

        packed = {p: sem("loaded_" + p) for p in PACKS}
        patches_in = [sem(f"patches_in{c}") for c in range(IN_CH)]
        masks_in = sem("masks_in")
        vec = sem("vec_step")
        act_step = sem("act_step")
        filled = sem("filled")
        tok_psum = sem("tok_psum")
        ln_ready = sem("ln_ready")
        xT_psum = sem("xT_psum")
        xT_ready = sem("xT_ready")
        qk_psum = sem("qk_psum")
        v_psum = sem("v_psum")
        rope_ready = sem("rope_ready")
        rope_used = sem("rope_used")
        qkT_psum = sem("qkT_psum")
        qkT_ready = sem("qkT_ready")
        kmask_ready = [sem("kmask0_ready"), sem("kmask1_ready")]
        v_ready = sem("v_ready")
        s_psum = sem("s_psum")
        sub_ready = sem("sub_ready")
        exp_ready = sem("exp_ready")
        pT_psum = sem("pT_psum")
        pT_ready = sem("pT_ready")
        o_psum = sem("o_psum")
        o_ready = sem("o_ready")
        proj_psum = sem("proj_psum")
        h_added = sem("h_added")
        tri_ready = sem("tri_ready")
        tri_psum = sem("tri_psum")
        tri_max = sem("tri_max")
        tri_exp = sem("tri_exp")
        triT_psum = sem("triT_psum")
        triT_ready = sem("triT_ready")
        trio_psum = sem("trio_psum")
        pad_ready = sem("pad_ready")
        dw_ready = sem("dw_ready")
        pw_psum = sem("pw_psum")
        ca_ready = sem("ca_ready")
        vt_psum = sem("vt_psum")
        vt_ready = sem("vt_ready")
        kern_psum = sem("kern_psum")
        kern_sub = sem("kern_sub")
        kern_exp = sem("kern_exp")
        shift_psum = sem("shift_psum")
        shift_used = sem("shift_used")
        r_psum = sem("r_psum")
        r_ready = sem("r_ready")
        gate_psum = sem("gate_psum")
        gate_in = sem("gate_in")
        gate_out = sem("gate_out")
        cw_ready = sem("cw_ready")
        cwT_psum = sem("cwT_psum")
        cwT_ready = sem("cwT_ready")
        bias_psum = sem("bias_psum")
        w1_loaded = [sem("w1_loaded0"), sem("w1_loaded1")]
        w1_high = sem("w1_high")
        w1_low = sem("w1_low")
        x_high = sem("x_high")
        x_low = sem("x_low")
        w2_loaded = [sem("w2_loaded0"), sem("w2_loaded1")]
        biases_loaded = [sem("biases_loaded0"), sem("biases_loaded1")]
        lin_bias_ready = sem("lin_bias_ready")
        hid_psum = sem("hid_psum")
        a_used = sem("a_used")
        b_used = sem("b_used")
        sig_ready = sem("sig_ready")
        glu_ready = sem("glu_ready")
        act_ready = sem("act_ready")
        y_psum = sem("y_psum")
        y_added = sem("y_added")
        h_done = sem("h_done")
        stored = sem("stored")

        for L, m in enumerate(MOE):
            prev = MOE[:L]
            m["u0"] = sum(p["n"] * p["units"] for p in prev)
            m["y0"] = sum(p["n"] * 3 for p in prev)
            m["q0"] = sum(p["n"] * p["pairs"] for p in prev)
            m["s0"] = sum(p["n"] * p["units"] for p in prev if p["kind"] == "swiglu")
            for b in range(2):
                m[f"w{b}"] = sum((p["n"] + b) // 2 for p in prev)
                m[f"b{b}"] = sum((p["n"] + b) // 2 for p in prev if p["bias"])

        def rows(t):
            return TR if t < TILES - 1 else LAST

        def need(eng, s, n):
            if n > 0:
                eng.wait_ge(s, n)

        block = ctx.enter_context(nc.Block())

        @block.sync
        def _(sp):
            sp.dma_start(packs["p_tok"][:, :], A["p_tok"][:, :]).then_inc(packed["p_tok"], 16)
            for c in range(IN_CH):
                sp.dma_start(patches[:, c, :], A["patches"][:, c, :]).then_inc(patches_in[c], 16)
            sp.dma_start(packs["p_l0"][:, :], A["p_l0"][:, :]).then_inc(packed["p_l0"], 16)

            def load_first(L, e, b):
                m = MOE[L]
                P = m["pairs"]
                if isinstance(e, int) and e < 2:
                    need(sp, w1_low, m["q0"])
                else:
                    sp.wait_ge(w1_low, (e - 1) * P + m["q0"])
                sp.dma_start(W1[0:KC, b, :, 0:P * 256], A[f"W1_{L}"][e, :, :, :]).then_inc(w1_loaded[b], 16)

            def load_rest(L, e, b):
                m = MOE[L]
                early = isinstance(e, int) and e < 2
                if m["bias"]:
                    for used in (a_used, b_used):
                        if early:
                            need(sp, used, m["u0"])
                        else:
                            sp.wait_ge(used, (e - 1) * m["units"] + m["u0"])
                    sp.dma_start(biases[:, b, 0:2 * m["pairs"]], A[f"bias_{L}"][e, :, :]).then_inc(biases_loaded[b], 16)
                if early:
                    need(sp, y_psum, m["y0"])
                else:
                    sp.wait_ge(y_psum, (e - 1) * 3 + m["y0"])
                sp.dma_start(W2[:, b, 0:m["blocks"], :], A[f"W2_{L}"][e, :, :, :]).then_inc(w2_loaded[b], 16)

            for L, m in enumerate(MOE):
                load_first(L, 0, 1)
                load_first(L, 1, 0)
                load_rest(L, 0, 1)
                load_rest(L, 1, 0)
                if L < 3:
                    p = f"p_l{L + 1}"
                    sp.dma_start(packs[p][:, :], A[p][:, :]).then_inc(packed[p], 16)
                load_first(L, 2, 1)
                load_first(L, 3, 0)
                load_rest(L, 2, 1)
                with sp.Fori(1, m["loops"] - 1) as i:
                    load_first(L, 2 * i + 2, 1)
                    load_rest(L, 2 * i + 1, 0)
                    load_first(L, 2 * i + 3, 0)
                    load_rest(L, 2 * i + 2, 1)
                n = m["n"]
                i = m["loops"] - 1
                load_first(L, 2 * i + 2, 1)
                load_rest(L, 2 * i + 1, 0)
                if m["tail"]:
                    load_first(L, 2 * i + 3, 0)
                load_rest(L, 2 * i + 2, 1)
                if m["tail"]:
                    load_rest(L, n - 1, 0)
            for t in range(TILES):
                sp.wait_ge(h_done, t + 1)
                sp.dma_start(out[t * TR:t * TR + rows(t), :], h[0:rows(t), t, :]).then_inc(stored, 16)
            sp.wait_ge(stored, 16 * TILES)

        @block.tensor
        def _(pe):
            def bank(i, r=TR, c0=0, c1=512):
                return ps[0:r, i, c0:c1]

            def tokens():
                pe.wait_ge(packed["p_tok"], 16)
                for t in range(TILES):
                    for c in range(IN_CH):
                        if t == 0:
                            pe.wait_ge(patches_in[c], 16)
                        pe.matmul(bank(t, TR, 0, D), patches[:, c, t * TR:(t + 1) * TR],
                                  v3("tokw", IN_CH)[:, c, :], start=(c == 0), stop=False)
                    pe.matmul(bank(t, TR, 0, D), V["ind"][:, t * TR:(t + 1) * TR], V["tokb"],
                              start=False, stop=True).then_inc(tok_psum, 1)

            def transpose_x(n, src):
                for t in range(TILES):
                    pe.wait_ge(ln_ready, TILES * n + t + 1)
                    need(pe, xT_ready, TILES * n + t - 1)
                    for c in range(CH):
                        last = pe.transpose(ps[0:KC, 6 + t % 2, c * TR:(c + 1) * TR],
                                            src[0:TR, t, c * KC:(c + 1) * KC], V["ident"][0:TR, 0:TR])
                    last.then_inc(xT_psum, 1)

            def attention(a, n):
                wqkv, wo = v3(f"wqkv{a}", CH), v3(f"wo{a}", CH)
                g0 = TILES * a
                h0 = 2 * TILES * a

                def project(t):
                    pe.wait_ge(xT_ready, TILES * n + t + 1)
                    need(pe, rope_used, g0 + t)
                    for c in range(CH):
                        k = KC + c
                        last = pe.matmul(bank(0, TR, 0, 2 * D), xT[0:k, c, t * TR:(t + 1) * TR],
                                         wqkv[0:k, c, 0:2 * D], start=(c == 0), stop=(c == 1))
                    last.then_inc(qk_psum, 1)
                    need(pe, v_ready, g0 + t)
                    need(pe, h_added, h0 + max(t - 2, 0))
                    for c in range(CH):
                        k = KC + c
                        last = pe.matmul(bank(1, TR, 0, D), xT[0:k, c, t * TR:(t + 1) * TR],
                                         wqkv[0:k, c, 2 * D:3 * D], start=(c == 0), stop=(c == 1))
                    last.then_inc(v_psum, 1)

                def transpose_qk(t):
                    pe.wait_ge(rope_ready, g0 + t + 1)
                    need(pe, o_ready, g0 + max(t - 1, 0))
                    need(pe, qkT_ready, g0 + t)
                    for c in range(2 * CH):
                        last = pe.transpose(ps[0:KC, 2, c * TR:(c + 1) * TR],
                                            qk[0:TR, t % 2, c * KC:(c + 1) * KC], V["ident"][0:TR, 0:TR])
                    last.then_inc(qkT_psum, 1)

                def scores(t):
                    pe.wait_ge(masks_in, 2)
                    pe.wait_ge(qkT_ready, g0 + t + 1)
                    pe.wait_ge(kmask_ready[0], g0 + t + 1)
                    pe.wait_ge(kmask_ready[1], g0 + t + 1)
                    need(pe, sub_ready, g0 + t)
                    for g in range(3):
                        for c in range(CH):
                            a0, a1 = max(4 * g, HPC * c), min(4 * g + 4, HPC * c + HPC)
                            if a0 < a1:
                                o = bank(3 + g, TR, (a0 - 4 * g) * TR, (a1 - 4 * g) * TR)
                                pe.matmul(o, maskA[:, :], maskB[:, 0:(a1 - a0) * TR], start=True, stop=False)
                                last = pe.matmul(o, qkT[0:KC, t % 2, c, :], kmask[0:KC, t % 2, a0:a1, :],
                                                 start=False, stop=True)
                    last.then_inc(s_psum, 1)

                def transpose_p(t):
                    pe.wait_ge(exp_ready, g0 + t + 1)
                    for g in range(3):
                        q = 3 * (g0 + t) + g
                        if q >= 2:
                            pe.wait_ge(pT_ready, q - 1)
                        for i in range(4):
                            last = pe.transpose(ps[0:TR, 6 + q % 2, i * TR:(i + 1) * TR],
                                                prob[0:TR, t % 2, 4 * g + i, :], V["ident"][0:TR, 0:TR])
                        last.then_inc(pT_psum, 1)

                def outputs(t):
                    pe.wait_ge(v_ready, g0 + t + 1)
                    pe.wait_ge(pT_ready, 3 * (g0 + t + 1))
                    pe.wait_ge(qkT_ready, g0 + min(t + 2, TILES))
                    for c in range(CH):
                        for i in range(HPC):
                            pe.matmul(ps[0:KC, 2, c * TR:(c + 1) * TR], vpad[0:TR, t % 2, HPC * c + i, :],
                                      probT[0:TR, t % 2, HPC * c + i, :], start=(i == 0), stop=(i == HPC - 1))
                    for c in range(CH):
                        for i in range(HPC):
                            last = pe.matmul(ps[0:KC, 2, (CH + c) * TR:(CH + c + 1) * TR],
                                             v3("onespad", HPC)[0:TR, i, :],
                                             probT[0:TR, t % 2, HPC * c + i, :], start=(i == 0), stop=(i == HPC - 1))
                    last.then_inc(o_psum, 1)

                def output_projection(t):
                    pe.wait_ge(o_ready, g0 + t + 1)
                    pe.wait_ge(v_ready, g0 + min(t + 3, TILES))
                    need(pe, h_added, h0 + t)
                    for c in range(CH):
                        k = KC + c
                        last = pe.matmul(bank(1, TR, 0, D), oT[0:k, c, :], wo[0:k, c, :],
                                         start=(c == 0), stop=(c == 1))
                    last.then_inc(proj_psum, 1)

                for s in range(TILES + 2):
                    if 0 <= s - 1 < TILES:
                        transpose_qk(s - 1)
                    if 0 <= s - 2 < TILES:
                        transpose_p(s - 2)
                    if s < TILES:
                        project(s)
                    if 0 <= s - 2 < TILES:
                        outputs(s - 2)
                    if 0 <= s - 1 < TILES:
                        scores(s - 1)
                    if 0 <= s - 2 < TILES:
                        output_projection(s - 2)

            def trilinear(n):
                def scores(t):
                    need(pe, tri_max, t - 1)
                    o = bank(3 + t % 2, TR, 0, TR)
                    pe.matmul(o, maskA[:, :], maskB[:, 0:TR], start=True, stop=False)
                    for c in range(CH):
                        pe.matmul(o, uT[0:KC, c, t * TR:(t + 1) * TR], xT[0:KC, c, t * TR:(t + 1) * TR],
                                  start=False, stop=False)
                    for c in range(CH):
                        last = pe.matmul(o, aT[0:KC, c, t * TR:(t + 1) * TR], V["ones"][0:KC, :],
                                         start=False, stop=(c == 1))
                    last.then_inc(tri_psum, 1)

                def transpose_p(t):
                    pe.wait_ge(tri_exp, t + 1)
                    need(pe, triT_ready, t - 1)
                    pe.transpose(ps[0:TR, 6 + t % 2, 0:TR], prob[0:TR, t % 2, 0, :],
                                 V["ident"][0:TR, 0:TR]).then_inc(triT_psum, 1)

                def outputs(t):
                    pe.wait_ge(triT_ready, t + 1)
                    need(pe, h_added, 2 * TILES - TILES + t - 1)
                    pe.matmul(bank(t % 2, TR, 0, D), probT[0:TR, t % 2, 0, :], xhat[0:TR, t, :],
                              start=True, stop=True).then_inc(trio_psum, 1)

                pe.wait_ge(packed["p_l1"], 16)
                pe.wait_ge(xT_ready, TILES * (n + 1))
                pe.wait_ge(tri_ready, 2 * CH)
                for s in range(TILES + 2):
                    if s < TILES:
                        scores(s)
                    if 0 <= s - 1 < TILES:
                        transpose_p(s - 1)
                    if 0 <= s - 2 < TILES:
                        outputs(s - 2)

            def convolution(n):
                pe.wait_ge(packed["p_l3"], 16)
                ptw = v3("ptw", CH)
                for t in range(TILES):
                    pe.wait_ge(xT_ready, TILES * n + t + 1)
                    pe.wait_ge(xT_ready, TILES * (n + 1))
                    need(pe, vt_ready, t - 1)
                    for c in range(CH):
                        k = KC + c
                        last = pe.matmul(bank(6 + t % 2, TR, 0, D), xT[0:k, c, t * TR:(t + 1) * TR],
                                         ptw[0:k, c, :], start=(c == 0), stop=(c == 1))
                    last.then_inc(vt_psum, 1)
                for c in range(CH):
                    pe.wait_ge(dw_ready, c + 1)
                    for f in range(2):
                        w = TPAD // 2 + f
                        a0 = f * (TPAD // 2)
                        pe.matmul(bank(2 * c + f, KC, 0, w), v3("pww", CH)[0:KC, c, :], dwc[0:KC, c, a0:a0 + w],
                                  start=True, stop=True).then_inc(pw_psum, 1)
                pe.wait_ge(ca_ready, 4)
                akw = v3("akw", CH)
                for t in range(TILES):
                    base = (t % 4) * TAPS * HEADS
                    o = ps[0:TR, 4 + t // 4, base:base + TAPS * HEADS].rearrange("p (k h) -> p k h", k=TAPS)
                    for c in range(CH):
                        last = pe.matmul(o[:, :, c * HPC:(c + 1) * HPC], ca[0:97, c, t * TR:(t + 1) * TR],
                                         akw[0:97, c, :], start=True, stop=True)
                last.then_inc(kern_psum, 1)
                sh = v3("shift", TAPS)
                for t in range(TILES):
                    pe.wait_ge(vt_ready, t + 1)
                    if t == 0:
                        pe.wait_ge(kern_sub, 1)
                    need(pe, shift_used, t)
                    for k in range(TAPS):
                        last = pe.matmul(bank(k // 2, TR, (k % 2) * D, (k % 2 + 1) * D), sh[0:TR, k, :],
                                         vtok[0:TR, t, :], start=True, stop=True)
                    last.then_inc(shift_psum, 1)

            def mixture(L, n):
                m = MOE[L]
                P, U, Bk, E = m["pairs"], m["units"], m["blocks"], m["routed"]
                gw = v3(f"gw{L}", CH)
                pe.wait_ge(packed[f"p_l{L}"], 16)
                pe.wait_ge(xT_ready, TILES * (n + 1))
                src = xT
                if L == 3:
                    wr1 = v3("wr1", CH)
                    for q in range(CH):
                        for f in range(2):
                            w = TPAD // 2 + f
                            a0 = f * (TPAD // 2)
                            for c in range(CH):
                                last = pe.matmul(bank(2 * q + f, KC, 0, w), wr1[0:KC, c, q * KC:(q + 1) * KC],
                                                 xT[0:KC, c, a0:a0 + w], start=(c == 0), stop=(c == 1))
                            last.then_inc(r_psum, 1)
                    pe.wait_ge(r_ready, 4)
                    src = rT
                for t in range(TILES):
                    for c in range(CH):
                        k = KC + c
                        last = pe.matmul(bank(7, TR, t * 16, t * 16 + E), src[0:k, c, t * TR:(t + 1) * TR],
                                         gw[0:k, c, :], start=(c == 0), stop=(c == 1))
                last.then_inc(gate_psum, 1)

                def hidden(e, b):
                    pe.wait_ge(w1_low, e * P + (m["q0"] + P))
                    for u in range(U):
                        j, f = u // 2, u % 2
                        if not (isinstance(e, int) and m["u0"] + e * U + u < 2):
                            pe.wait_ge(a_used, e * U + (m["u0"] + u - 1))
                            pe.wait_ge(b_used, e * U + (m["u0"] + u - 1))
                        for ab in range(2):
                            col = (2 * j + ab) * 128
                            for c in range(CH):
                                for q, (w, x) in enumerate(((W1h, xh), (W1h, xl), (W1l, xh))):
                                    last = pe.matmul(bank(2 * f + ab, 128, 0, HALF), w[0:KC, b, c, col:col + 128],
                                                     x[0:KC, c, f * HALF:(f + 1) * HALF],
                                                     start=(c == 0 and q == 0), stop=(c == 1 and q == 2))
                        last.then_inc(hid_psum, 1)

                def down(e, b, loads):
                    pe.wait_ge(w2_loaded[b], loads * 16)
                    if m["kind"] == "swiglu":
                        pe.wait_ge(act_ready, (e + 1) * U + m["s0"])
                    else:
                        pe.wait_ge(a_used, (e + 1) * U + m["u0"])
                        pe.wait_ge(b_used, (e + 1) * U + m["u0"])
                    for k in range(3):
                        if not (isinstance(e, int) and e == 0):
                            pe.wait_ge(y_added, (e - 1) * 3 + (m["y0"] + k + 1))
                        for t in range(2 * k, min(2 * k + 2, TILES)):
                            r = rows(t)
                            for q in range(Bk):
                                last = pe.matmul(bank(4 + k, r, (t % 2) * D, (t % 2 + 1) * D),
                                                 act[:, b, q, t * TR:t * TR + r], W2[:, b, q, :],
                                                 start=(q == 0), stop=(q == Bk - 1))
                        last.then_inc(y_psum, 1)

                pe.wait_ge(x_low, TILES * (L + 1))
                hidden(0, 1)
                hidden(1, 0)
                down(0, 1, m["w1"] + 1)
                hidden(2, 1)
                down(1, 0, m["w0"] + 1)
                with pe.Fori(1, m["loops"]) as i:
                    hidden(2 * i + 1, 0)
                    down(2 * i, 1, i + (m["w1"] + 1))
                    hidden(2 * i + 2, 1)
                    down(2 * i + 1, 0, i + (m["w0"] + 1))
                if m["tail"]:
                    hidden(m["n"] - 1, 0)
                    down(m["n"] - 2, 1, m["w1"] + m["n"] // 2)
                if m["bias"]:
                    G = 2 * m["n"] * 0 + m["n"]
                    at = sum(1 for x in MOE[:L] if x["bias"])
                    pe.wait_ge(cw_ready, L + 1)
                    for t in range(4):
                        last = pe.transpose(bank(7, G, t * TR, (t + 1) * TR), cw[0:TR, t, 0:G], V["ident"][0:TR, 0:TR])
                    last.then_inc(cwT_psum, 1)
                    pe.wait_ge(cwT_ready, 2 * at + 1)
                    pe.transpose(bank(7, G, 0, TR), cw[0:TR, 4, 0:G], V["ident"][0:TR, 0:TR]).then_inc(cwT_psum, 1)
                    pe.wait_ge(cwT_ready, 2 * at + 2)
                    pe.wait_ge(a_used, m["u0"] + m["n"] * U)
                    pe.wait_ge(b_used, m["u0"] + m["n"] * U)
                    for t in range(TILES):
                        last = pe.matmul(bank(t // 2, rows(t), (t % 2) * D, (t % 2 + 1) * D),
                                         cwT[0:G, t * TR:t * TR + rows(t)], V[f"b2_{L}"][0:G, :], start=True, stop=True)
                    last.then_inc(bias_psum, 1)
                e = m["n"] - 1
                down(e, (e + 1) % 2, m[f"w{(e + 1) % 2}"] + e // 2 + 1)

            tokens()
            pe.wait_ge(packed["p_l0"], 16)
            pe.wait_ge(filled, 5)
            transpose_x(0, xhat)
            attention(0, 0)
            transpose_x(1, xhat)
            mixture(0, 1)
            transpose_x(2, xhat)
            trilinear(2)
            transpose_x(3, xhat)
            mixture(1, 3)
            pe.wait_ge(packed["p_l2"], 16)
            transpose_x(4, xhat)
            attention(1, 4)
            transpose_x(5, xrms)
            mixture(2, 5)
            transpose_x(6, xhat)
            convolution(6)
            transpose_x(7, xhat)
            mixture(3, 7)

        @block.scalar
        def _(sc_):
            act_ = sc_.activation

            def take_x(n):
                for t in range(TILES):
                    sc_.wait_ge(xT_psum, TILES * n + t + 1)
                    src = ps[0:KC, 6 + t % 2, 0:CH * TR].rearrange("p (c r) -> p c r", c=CH)
                    if n % 2:
                        r = rows(t)
                        for c in range(CH):
                            scale = V["nscale"][0:KC, c:c + 1] if n == 5 else 1.0
                            hi = act_(xh[0:KC, c, t * TR:t * TR + r], src[:, c, 0:r], ACT.Copy, scale=scale)
                        hi.then_inc(x_high, 1)
                    if n == 5:
                        for c in range(CH):
                            last = act_(xT[0:KC, c, t * TR:(t + 1) * TR], src[:, c, :], ACT.Copy,
                                        scale=V["nscale"][0:KC, c:c + 1])
                    elif n == 6:
                        for c in range(CH):
                            act_(xpad[0:KC, c, t * PER_TILE:(t + 1) * PER_TILE, PAD:PAD + SEQ],
                                 src[:, c, :].rearrange("p (i s) -> p i s", i=PER_TILE), ACT.Copy).then_inc(pad_ready, 1)
                        last = act_(xT[0:KC, :, t * TR:(t + 1) * TR], src, ACT.Copy)
                    else:
                        last = act_(xT[0:KC, :, t * TR:(t + 1) * TR], src, ACT.Copy)
                    last.then_inc(xT_ready, 1)

            def attention(a):
                g0 = TILES * a

                def take_qk(t):
                    sc_.wait_ge(qkT_psum, g0 + t + 1)
                    need(sc_, s_psum, g0 + t - 1)
                    act_(qkT[0:KC, t % 2, :, :], ps[0:KC, 2, 0:2 * CH * TR].rearrange("p (c r) -> p c r", c=2 * CH),
                         ACT.Copy).then_inc(qkT_ready, 1)

                def take_p(t):
                    need(sc_, o_psum, g0 + t - 1)
                    for g in range(3):
                        q = 3 * (g0 + t) + g
                        sc_.wait_ge(pT_psum, q + 1)
                        act_(probT[0:TR, t % 2, 4 * g:4 * g + 4, :],
                             ps[0:TR, 6 + q % 2, 0:4 * TR].rearrange("p (c r) -> p c r", c=4),
                             ACT.Copy).then_inc(pT_ready, 1)

                def take_v(t):
                    sc_.wait_ge(v_psum, g0 + t + 1)
                    need(sc_, o_psum, g0 + t - 1)
                    flat = vpad[0:TR, t % 2, :, :].rearrange("p h c -> p (h c)")
                    for c in range(CH):
                        dst = flat[:, c * HPC * KC:(c + 1) * HPC * KC]
                        for i in range(HPC):
                            last = act_(vpad[0:TR, t % 2, HPC * c + i, i * HD:(i + 1) * HD],
                                        ps[0:TR, 1, (HPC * c + i) * HD:(HPC * c + i + 1) * HD], ACT.Copy)
                    last.then_inc(v_ready, 1)

                def exps(t):
                    sc_.wait_ge(sub_ready, g0 + t + 1)
                    act_(prob[0:TR, t % 2, :, :], prob[0:TR, t % 2, :, :], ACT.Exp, scale=HD ** -0.5).then_inc(exp_ready, 1)

                for s in range(TILES + 2):
                    if 0 <= s - 1 < TILES:
                        take_qk(s - 1)
                    if 0 <= s - 2 < TILES:
                        take_p(s - 2)
                    if s < TILES:
                        take_v(s)
                    if 0 <= s - 1 < TILES:
                        exps(s - 1)

            def trilinear():
                for s in range(TILES + 1):
                    if s < TILES:
                        sc_.wait_ge(tri_max, s + 1)
                        need(sc_, triT_psum, s - 1)
                        act_(prob[0:TR, s % 2, 0, :], ps[0:TR, 3 + s % 2, 0:TR], ACT.Exp,
                             bias=nmax[0:TR, s:s + 1], accum_out=psumr[0:TR, s:s + 1]).then_inc(tri_exp, 1)
                    if s >= 1:
                        t = s - 1
                        sc_.wait_ge(triT_psum, t + 1)
                        need(sc_, trio_psum, t - 1)
                        act_(probT[0:TR, t % 2, 0, :], ps[0:TR, 6 + t % 2, 0:TR], ACT.Copy).then_inc(triT_ready, 1)

            def convolution():
                for t in range(TILES):
                    sc_.wait_ge(vt_psum, t + 1)
                    act_(vtok[0:TR, t, :], ps[0:TR, 6 + t % 2, 0:D], ACT.Copy).then_inc(vt_ready, 1)
                sc_.wait_ge(kern_sub, 1)
                act_(kexp[0:TR, :, :], kexp[0:TR, :, :], ACT.Exp).then_inc(kern_exp, 1)

            def split(L, e, b, j, loads):
                m = MOE[L]
                cols = slice(j * 256, (j + 1) * 256)
                sc_.wait_ge(w1_loaded[b], loads * 16)
                if isinstance(e, int) and e < 2:
                    need(sc_, hid_psum, m["u0"])
                else:
                    sc_.wait_ge(hid_psum, (e - 2) * m["units"] + (m["u0"] + 2 * j + 2))
                act_(W1h[0:KC, b, :, cols], W1[0:KC, b, :, cols], ACT.Copy).then_inc(w1_high, 1)

            def mixture(L):
                m = MOE[L]
                P, U, E = m["pairs"], m["units"], m["routed"]
                if L == 3:
                    for q in range(CH):
                        for f in range(2):
                            w = TPAD // 2 + f
                            a0 = f * (TPAD // 2)
                            sc_.wait_ge(r_psum, 2 * q + f + 1)
                            act_(rT[0:KC, q, a0:a0 + w], ps[0:KC, 2 * q + f, 0:w], ACT.Relu,
                                 bias=V["br1"][0:KC, q:q + 1]).then_inc(r_ready, 1)
                sc_.wait_ge(gate_in, L + 1)
                act_(sc[0:TR, :, 0:E], sc[0:TR, :, 0:E] if L != 1 else lg[0:TR, :, 0:E],
                     ACT.Sigmoid if L == 1 else ACT.Exp).then_inc(gate_out, 1)

                def units(e, b, loads, ahead=True):
                    if m["bias"] and m["kind"] != "swiglu":
                        sc_.wait_ge(biases_loaded[b], (loads + m[f"b{b}"]) * 16)
                    for u in range(U):
                        j, f = u // 2, u % 2
                        U0 = m["u0"] + u
                        if m["kind"] == "silu":
                            sc_.wait_ge(hid_psum, e * U + (U0 + 1))
                            if not (isinstance(e, int) and U0 + e * U < 2):
                                sc_.wait_ge(b_used, e * U + (U0 - 1))
                            bias = biases[:, b, 2 * j:2 * j + 1] if m["bias"] else 0.0
                            act_(gate[:, f, :], ps[:, 2 * f, 0:HALF], ACT.Silu, bias=bias).then_inc(a_used, 1)
                        elif m["kind"] == "relu":
                            sc_.wait_ge(hid_psum, e * U + (U0 + 1))
                            act_(act[:, b, 2 * j, f * HALF:(f + 1) * HALF], ps[:, 2 * f, 0:HALF], ACT.Relu,
                                 bias=biases[:, b, 2 * j:2 * j + 1]).then_inc(a_used, 1)
                        else:
                            sc_.wait_ge(a_used, e * U + (U0 + 1))
                            if not (isinstance(e, int) and u + e * U < 2):
                                sc_.wait_ge(glu_ready, e * U + (u - 1))
                            act_(gsig[:, f, :], gate[:, f, :], ACT.Sigmoid, scale=1.702).then_inc(sig_ready, 1)
                        if f and ahead:
                            split(L, e + 2, b, j, loads + (m[f"w{b}"] + 1))

                units(0, 1, 1)
                with sc_.Fori(0, m["loops"] - 1) as i:
                    units(2 * i + 1, 0, i + 1)
                    units(2 * i + 2, 1, i + 2)
                i = m["loops"] - 1
                units(2 * i + 1, 0, i + 1, ahead=m["tail"])
                units(2 * i + 2, 1, i + 2, ahead=False)
                if m["tail"]:
                    units(m["n"] - 1, 0, m["n"] // 2, ahead=False)
                if m["bias"]:
                    G = m["n"]
                    at = sum(1 for x in MOE[:L] if x["bias"])
                    sc_.wait_ge(cwT_psum, 2 * at + 1)
                    act_(cwT[0:G, 0:4 * TR], ps[0:G, 7, 0:4 * TR], ACT.Copy).then_inc(cwT_ready, 1)
                    sc_.wait_ge(cwT_psum, 2 * at + 2)
                    act_(cwT[0:G, 4 * TR:5 * TR], ps[0:G, 7, 0:TR], ACT.Copy).then_inc(cwT_ready, 1)

            take_x(0)
            attention(0)
            for L, between in enumerate((lambda: (take_x(2), trilinear()), lambda: (take_x(4), attention(1)),
                                         lambda: (take_x(6), convolution()), lambda: None)):
                for e in range(2):
                    for j in range(MOE[L]["pairs"]):
                        split(L, e, 1 - e, j, MOE[L][f"w{1 - e}"] + 1)
                take_x(2 * L + 1)
                mixture(L)
                between()

        @block.gpsimd
        def _(pool):
            pool.memset(vpad[:, :, :, :], 0.0).then_inc(filled, 1)
            pool.memset(xpad[:, :, :, :], 0.0).then_inc(filled, 1)

            def attention(a):
                g0 = TILES * a
                for t in range(TILES):
                    pool.wait_ge(qkT_ready, g0 + t + 1)
                    pool.tensor_tensor(kmask[0:KC, t % 2, HPC:, :],
                                       qkT[0:KC, t % 2, CH + 1, :].unsqueeze(1).broadcast_to([KC, HPC, TR]),
                                       V["hmask"][0:KC, :].unsqueeze(2).broadcast_to([KC, HPC, TR]),
                                       ALU.mult).then_inc(kmask_ready[1], 1)

            def mixture(L):
                m = MOE[L]
                P, U = m["pairs"], m["units"]

                def split(e, b, j):
                    cols = slice(j * 256, (j + 1) * 256)
                    pool.wait_ge(w1_high, e * P + (m["q0"] + j + 1))
                    pool.tensor_tensor(W1l[0:KC, b, :, cols], W1[0:KC, b, :, cols],
                                       W1h[0:KC, b, :, cols].bitcast(F32), ALU.subtract).then_inc(w1_low, 1)

                def units(e, b, ahead=True):
                    for u in range(U):
                        j, f = u // 2, u % 2
                        if m["kind"] == "swiglu":
                            pool.wait_ge(sig_ready, e * U + (u + 1))
                            pool.tensor_tensor(gsig[:, f, :], gate[:, f, :], gsig[:, f, :],
                                               ALU.mult).then_inc(glu_ready, 1)
                        if f and ahead:
                            split(e + 2, b, j)

                for e in range(2):
                    for j in range(P):
                        split(e, 1 - e, j)
                units(0, 1)
                with pool.Fori(0, m["loops"] - 1) as i:
                    units(2 * i + 1, 0)
                    units(2 * i + 2, 1)
                i = m["loops"] - 1
                units(2 * i + 1, 0, ahead=m["tail"])
                units(2 * i + 2, 1, ahead=False)
                if m["tail"]:
                    units(m["n"] - 1, 0, ahead=False)

            pool.wait_ge(packed["p_l0"], 16)
            pool.tensor_copy(maskA[:, :], V["same_q"]).then_inc(masks_in, 1)
            pool.tensor_copy(maskB[:, :], V["same_k"]).then_inc(masks_in, 1)
            attention(0)
            mixture(0)
            mixture(1)
            attention(1)
            mixture(2)
            mixture(3)

        @block.vector
        def _(dve):
            steps = [0]

            def link(ins):
                steps[0] += 1
                ins.then_inc(vec, 1)
                dve.wait_ge(vec, steps[0])

            tt, ts, stt = dve.tensor_tensor, dve.tensor_scalar, dve.scalar_tensor_tensor

            def rsqrt(dst, x):
                y, a = nt[0:TR, 0, :], nt[0:TR, 1, :]
                link(ts(nti[0:TR, :], x.bitcast(I32), 1, None, ALU.logical_shift_right))
                link(ts(y.bitcast(I32), nti[0:TR, :], -1.0, 1597463007.0, ALU.mult, ALU.add))
                for k in range(3):
                    link(stt(out=a, in0=y, scalar=-0.5, in1=y, op0=ALU.mult, op1=ALU.mult))
                    link(tt(a, a, x, ALU.mult))
                    link(stt(out=dst if k == 2 else y, in0=a, scalar=1.5, in1=y, op0=ALU.add, op1=ALU.mult))

            def layernorm(n):
                for t in range(TILES):
                    last = dve.bn_stats(st[0:TR, t, :], h[0:TR, t, :])
                link(last)
                for t in range(TILES):
                    last = dve.bn_aggr(mv[0:TR, t, :], st[0:TR, t, :])
                link(last)
                x, rstd = nt[0:TR, 2, :], nt[0:TR, 3, :]
                link(ts(x, mv[0:TR, :, 1], EPS, None, ALU.add))
                rsqrt(rstd, x)
                for t in range(TILES):
                    ins = ts(xhat[0:TR, t, :], h[0:TR, t, :], mv[0:TR, t, 0:1], rstd[:, t:t + 1],
                             ALU.subtract, ALU.mult)
                    if n == 5:
                        last = ins
                    else:
                        ins.then_inc(ln_ready, 1)
                if n == 5:
                    link(last)
                    for t in range(TILES):
                        last = dve.tensor_tensor_reduce(xrms[0:TR, t, :], xhat[0:TR, t, :], xhat[0:TR, t, :],
                                                        1.0, 0.0, ALU.mult, ALU.add, s5[0:TR, 0, t:t + 1])
                    link(last)
                    link(ts(x, s5[0:TR, 0, :], 1.0 / D, EPS, ALU.mult, ALU.add))
                    rsqrt(rstd, x)
                    for t in range(TILES):
                        ts(xrms[0:TR, t, :], xhat[0:TR, t, :], rstd[:, t:t + 1], None, ALU.mult).then_inc(ln_ready, 1)
                    link(tt(h[0:TR, :, :], h[0:TR, :, :], xhat[0:TR, :, :], ALU.add))

            def attention(a):
                g0 = TILES * a
                cos = V[f"cos{a}"][0:TR, :].unsqueeze(1).broadcast_to([TR, 2 * HEADS, HD])
                sin = V[f"sin{a}"][0:TR, :]

                def rotate(t):
                    src = ps[0:TR, 0, 0:2 * D].rearrange("p (g d) -> p g d", d=HD)
                    r0 = rope[0:TR, 0, :].rearrange("p (g d) -> p g d", d=HD)
                    r1 = rope[0:TR, 1, :].rearrange("p (g d) -> p g d", d=HD)
                    dve.wait_ge(qk_psum, g0 + t + 1)
                    tt(r0, src, cos, ALU.mult)
                    for f in range(2):
                        w = HD // 2
                        last = tt(r1[:, :, f * w:(f + 1) * w], src[:, :, (1 - f) * w:(2 - f) * w],
                                  sin[:, f * w:(f + 1) * w].unsqueeze(1).broadcast_to([TR, 2 * HEADS, w]), ALU.mult)
                    last.then_inc(rope_used, 1)
                    dve.wait_ge(rope_used, g0 + t + 1)
                    need(dve, qkT_psum, g0 + t - 1)
                    tt(qk[0:TR, t % 2, :], rope[0:TR, 0, :], rope[0:TR, 1, :], ALU.add).then_inc(rope_ready, 1)
                    dve.wait_ge(rope_ready, g0 + t + 1)

                def mask_keys(t):
                    dve.wait_ge(qkT_ready, g0 + t + 1)
                    tt(kmask[0:KC, t % 2, 0:HPC, :],
                       qkT[0:KC, t % 2, CH, :].unsqueeze(1).broadcast_to([KC, HPC, TR]),
                       V["hmask"][0:KC, :].unsqueeze(2).broadcast_to([KC, HPC, TR]), ALU.mult).then_inc(kmask_ready[0], 1)

                def shift_scores(t):
                    dve.wait_ge(s_psum, g0 + t + 1)
                    s3 = ps[0:TR, 3:6, 0:4 * TR].rearrange("p b (i k) -> p b i k", i=4)
                    link(dve.tensor_reduce(smax[0:TR, :].rearrange("p (b i) -> p b i", b=3), s3, AX, ALU.max))
                    need(dve, pT_psum, 3 * (g0 + t - 1))
                    for g in range(3):
                        last = tt(prob[0:TR, t % 2, 4 * g:4 * g + 4, :], s3[:, g, :, :],
                                  smax[0:TR, 4 * g:4 * g + 4].unsqueeze(2).broadcast_to([TR, 4, TR]), ALU.subtract)
                    last.then_inc(sub_ready, 1)

                def normalise(t):
                    dve.wait_ge(o_psum, g0 + t + 1)
                    need(dve, proj_psum, g0 + t)
                    o4 = ps[0:KC, 2, 0:2 * CH * TR].rearrange("p (c r) -> p c r", c=2 * CH)
                    link(dve.reciprocal(rden[0:KC, :, :], o4[:, CH:, :]))
                    tt(oT[0:KC, :, :], o4[:, 0:CH, :], rden[0:KC, :, :], ALU.mult).then_inc(o_ready, 1)

                def add(t):
                    dve.wait_ge(proj_psum, g0 + t + 1)
                    tt(h[0:TR, t, :], ps[0:TR, 1, 0:D], h[0:TR, t, :], ALU.add).then_inc(h_added, 1)

                for s in range(TILES + 2):
                    if 0 <= s - 1 < TILES:
                        mask_keys(s - 1)
                    if s < TILES:
                        rotate(s)
                    if 0 <= s - 2 < TILES:
                        normalise(s - 2)
                    if 0 <= s - 1 < TILES:
                        shift_scores(s - 1)
                    if 0 <= s - 2 < TILES:
                        add(s - 2)
                dve.wait_ge(h_added, TILES * (1 if a == 0 else 3))

            def trilinear():
                dve.wait_ge(xT_ready, 3 * TILES)
                for c in range(CH):
                    ts(uT[0:KC, c, :], xT[0:KC, c, :], V["w3v"][0:KC, c:c + 1], V["w1v"][0:KC, c:c + 1],
                       ALU.mult, ALU.add).then_inc(tri_ready, 1)
                    ts(aT[0:KC, c, :], xT[0:KC, c, :], V["w2v"][0:KC, c:c + 1], None, ALU.mult).then_inc(tri_ready, 1)
                for s in range(TILES + 2):
                    if s < TILES:
                        dve.wait_ge(tri_psum, s + 1)
                        dve.tensor_reduce(nmax[0:TR, s:s + 1], ps[0:TR, 3 + s % 2, 0:TR], AX, ALU.max,
                                          negate=True).then_inc(tri_max, 1)
                    if s >= 2:
                        t = s - 2
                        dve.wait_ge(trio_psum, t + 1)
                        link(dve.reciprocal(rsum[0:TR, t:t + 1], psumr[0:TR, t:t + 1]))
                        stt(out=h[0:TR, t, :], in0=ps[0:TR, t % 2, 0:D], scalar=rsum[0:TR, t:t + 1],
                            in1=h[0:TR, t, :], op0=ALU.mult, op1=ALU.add).then_inc(h_added, 1)
                dve.wait_ge(h_added, 2 * TILES)

            def convolution():
                for c in range(CH):
                    dve.wait_ge(pad_ready, CH * TILES)
                    dst = dwc[0:KC, c, :].rearrange("p (i s) -> p i s", s=SEQ)
                    w = v3("dww", CH)[0:KC, c, :]
                    link(ts(dst, xpad[0:KC, c, :, 0:SEQ], w[:, 0:1], None, ALU.mult))
                    for k in range(1, TAPS):
                        ins = stt(out=dst, in0=xpad[0:KC, c, :, k:k + SEQ], scalar=w[:, k:k + 1], in1=dst,
                                  op0=ALU.mult, op1=ALU.add)
                        if k < TAPS - 1:
                            link(ins)
                    ins.then_inc(dw_ready, 1)
                for c in range(CH):
                    for f in range(2):
                        w = TPAD // 2 + f
                        a0 = f * (TPAD // 2)
                        dve.wait_ge(pw_psum, 2 * c + f + 1)
                        stt(out=ca[0:KC, c, a0:a0 + w], in0=ps[0:KC, 2 * c + f, 0:w], scalar=V["pwb"][0:KC, c:c + 1],
                            in1=xT[0:KC, c, a0:a0 + w], op0=ALU.add, op1=ALU.mult).then_inc(ca_ready, 1)
                N = TAPS * HEADS
                dve.wait_ge(kern_psum, 1)
                dve.tensor_copy(kern[0:TR, 0:4, :], ps[0:TR, 4, 0:4 * N].rearrange("p (t n) -> p t n", t=4))
                link(dve.tensor_copy(kern[0:TR, 4, :], ps[0:TR, 5, 0:N]))

                def by_tap(x):
                    return x[0:TR, :, :].rearrange("p t (k h) -> p t k h", k=TAPS)

                def over(x):
                    return x[0:TR, :, :].rearrange("p t (k h) -> p t h k", k=TAPS)

                def spread(x, t):
                    return x[0:TR, t, :].unsqueeze(1).broadcast_to([TR, TAPS, HEADS])

                for t in range(TILES):
                    last = dve.tensor_reduce(kmx[0:TR, t, :], over(kern)[:, t, :, :], AX, ALU.max)
                link(last)
                for t in range(TILES):
                    last = tt(by_tap(kexp)[:, t, :, :], by_tap(kern)[:, t, :, :], spread(kmx, t), ALU.subtract)
                last.then_inc(kern_sub, 1)
                dve.wait_ge(kern_exp, 1)
                for t in range(TILES):
                    last = dve.tensor_reduce(kmx[0:TR, t, :], over(kexp)[:, t, :, :], AX, ALU.add)
                link(last)
                link(dve.reciprocal(kmx[0:TR, :, :], kmx[0:TR, :, :]))
                for t in range(TILES):
                    last = tt(by_tap(kern)[:, t, :, :], by_tap(kexp)[:, t, :, :], spread(kmx, t), ALU.mult)
                link(last)
                for t in range(TILES):
                    dve.wait_ge(shift_psum, t + 1)
                    w = kern[0:TR, t, :].unsqueeze(2)
                    n8 = (TAPS - 1) * HEADS
                    for b in range(4):
                        tt(prod[0:TR, 2 * b:2 * b + 2, :].rearrange("p k (h d) -> p (k h) d", d=HD),
                           ps[0:TR, b, 0:2 * D].rearrange("p (h d) -> p h d", d=HD),
                           w[:, 2 * b * HEADS:(2 * b + 2) * HEADS, :].broadcast_to([TR, 2 * HEADS, HD]), ALU.mult)
                    tt(prod[0:TR, 8, :].rearrange("p (h d) -> p h d", d=HD),
                       ps[0:TR, 4, 0:D].rearrange("p (h d) -> p h d", d=HD),
                       w[:, n8:, :].broadcast_to([TR, HEADS, HD]), ALU.mult).then_inc(shift_used, 1)
                    dve.wait_ge(shift_used, t + 1)
                    link(dve.tensor_reduce(conv[0:TR, :], prod[0:TR, :, :].rearrange("p k d -> p d k"), AX, ALU.add))
                    link(tt(h[0:TR, t, :], h[0:TR, t, :], conv[0:TR, :], ALU.add))

            def choose(s, N, top, tri, dst):
                g, q = cmpg[0:TR, :, 0:N, 0:N], cmpe[0:TR, :, 0:N, 0:N]
                mine = s.unsqueeze(3).broadcast_to([TR, TILES, N, N])
                other = s.unsqueeze(2).broadcast_to([TR, TILES, N, N])
                order = V[tri][0:TR, :].rearrange("p (a b) -> p a b", a=N).unsqueeze(1).broadcast_to([TR, TILES, N, N])
                tt(g, other, mine, ALU.is_gt)
                link(tt(q, other, mine, ALU.is_equal))
                for t in range(TILES):
                    last = tt(q[:, t], q[:, t], order[:, t], ALU.mult)
                link(last)
                link(tt(g, g, q, ALU.add))
                link(dve.tensor_reduce(rank[0:TR, :, 0:N], g, AX, ALU.add))
                link(ts(dst, rank[0:TR, :, 0:N], float(top), None, ALU.is_lt))

            def wide(x, N):
                return x.unsqueeze(2).broadcast_to([TR, TILES, N])

            def gating(L):
                m = MOE[L]
                E = m["routed"]
                c0 = m["shared"]
                dve.wait_ge(gate_psum, L + 1)
                l, s, r, p = lg[0:TR, :, 0:E], sc[0:TR, :, 0:E], sr[0:TR, :, 0:E], pick[0:TR, :, 0:E]
                mx, sm = s5[0:TR, 0, :], s5[0:TR, 1, :]
                ins = dve.tensor_copy(l, ps[0:TR, 7, 0:16 * TILES].rearrange("p (t e) -> p t e", e=16)[:, :, 0:E])
                if L == 1:
                    ins.then_inc(gate_in, 1)
                else:
                    link(ins)
                    link(dve.tensor_reduce(mx, l, AX, ALU.max))
                    tt(s, l, wide(mx, E), ALU.subtract).then_inc(gate_in, 1)
                if L >= 2:
                    choose(l, E, m["top"], f"tri{E}", p)
                    dve.wait_ge(gate_out, L + 1)
                    link(tt(r, s, p, ALU.mult))
                    link(dve.tensor_reduce(sm, r, AX, ALU.add))
                    link(dve.reciprocal(sm, sm))
                    tt(cw[0:TR, :, 0:E], r, wide(sm, E), ALU.mult).then_inc(cw_ready, 1)
                    dve.wait_ge(cw_ready, L + 1)
                    return
                dve.wait_ge(gate_out, L + 1)
                if L == 0:
                    link(dve.tensor_reduce(sm, s, AX, ALU.add))
                    link(dve.reciprocal(sm, sm))
                    link(tt(s, s, wide(sm, E), ALU.mult))
                link(tt(r, s, V[f"gb{L}"][0:TR, :].unsqueeze(1).broadcast_to([TR, TILES, E]), ALU.add))
                G = m["groups"]
                gs, gp = gsum[0:TR, :, 0:G], gpick[0:TR, :, 0:G]
                link(tt(gs, r[:, :, 0::2], r[:, :, 1::2], ALU.add))
                choose(gs, G, m["top_groups"], f"tri{G}", gp)
                for f in range(2):
                    last = tt(r[:, :, f::2], r[:, :, f::2], gp, ALU.mult)
                link(last)
                link(ts(gs, gp, 1e30, -1e30, ALU.mult, ALU.add))
                for f in range(2):
                    last = tt(r[:, :, f::2], r[:, :, f::2], gs, ALU.add)
                link(last)
                choose(r, E, m["top"], f"tri{E}", p)
                out_ = cw[0:TR, :, c0:c0 + E]
                if L == 0:
                    stt(out=out_, in0=p, scalar=2.5, in1=s, op0=ALU.mult, op1=ALU.mult).then_inc(cw_ready, 1)
                else:
                    link(tt(r, s, p, ALU.mult))
                    link(dve.tensor_reduce(sm, r, AX, ALU.add))
                    link(ts(sm, sm, 1e-6, None, ALU.add))
                    link(dve.reciprocal(sm, sm))
                    tt(out_, r, wide(sm, E), ALU.mult).then_inc(cw_ready, 1)
                dve.wait_ge(cw_ready, L + 1)

            def mixture(L):
                m = MOE[L]
                P, U = m["pairs"], m["units"]
                if m["shared"]:
                    link(dve.memset(cw[:, :, 0:1], 1.0))
                for t in range(TILES):
                    dve.wait_ge(xT_ready, TILES * (2 * L + 1) + t + 1)
                    a0, a1 = t * TR, t * TR + rows(t)
                    tt(xl[0:KC, :, a0:a1], xT[0:KC, :, a0:a1], xh[0:KC, :, a0:a1].bitcast(F32),
                       ALU.subtract).then_inc(x_low, 1)

                def units(e, b, loads):
                    if m["bias"]:
                        dve.wait_ge(biases_loaded[b], (loads + m[f"b{b}"]) * 16)
                    if m["kind"] == "swiglu":
                        ts(lin_bias[:, b, :], biases[:, b, 1::2], 1.0, None, ALU.add).then_inc(lin_bias_ready, 1)
                        dve.wait_ge(lin_bias_ready, e + 1)

                    def last_factor(u):
                        j, f = u // 2, u % 2
                        dve.wait_ge(glu_ready, e * U + (u + 1))
                        stt(out=act[:, b, j, f * HALF:(f + 1) * HALF], in0=lin[:, f, :], scalar=-6.0,
                            in1=gsig[:, f, :], op0=ALU.max, op1=ALU.mult).then_inc(act_ready, 1)

                    for u in range(U):
                        j, f = u // 2, u % 2
                        U0 = m["u0"] + u
                        if m["kind"] == "silu":
                            dve.wait_ge(a_used, e * U + (U0 + 1))
                            bias = biases[:, b, 2 * j + 1:2 * j + 2] if m["bias"] else 0.0
                            stt(out=act[:, b, j, f * HALF:(f + 1) * HALF], in0=ps[:, 2 * f + 1, 0:HALF], scalar=bias,
                                in1=gate[:, f, :], op0=ALU.add, op1=ALU.mult).then_inc(b_used, 1)
                        elif m["kind"] == "relu":
                            dve.wait_ge(hid_psum, e * U + (U0 + 1))
                            ts(act[:, b, 2 * j + 1, f * HALF:(f + 1) * HALF], ps[:, 2 * f + 1, 0:HALF],
                               biases[:, b, 2 * j + 1:2 * j + 2], 0.0, ALU.add, ALU.max).then_inc(b_used, 1)
                        else:
                            if u >= 2:
                                dve.wait_ge(act_ready, e * U + (u - 1))
                            elif not (isinstance(e, int) and e == 0):
                                dve.wait_ge(act_ready, e * U + (u - 1))
                            dve.wait_ge(hid_psum, e * U + (U0 + 1))
                            ts(gate[:, f, :], ps[:, 2 * f, 0:HALF], biases[:, b, 2 * j:2 * j + 1], 7.0,
                               ALU.add, ALU.min).then_inc(a_used, 1)
                            ts(lin[:, f, :], ps[:, 2 * f + 1, 0:HALF], lin_bias[:, b, j:j + 1], 8.0,
                               ALU.add, ALU.min).then_inc(b_used, 1)
                            if u >= 1:
                                dve.wait_ge(b_used, e * U + U0)
                                last_factor(u - 1)
                    if m["kind"] == "swiglu":
                        dve.wait_ge(b_used, e * U + (m["u0"] + U))
                        last_factor(U - 1)

                def add(e, first=False):
                    for k in range(3):
                        dve.wait_ge(y_psum, e * 3 + (m["y0"] + k + 1))
                        if not first:
                            dve.wait_ge(y_added, e * 3 + (m["y0"] + k - 2))
                        for t in range(2 * k, min(2 * k + 2, TILES)):
                            r = rows(t)
                            last = stt(out=h[0:r, t, :], in0=ps[0:r, 4 + k, (t % 2) * D:(t % 2 + 1) * D],
                                       scalar=cw[0:r, t, bass.ds(e, 1)], in1=h[0:r, t, :], op0=ALU.mult, op1=ALU.add)
                        last.then_inc(y_added, 1)

                gating(L)
                units(0, 1, 1)
                units(1, 0, 1)
                add(0, True)
                units(2, 1, 2)
                add(1)
                with dve.Fori(1, m["loops"]) as i:
                    units(2 * i + 1, 0, i + 1)
                    add(2 * i)
                    units(2 * i + 2, 1, i + 2)
                    add(2 * i + 1)
                n = m["n"]
                if m["tail"]:
                    units(n - 1, 0, n // 2)
                    add(n - 2)
                if m["bias"]:
                    at = sum(1 for x in MOE[:L] if x["bias"])
                    dve.wait_ge(bias_psum, at + 1)
                    dve.wait_ge(y_added, m["y0"] + 3 * (n - 1))
                    for t in range(TILES):
                        r = rows(t)
                        last = tt(h[0:r, t, :], ps[0:r, t // 2, (t % 2) * D:(t % 2 + 1) * D], h[0:r, t, :], ALU.add)
                    link(last)
                add(n - 1)
                dve.wait_ge(y_added, m["y0"] + 3 * n)

            dve.memset(xT[96:97, :, :], 1.0).then_inc(filled, 1)
            dve.memset(oT[96:97, :, :], 1.0).then_inc(filled, 1)
            dve.memset(rT[96:97, :, :], 1.0).then_inc(filled, 1)
            link(dve.memset(ca[96:97, :, :], 1.0))
            for t in range(TILES):
                dve.wait_ge(tok_psum, t + 1)
                last = dve.tensor_copy(h[0:TR, t, :], ps[0:TR, t, 0:D])
            link(last)
            dve.wait_ge(packed["p_l0"], 16)
            layernorm(0)
            attention(0)
            layernorm(1)
            mixture(0)
            layernorm(2)
            dve.wait_ge(packed["p_l1"], 16)
            trilinear()
            layernorm(3)
            mixture(1)
            layernorm(4)
            dve.wait_ge(packed["p_l2"], 16)
            attention(1)
            layernorm(5)
            mixture(2)
            layernorm(6)
            dve.wait_ge(packed["p_l3"], 16)
            convolution()
            layernorm(7)
            mixture(3)
            dve.nop().then_inc(h_done, TILES)


def chunks(w, bias=None):
    n = w.shape[1]
    o = np.zeros((97, CH, n), w.dtype)
    o[0:KC] = w.reshape(CH, KC, n).transpose(1, 0, 2)
    if bias is not None:
        o[KC, CH - 1] = bias
    return o.reshape(97, CH * n)


def rope_table(inv):
    pos = (np.arange(128) % SEQ).astype(np.float32)
    ang = (pos[:, None] * inv[None, :].astype(np.float32)).astype(np.float32)
    cos, sin = np.cos(ang).astype(np.float32), np.sin(ang).astype(np.float32)
    return np.concatenate([cos, cos], 1), np.concatenate([-sin, sin], 1)


def layout(I):
    f = np.float32
    S = {}
    x = I["x"].reshape(IMAGES, 3, 4, 16, 4, 16).transpose(1, 3, 5, 0, 2, 4).reshape(768, IMAGES, PATCHES)
    pt = np.zeros((768, TILES * PER_TILE, SEQ), f)
    pt[:, :IMAGES, 1:] = x
    patches = np.ascontiguousarray(pt.reshape(IN_CH, 128, TPAD).transpose(1, 0, 2))
    w = I["L0_tok_W"].reshape(D, 16, 16, 3).transpose(3, 1, 2, 0).reshape(IN_CH, 128, D)
    S["tokw"] = w.transpose(1, 0, 2).reshape(128, IN_CH * D)
    ind = np.zeros((128, TILES * PER_TILE, SEQ), f)
    ind[0, :IMAGES, 1:] = 1
    ind[1, :IMAGES, 0] = 1
    S["ind"] = ind.reshape(128, TPAD)
    S["tokb"] = np.zeros((128, D), f)
    S["tokb"][0] = I["L0_tok_b"]
    S["tokb"][1] = I["cls_tok"].reshape(D)
    S["ident"] = np.eye(128, dtype=f)

    S["wqkv0"] = chunks(np.concatenate([I["L0_attn_wq"].T, I["L0_attn_wk"].T, I["L0_attn_wv"].T], 1),
                        np.concatenate([I["L0_attn_bq"], I["L0_attn_bk"], I["L0_attn_bv"]]))
    S["wo0"] = chunks(I["L0_attn_wo"].T, I["L0_attn_bo"])
    frac = 2.0 * np.arange(4, dtype=f) / HD
    inv0 = np.concatenate([1.0 / (f(10000.0) ** frac), np.zeros(4, f)]).astype(f)
    S["cos0"], S["sin0"] = rope_table(inv0)
    S["hmask"] = np.repeat(np.eye(HPC, dtype=f), HD, 0)
    S["onespad"] = np.broadcast_to(np.repeat(np.eye(HPC, dtype=f), HD, 1).reshape(1, HPC * KC), (TR, HPC * KC))
    S["gw0"] = chunks(I["L0_ffn_gate_w"], I["L0_ffn_gate_b"])
    S["gb0"] = np.broadcast_to(I["L0_ffn_bias"], (128, 16))
    for n in (16, 8, 4):
        S[f"tri{n}"] = np.broadcast_to(np.tril(np.ones((n, n), f), -1).reshape(1, n * n), (128, n * n))
    S["b2_0"] = np.concatenate([I["L0_ffn_sbd"][None], I["L0_ffn_bd"]])

    for i, name in enumerate(["w1v", "w2v", "w3v"]):
        S[name] = I["L1_attn_w"][0, i * D:(i + 1) * D].reshape(CH, KC).T
    S["ones"] = np.ones((KC, TR), f)
    S["gw1"] = chunks(I["L1_ffn_gate_weight"].T)
    S["gb1"] = np.broadcast_to(I["L1_ffn_gate_bias"], (128, 8))

    S["wqkv1"] = chunks(I["L2_attn_w_qkv"].T, I["L2_attn_b_qkv"])
    S["wo1"] = chunks(I["L2_attn_w_proj"].T, I["L2_attn_b_proj"])
    inv1 = (1.0 / f(10000.0) ** (np.arange(0, HD, 2, dtype=f) / HD)).astype(f)
    S["cos1"], S["sin1"] = rope_table(inv1)
    S["nscale"] = I["L2_ffn_norm_scale"].reshape(CH, KC).T
    S["gw2"] = chunks(I["L2_ffn_gate_w"].T, I["L2_ffn_gate_b"])
    S["b2_2"] = I["L2_ffn_mlp2_b"]

    S["dww"] = I["L3_attn_dw_w"].reshape(CH, KC, TAPS).transpose(1, 0, 2).reshape(KC, CH * TAPS)
    pw = np.zeros((KC, CH, KC), f)
    ak = np.zeros((97, CH, TAPS, HPC), f)
    for c in range(CH):
        for i in range(HPC):
            hh = c * HPC + i
            pw[i * HD:(i + 1) * HD, c, i * HD:(i + 1) * HD] = I["L3_attn_pw_w"][hh].T
            ak[i * HD:(i + 1) * HD, c, :, i] = I["L3_attn_ak_w"][hh].T
            ak[KC, c, :, i] = I["L3_attn_ak_b"].reshape(HEADS, TAPS)[hh]
    S["pww"] = pw.reshape(KC, CH * KC)
    S["akw"] = ak.reshape(97, CH * TAPS * HPC)
    S["pwb"] = I["L3_attn_pw_b"].reshape(CH, KC).T
    S["ptw"] = chunks(I["L3_attn_pt_w"].T, I["L3_attn_pt_b"])
    l = np.arange(TR)
    sh = np.stack([(l[:, None] == l[None, :] + k - PAD) & (l[:, None] // SEQ == l[None, :] // SEQ)
                   for k in range(TAPS)], 1)
    S["shift"] = sh.astype(f).reshape(TR, TAPS * TR)
    S["wr1"] = chunks(I["L3_ffn_Wr1"].T)[0:KC]
    S["br1"] = I["L3_ffn_br1"].reshape(CH, KC).T
    S["gw3"] = chunks(I["L3_ffn_Wr2"].T, I["L3_ffn_br2"])
    S["b2_3"] = I["L3_ffn_b2"]

    same = (l[None, :] // SEQ == np.arange(PER_TILE)[:, None]).astype(f)
    mA, mB = np.zeros((128, TR), f), np.zeros((128, TR), f)
    mA[0:PER_TILE], mA[PER_TILE] = same, 1
    mB[0:PER_TILE], mB[PER_TILE] = same * BIG, -BIG
    S["same_q"], S["same_k"] = mA, np.tile(mB, (1, 4))



    O = {"patches": patches}
    for p, items in PACKS.items():
        blob = np.zeros((128, sum(c for _, _, c in items)), f)
        at = 0
        for name, rows, cols in items:
            blob[0:rows, at:at + cols] = S[name]
            at += cols
        O[p] = blob

    def up(pairs):
        e, p = pairs.shape[:2]
        return np.ascontiguousarray(pairs.reshape(e, p * 256, CH, KC).transpose(0, 3, 2, 1))

    def down(w):
        return np.ascontiguousarray(w.reshape(w.shape[0], -1, 128, D).transpose(0, 2, 1, 3))

    def with_shared(s, w):
        return np.concatenate([s[None], w])

    a0 = with_shared(I["L0_ffn_sWu"], I["L0_ffn_Wu"]).transpose(0, 2, 1)
    g0 = with_shared(I["L0_ffn_sWg"], I["L0_ffn_Wg"]).transpose(0, 2, 1)
    O["W1_0"] = up(np.stack([a0, g0], 1)[:, None])
    O["W2_0"] = down(with_shared(I["L0_ffn_sWd"], I["L0_ffn_Wd"]))
    a1 = with_shared(I["L1_ffn_sw1"], I["L1_ffn_w1"])
    g1 = with_shared(I["L1_ffn_sw3"], I["L1_ffn_w3"])
    O["W1_1"] = up(np.stack([a1, g1], 1)[:, None])
    O["W2_1"] = down(with_shared(I["L1_ffn_sw2"], I["L1_ffn_w2"]).transpose(0, 2, 1))
    w = I["L2_ffn_mlp1_w"].reshape(16, 3, 128, 2, D).transpose(0, 1, 3, 2, 4)
    O["W1_2"] = up(w)
    O["W2_2"] = down(I["L2_ffn_mlp2_w"].transpose(0, 2, 1))
    O["W1_3"] = up(I["L3_ffn_W1"].reshape(8, 3, 2, 128, D))
    O["bias_0"] = np.ascontiguousarray(np.stack([with_shared(I["L0_ffn_sbu"], I["L0_ffn_bu"]),
                                                 with_shared(I["L0_ffn_sbg"], I["L0_ffn_bg"])], 2))
    b = I["L2_ffn_mlp1_b"].reshape(16, 3, 128, 2).transpose(0, 2, 1, 3)
    O["bias_2"] = np.ascontiguousarray(b.reshape(16, 128, 6))
    O["bias_3"] = np.ascontiguousarray(I["L3_ffn_b1"].reshape(8, 6, 128).transpose(0, 2, 1))
    O["W2_3"] = down(I["L3_ffn_W2"].transpose(0, 2, 1))
    return O


def kernel(**inputs):
    import concourse.bacc as bacc
    from concourse.bass_utils import run_bass_kernel_spmd

    arrays = layout({k: np.asarray(v) for k, v in inputs.items()})
    nc = bacc.Bacc("TRN2", target_bir_lowering=False, num_devices=1)
    A = {k: nc.dram_tensor(k + "_dram", a.shape, mybir.dt.from_np(a.dtype), kind="ExternalInput").ap()
         for k, a in arrays.items()}
    out = nc.dram_tensor("out_dram", (TOKENS, D), F32, kind="ExternalOutput").ap()
    vit_tower(nc, A, out)
    r = run_bass_kernel_spmd(nc, [{k + "_dram": a for k, a in arrays.items()}], core_ids=[0])
    return r.results[0]["out_dram"].reshape(IMAGES, SEQ, D)
```

```python
from contextlib import ExitStack

import numpy as np

import concourse.bass as bass
from concourse import mybir

F32 = mybir.dt.float32
F32R = mybir.dt.float32r
BF16 = mybir.dt.bfloat16
I32 = mybir.dt.int32
ALU = mybir.AluOpType
ACT = mybir.ActivationFunctionType
AX = mybir.AxisListType.X

IMAGES, PATCHES = 32, 16
SEQ = PATCHES + 1
TOKENS = IMAGES * SEQ
D = 192
KC = 96
CH = D // KC
PER_TILE = 7
TR = PER_TILE * SEQ
TILES = -(-IMAGES // PER_TILE)
TPAD = TILES * TR
LAST = TOKENS - (TILES - 1) * TR
HALF = TOKENS // 2
FIRST = -(-HALF // TR)
HEADS, HD = 12, 16
HPC = HEADS // CH
TAPS = 9
PAD = (TAPS - 1) // 2
LPAD = SEQ + TAPS - 1
TAP_BANKS = -(-TAPS // 2)
IN_CH = 768 // 128
EPS = 1e-5
BIG = 2.0 ** 60
GMAX = 17
NEVER, MARK = -3.0e38, 3.0e38

MOE = [
    dict(kind="silu", n=17, pairs=1, routed=16, top=4, groups=8, top_groups=4, shared=1, bias=True),
    dict(kind="silu", n=9, pairs=1, routed=8, top=2, groups=4, top_groups=2, shared=1, bias=False),
    dict(kind="swiglu", n=16, pairs=3, routed=16, top=4, groups=0, top_groups=0, shared=0, bias=True),
    dict(kind="relu", n=8, pairs=3, routed=8, top=2, groups=0, top_groups=0, shared=0, bias=True),
]
for _m in MOE:
    _m["units"] = 2 * _m["pairs"]
    _m["blocks"] = _m["pairs"] * (2 if _m["kind"] == "relu" else 1)
    _m["tail"] = _m["n"] % 2 == 0
    _m["loops"] = (_m["n"] - 1) // 2
MAXP, MAXB = 3, 6

PACKS = {
    "p_tok": [("ind", 128, TPAD), ("tokb", 128, D), ("ident", 128, 128)],
    "p_l0": [("wqkv0", 97, CH * 3 * D), ("wo0", 97, CH * D), ("cos0", 128, HD), ("sin0", 128, HD),
             ("same_q", 128, TR), ("same_k", 128, 4 * TR), ("hmask", KC, HPC), ("gw0", 97, CH * 16), ("gb0", 128, 16),
             ("b2_0", 17, D)],
    "p_l1": [("w1v", KC, CH), ("w2v", KC, CH), ("w3v", KC, CH), ("ones", KC, TR), ("gw1", 97, CH * 8), ("gb1", 128, 8)],
    "p_l2": [("wqkv1", 97, CH * 3 * D), ("wo1", 97, CH * D), ("cos1", 128, HD), ("sin1", 128, HD),
             ("nscale", KC, CH), ("gw2", 97, CH * 16), ("b2_2", 16, D)],
    "p_l3": [("dww", KC, CH * TAPS), ("pww", KC, CH * KC), ("pwb", KC, CH), ("akw", 97, CH * TAPS * HPC),
             ("ptw", 97, CH * D), ("shift", TR, TAPS * TR), ("wr1", KC, CH * D), ("br1", KC, CH),
             ("gw3", 97, CH * 8), ("b2_3", 8, D)],
}


def vit_tower(nc, A, out):
    with ExitStack() as ctx:
        def sb(name, shape, dt=F32):
            return ctx.enter_context(nc.sbuf_tensor(name, shape, dt))

        def sem(name):
            return ctx.enter_context(nc.semaphore(name))

        V = {}
        packs = {}
        for p, items in PACKS.items():
            packs[p] = sb(p, [128, sum(c for _, _, c in items)])
            at = 0
            for name, rows, cols in items:
                V[name] = packs[p][:, at:at + cols]
                at += cols

        def v3(name, a):
            return V[name].rearrange("p (a b) -> p a b", a=a)

        maskA = sb("maskA", [128, TR], BF16)
        maskB = sb("maskB", [128, 4 * TR], BF16)
        h = sb("h", [128, TILES, D])
        xhat = sb("xhat", [128, TILES, D])
        xrms = sb("xrms", [128, TILES, D])
        xT = sb("xT", [128, CH, TPAD])
        st = sb("st", [128, TILES, 6])
        mv = sb("mv", [128, TILES, 2])
        nt = sb("nt", [128, 4, TILES])
        nti = sb("nti", [128, TILES], I32)
        rope = sb("rope", [128, 2, 2 * D])
        qk = sb("qk", [128, 2, 2 * D])
        qkT = sb("qkT", [128, 2, 2 * CH, TR])
        hidden_or_scores = sb("hidden_or_scores", [128, 2 * MAXB * TOKENS])
        patches = hidden_or_scores[:, 0:IN_CH * (D + TPAD)].rearrange("p (c r) -> p c r", c=IN_CH)
        n = 2 * HEADS * TR
        kmask = hidden_or_scores[:, 0:n].rearrange("p (b h r) -> p b h r", b=2, h=HEADS)
        prob = hidden_or_scores[:, n:2 * n].rearrange("p (b h r) -> p b h r", b=2, h=HEADS)
        probT_or_prod = sb("probT_or_prod", [128, n])
        probT = probT_or_prod[:, :].rearrange("p (b h r) -> p b h r", b=2, h=HEADS)
        prod = probT_or_prod[:, 0:TAPS * D].rearrange("p (k d) -> p k d", k=TAPS)
        vpad_all = sb("vpad", [128, 2 * HEADS * KC + KC])
        vpad = vpad_all[:, 0:2 * HEADS * KC].rearrange("p (b h c) -> p b h c", b=2, h=HEADS)
        smax = sb("smax", [128, HEADS])
        nbias = sb("nbias", [128, 2, HEADS])
        rowsum = sb("rowsum", [128, 2, HEADS])
        oT = sb("oT", [128, CH, TR])
        uT = sb("uT", [128, CH, TPAD])
        aT = sb("aT", [128, CH, TPAD])
        nmax = sb("nmax", [128, TILES])
        psumr = sb("psumr", [128, TILES])
        rsum = sb("rsum", [128, TILES])
        xpad = sb("xpad", [128, CH, TILES * PER_TILE, LPAD])
        dwc = uT
        fold = sb("fold", [128, TAPS, KC])
        ca = sb("ca", [128, CH, TPAD])
        kern = sb("kern", [128, TILES, TAPS * HEADS])
        kexp = sb("kexp", [128, TILES, TAPS * HEADS])
        kmx = sb("kmx", [128, TILES, HEADS])
        vtok = sb("vtok", [128, TILES, D])
        conv = sb("conv", [128, D])
        W1 = sb("W1", [128, 2, CH, MAXP * 256])
        W1h = sb("W1h", [128, 2, CH, MAXP * 256], F32R)
        W1l = sb("W1l", [128, 2, CH, MAXP * 256], F32R)
        xh = sb("xh", [128, CH, TOKENS], F32R)
        xl = sb("xl", [128, CH, TOKENS], F32R)
        W2 = sb("W2", [128, 2, MAXB, D])
        act = hidden_or_scores[:, :].rearrange("p (b q r) -> p b q r", b=2, q=MAXB)
        gate = sb("gate", [128, 2, HALF])
        gsig = sb("gsig", [128, 2, HALF])
        lin = sb("lin", [128, 2, HALF])
        cw = sb("cw", [128, TILES, GMAX])
        lg = sb("lg", [128, TILES, 16])
        sc = sb("sc", [128, TILES, 16])
        sr = sb("sr", [128, TILES, 16])
        gsum = sb("gsum", [128, TILES, 8])
        pick = sb("pick", [128, TILES, 16])
        gpick = sb("gpick", [128, TILES, 8])
        chosen = sb("chosen", [128, TILES, 24])
        largest = sb("largest", [128, TILES, 8])
        s5 = sb("s5", [128, 2, TILES])
        biases = sb("biases", [128, 2, 2 * MAXP])
        lin_bias = sb("lin_bias", [128, 2, MAXP])
        rT = aT
        cwT = sb("cwT", [128, TPAD])

        ps = ctx.enter_context(nc.psum_tensor("ps", [128, 8, 512], F32))

        packed = {p: sem("loaded_" + p) for p in PACKS}
        patches_in = [sem(f"patches_in{c}") for c in range(IN_CH)]
        masks_in = sem("masks_in")
        vec = sem("vec_step")
        filled = sem("filled")
        tok_psum = sem("tok_psum")
        ln_ready = sem("ln_ready")
        xT_psum = sem("xT_psum")
        xT_ready = sem("xT_ready")
        qk_psum = sem("qk_psum")
        v_psum = sem("v_psum")
        rope_ready = sem("rope_ready")
        rope_used = sem("rope_used")
        qkT_psum = sem("qkT_psum")
        qkT_ready = sem("qkT_ready")
        kmask_ready = [sem("kmask0_ready"), sem("kmask1_ready")]
        v_ready = sem("v_ready")
        s_psum = sem("s_psum")
        smax_ready = sem("smax_ready")
        exp_ready = sem("exp_ready")
        rowsum_ready = sem("rowsum_ready")
        prob_ready = sem("prob_ready")
        pT_psum = sem("pT_psum")
        pT_ready = sem("pT_ready")
        o_psum = sem("o_psum")
        o_ready = sem("o_ready")
        proj_psum = sem("proj_psum")
        h_added = sem("h_added")
        tri_psum = sem("tri_psum")
        tri_max = sem("tri_max")
        tri_exp = sem("tri_exp")
        triT_psum = sem("triT_psum")
        triT_ready = sem("triT_ready")
        trio_psum = sem("trio_psum")
        pad_ready = sem("pad_ready")
        dw_ready = sem("dw_ready")
        folded = sem("folded")
        pw_psum = sem("pw_psum")
        ca_ready = sem("ca_ready")
        vt_psum = sem("vt_psum")
        vt_ready = sem("vt_ready")
        kern_psum = sem("kern_psum")
        kern_sub = sem("kern_sub")
        kern_exp = sem("kern_exp")
        shift_psum = sem("shift_psum")
        shift_used = sem("shift_used")
        r_psum = sem("r_psum")
        r_ready = sem("r_ready")
        gate_psum = sem("gate_psum")
        gate_in = sem("gate_in")
        gate_out = sem("gate_out")
        cw_ready = sem("cw_ready")
        cwT_psum = sem("cwT_psum")
        cwT_ready = sem("cwT_ready")
        bias_psum = sem("bias_psum")
        w1_loaded = [sem("w1_loaded0"), sem("w1_loaded1")]
        w1_high = sem("w1_high")
        w1_low = sem("w1_low")
        x_high = sem("x_high")
        x_low = sem("x_low")
        w2_loaded = [sem("w2_loaded0"), sem("w2_loaded1")]
        biases_loaded = [sem("biases_loaded0"), sem("biases_loaded1")]
        lin_bias_ready = sem("lin_bias_ready")
        hid_psum = sem("hid_psum")
        a_used = sem("a_used")
        b_used = sem("b_used")
        sig_ready = sem("sig_ready")
        glu_ready = sem("glu_ready")
        act_ready = sem("act_ready")
        y_psum = sem("y_psum")
        y_added = sem("y_added")
        h_done = sem("h_done")
        stored = sem("stored")

        for L, m in enumerate(MOE):
            prev = MOE[:L]
            m["u0"] = sum(p["n"] * p["units"] for p in prev)
            m["y0"] = sum(p["n"] * 3 for p in prev)
            m["q0"] = sum(p["n"] * p["pairs"] for p in prev)
            m["s0"] = sum(p["n"] * p["units"] for p in prev if p["kind"] == "swiglu")
            for b in range(2):
                m[f"w{b}"] = sum((p["n"] + b) // 2 for p in prev)
                m[f"b{b}"] = sum((p["n"] + b) // 2 for p in prev if p["bias"])

        def x_bank(n, t):
            return (7, 2, 6, 7, 6)[t] if n in (2, 4, 6) else 6 + t % 2

        def image_half(f):
            mid = TILES * PER_TILE // 2 * SEQ
            return (0, mid) if f == 0 else (mid, TPAD)

        def rows(t):
            return TR if t < TILES - 1 else LAST

        def need(eng, s, n):
            if n > 0:
                eng.wait_ge(s, n)

        block = ctx.enter_context(nc.Block())

        @block.sync
        def _(sp):
            for c in range(IN_CH):
                sp.dma_start(patches[:, c, :], A["patches"][:, c, :]).then_inc(patches_in[c], 16)
            sp.dma_start(packs["p_tok"][:, :], A["p_tok"][:, :]).then_inc(packed["p_tok"], 16)
            sp.dma_start(packs["p_l0"][:, :], A["p_l0"][:, :]).then_inc(packed["p_l0"], 16)

            def load_first(L, e, b):
                m = MOE[L]
                P = m["pairs"]
                if isinstance(e, int) and e < 2:
                    need(sp, w1_low, m["q0"])
                else:
                    sp.wait_ge(w1_low, (e - 1) * P + m["q0"])
                sp.dma_start(W1[0:KC, b, :, 0:P * 256], A[f"W1_{L}"][e, :, :, :]).then_inc(w1_loaded[b], 16)

            def load_rest(L, e, b):
                m = MOE[L]
                early = isinstance(e, int) and e < 2
                if m["bias"]:
                    for used in (a_used, b_used):
                        if early:
                            need(sp, used, m["u0"])
                        else:
                            sp.wait_ge(used, (e - 1) * m["units"] + m["u0"])
                    sp.dma_start(biases[:, b, 0:2 * m["pairs"]], A[f"bias_{L}"][e, :, :]).then_inc(biases_loaded[b], 16)
                if early:
                    need(sp, y_psum, m["y0"])
                else:
                    sp.wait_ge(y_psum, (e - 1) * 3 + m["y0"])
                sp.dma_start(W2[:, b, 0:m["blocks"], :], A[f"W2_{L}"][e, :, :, :]).then_inc(w2_loaded[b], 16)

            for L, m in enumerate(MOE):
                load_first(L, 0, 1)
                load_first(L, 1, 0)
                load_rest(L, 0, 1)
                load_rest(L, 1, 0)
                if L < 3:
                    p = f"p_l{L + 1}"
                    sp.dma_start(packs[p][:, :], A[p][:, :]).then_inc(packed[p], 16)
                load_first(L, 2, 1)
                load_first(L, 3, 0)
                load_rest(L, 2, 1)
                with sp.Fori(1, m["loops"] - 1) as i:
                    load_first(L, 2 * i + 2, 1)
                    load_rest(L, 2 * i + 1, 0)
                    load_first(L, 2 * i + 3, 0)
                    load_rest(L, 2 * i + 2, 1)
                n = m["n"]
                i = m["loops"] - 1
                load_first(L, 2 * i + 2, 1)
                load_rest(L, 2 * i + 1, 0)
                if m["tail"]:
                    load_first(L, 2 * i + 3, 0)
                load_rest(L, 2 * i + 2, 1)
                if m["tail"]:
                    load_rest(L, n - 1, 0)
            for t in range(TILES):
                sp.wait_ge(h_done, t + 1)
                sp.dma_start(out[t * TR:t * TR + rows(t), :], h[0:rows(t), t, :]).then_inc(stored, 16)
            sp.wait_ge(stored, 16 * TILES)

        @block.tensor
        def _(pe):
            def bank(i, r=TR, c0=0, c1=512):
                return ps[0:r, i, c0:c1]

            def tokens():
                for c in range(IN_CH):
                    pe.wait_ge(patches_in[c], 16)
                    for t in range(TILES):
                        pe.matmul(bank(t, TR, 0, D), patches[:, c, D + t * TR:D + (t + 1) * TR],
                                  patches[:, c, 0:D], start=(c == 0), stop=False)
                pe.wait_ge(packed["p_tok"], 16)
                for t in range(TILES):
                    pe.matmul(bank(t, TR, 0, D), V["ind"][:, t * TR:(t + 1) * TR], V["tokb"],
                              start=False, stop=True).then_inc(tok_psum, 1)

            def xhat_of(n):
                return xrms if n == 5 else xhat

            def transpose_x(n, t0, t1):
                for t in range(t0, t1):
                    pe.wait_ge(ln_ready, TILES * n + t + 1)
                    before = [p for p in range(t) if x_bank(n, p) == x_bank(n, t)]
                    if before:
                        pe.wait_ge(xT_ready, TILES * n + before[-1] + 1)
                    transpose_tile(n, t, x_bank(n, t))

            def transpose_tile(n, t, b):
                for c in range(CH):
                    last = pe.transpose(ps[0:KC, b, c * TR:(c + 1) * TR],
                                        xhat_of(n)[0:TR, t, c * KC:(c + 1) * KC], V["ident"][0:TR, 0:TR])
                last.then_inc(xT_psum, 1)

            def attention(a, n):
                wqkv, wo = v3(f"wqkv{a}", CH), v3(f"wo{a}", CH)
                g0 = TILES * a
                h0 = 2 * TILES * a

                def project_qk(t):
                    pe.wait_ge(xT_ready, TILES * n + t + 1)
                    need(pe, rope_used, g0 + t)
                    for c in range(CH):
                        k = KC + c
                        last = pe.matmul(bank(0, TR, 0, 2 * D), xT[0:k, c, t * TR:(t + 1) * TR],
                                         wqkv[0:k, c, 0:2 * D], start=(c == 0), stop=(c == 1))
                    last.then_inc(qk_psum, 1)

                def project_v(t):
                    need(pe, o_ready, g0 + t - 1)
                    for c in range(CH):
                        k = KC + c
                        last = pe.matmul(bank(1, TR, 0, D), xT[0:k, c, t * TR:(t + 1) * TR],
                                         wqkv[0:k, c, 2 * D:3 * D], start=(c == 0), stop=(c == 1))
                    last.then_inc(v_psum, 1)

                def transpose_qk(t):
                    pe.wait_ge(rope_ready, g0 + t + 1)
                    need(pe, h_added, h0 + max(t - 2, 0))
                    need(pe, qkT_ready, g0 + t)
                    for c in range(2 * CH):
                        last = pe.transpose(ps[0:KC, 2, c * TR:(c + 1) * TR],
                                            qk[0:TR, t % 2, c * KC:(c + 1) * KC], V["ident"][0:TR, 0:TR])
                    last.then_inc(qkT_psum, 1)

                def scores(t):
                    pe.wait_ge(masks_in, 2)
                    pe.wait_ge(qkT_ready, g0 + t + 1)
                    pe.wait_ge(kmask_ready[0], g0 + t + 1)
                    pe.wait_ge(kmask_ready[1], g0 + t + 1)
                    for g in range(3):
                        need(pe, exp_ready, 3 * (g0 + t - 1) + g + 1)
                        for c in range(CH):
                            a0, a1 = max(4 * g, HPC * c), min(4 * g + 4, HPC * c + HPC)
                            if a0 < a1:
                                o = bank(3 + g, TR, (a0 - 4 * g) * TR, (a1 - 4 * g) * TR)
                                pe.matmul(o, maskA[:, :], maskB[:, 0:(a1 - a0) * TR], start=True, stop=False)
                                last = pe.matmul(o, qkT[0:KC, t % 2, c, :], kmask[0:KC, t % 2, a0:a1, :],
                                                 start=False, stop=True)
                    last.then_inc(s_psum, 1)

                def transpose_p(t):
                    pe.wait_ge(prob_ready, g0 + t + 1)
                    for g in range(3):
                        if g == 1:
                            pe.wait_ge(xT_ready, TILES * (n + 1) + max(t - 1, 0))
                        if g == 0:
                            pe.wait_ge(xT_ready, TILES * (n + 1))
                        need(pe, pT_ready, 3 * (g0 + t) + (0, 0, 1)[g])
                        for i in range(4):
                            last = pe.transpose(ps[0:TR, 6 + g % 2, i * TR:(i + 1) * TR],
                                                prob[0:TR, t % 2, 4 * g + i, :], V["ident"][0:TR, 0:TR])
                        last.then_inc(pT_psum, 1)

                def outputs(t):
                    pe.wait_ge(pT_ready, 3 * (g0 + t + 1))
                    pe.wait_ge(v_ready, g0 + min(t + 2, TILES))
                    for c in range(CH):
                        for i in range(HPC):
                            last = pe.matmul(ps[0:KC, 1, c * TR:(c + 1) * TR], vpad[0:TR, t % 2, HPC * c + i, :],
                                             probT[0:TR, t % 2, HPC * c + i, :], start=(i == 0), stop=(i == HPC - 1))
                    last.then_inc(o_psum, 1)

                def output_projection(t):
                    pe.wait_ge(o_ready, g0 + t + 1)
                    pe.wait_ge(qkT_ready, g0 + min(t + 3, TILES))
                    need(pe, h_added, h0 + t)
                    for c in range(CH):
                        k = KC + c
                        last = pe.matmul(bank(2, TR, 0, D), oT[0:k, c, :], wo[0:k, c, :],
                                         start=(c == 0), stop=(c == 1))
                    last.then_inc(proj_psum, 1)

                def transpose_result(t):
                    pe.wait_ge(ln_ready, TILES * (n + 1) + t + 1)
                    pe.wait_ge(xT_ready, TILES * (n + 1) + t)
                    pe.wait_ge(pT_ready, 3 * (g0 + min(t + 2, TILES)))
                    transpose_tile(n + 1, t, 7)

                transpose_x(n, 0, 2)
                project_qk(0)
                pe.wait_ge(xT_ready, TILES * n + 2)
                transpose_qk(0)
                transpose_x(n, 2, TILES)
                for s in range(TILES + 3):
                    if s < TILES:
                        scores(s)
                    if s >= 3:
                        transpose_result(s - 3)
                    if 0 <= s - 2 < TILES:
                        output_projection(s - 2)
                    if s + 1 < TILES:
                        project_qk(s + 1)
                    if s < TILES:
                        project_v(s)
                    if 0 <= s - 1 < TILES:
                        transpose_p(s - 1)
                    if s + 1 < TILES:
                        transpose_qk(s + 1)
                    if 0 <= s - 1 < TILES:
                        outputs(s - 1)

            def trilinear(n):
                def scores(t):
                    pe.wait_ge(xT_ready, TILES * n + t + 1)
                    need(pe, tri_exp, t - 1)
                    o = bank(3 + t % 2, TR, 0, TR)
                    pe.matmul(o, maskA[:, :], maskB[:, 0:TR], start=True, stop=False)
                    for c in range(CH):
                        pe.matmul(o, uT[0:KC, c, t * TR:(t + 1) * TR], xT[0:KC, c, t * TR:(t + 1) * TR],
                                  start=False, stop=False)
                    for c in range(CH):
                        last = pe.matmul(o, aT[0:KC, c, t * TR:(t + 1) * TR], V["ones"][0:KC, :],
                                         start=False, stop=(c == 1))
                    last.then_inc(tri_psum, 1)

                def transpose_p(t):
                    pe.wait_ge(tri_exp, t + 1)
                    need(pe, triT_ready, t - 1)
                    pe.transpose(ps[0:TR, (5, 2)[t % 2], 0:TR], prob[0:TR, t % 2, 0, :],
                                 V["ident"][0:TR, 0:TR]).then_inc(triT_psum, 1)

                def outputs(t):
                    pe.wait_ge(triT_ready, t + 1)
                    need(pe, h_added, TILES + t - 1)
                    pe.matmul(bank(t % 2, TR, 0, D), probT[0:TR, t % 2, 0, :], xhat[0:TR, t, :],
                              start=True, stop=True).then_inc(trio_psum, 1)

                transpose_x(n, 0, 2)
                pe.wait_ge(packed["p_l1"], 16)
                scores(0)
                scores(1)
                transpose_x(n, 2, TILES)
                transpose_p(0)
                scores(2)
                for t in range(1, TILES):
                    transpose_p(t)
                    outputs(t - 1)
                    if t + 2 < TILES:
                        scores(t + 2)
                outputs(TILES - 1)

            def convolution(n):
                pe.wait_ge(packed["p_l3"], 16)
                ptw = v3("ptw", CH)
                transpose_x(n, 0, TILES)
                pe.wait_ge(pad_ready, CH * TILES)
                pe.wait_ge(folded, 1)
                for f in range(2):
                    a0, a1 = image_half(f)
                    for k in range(TAPS):
                        last = pe.matmul(bank(2 + f, KC, 0, a1 - a0), fold[0:KC, k, :],
                                         xpad[0:KC, 1, a0 // SEQ:a1 // SEQ, k:k + SEQ],
                                         start=(k == 0), stop=(k == TAPS - 1))
                    last.then_inc(pw_psum, 1)
                for t in range(TILES):
                    pe.wait_ge(xT_ready, TILES * (n + 1))
                    need(pe, vt_ready, t - 1)
                    for c in range(CH):
                        k = KC + c
                        last = pe.matmul(bank(6 + t % 2, TR, 0, D), xT[0:k, c, t * TR:(t + 1) * TR],
                                         ptw[0:k, c, :], start=(c == 0), stop=(c == 1))
                    last.then_inc(vt_psum, 1)
                pe.wait_ge(dw_ready, 1)
                for f in range(2):
                    a0, a1 = image_half(f)
                    pe.matmul(bank(f, KC, 0, a1 - a0), v3("pww", CH)[0:KC, 0, :], dwc[0:KC, 0, a0:a1],
                              start=True, stop=True).then_inc(pw_psum, 1)
                pe.wait_ge(ca_ready, 4)
                akw = v3("akw", CH)
                for t in range(TILES):
                    base = (t % 4) * TAPS * HEADS
                    o = ps[0:TR, 4 + t // 4, base:base + TAPS * HEADS].rearrange("p (k h) -> p k h", k=TAPS)
                    for c in range(CH):
                        last = pe.matmul(o[:, :, c * HPC:(c + 1) * HPC], ca[0:97, c, t * TR:(t + 1) * TR],
                                         akw[0:97, c, :], start=True, stop=True)
                last.then_inc(kern_psum, 1)
                sh = v3("shift", TAPS)
                for t in range(TILES):
                    pe.wait_ge(vt_ready, t + 1)
                    if t == 0:
                        pe.wait_ge(kern_sub, 1)
                    for b in range(TAP_BANKS):
                        need(pe, shift_used, TAP_BANKS * (t - 1) + b + 1)
                        for k in range(2 * b, min(2 * b + 2, TAPS)):
                            last = pe.matmul(bank(b, TR, (k % 2) * D, (k % 2 + 1) * D), sh[0:TR, k, :],
                                             vtok[0:TR, t, :], start=True, stop=True)
                        last.then_inc(shift_psum, 1)

            def mixture(L, n):
                m = MOE[L]
                P, U, Bk, E = m["pairs"], m["units"], m["blocks"], m["routed"]
                gw = v3(f"gw{L}", CH)
                pe.wait_ge(packed[f"p_l{L}"], 16)
                def gate_logits():
                    src = xT
                    pe.wait_ge(xT_ready, TILES * (n + 1))
                    if L == 3:
                        wr1 = v3("wr1", CH)
                        for q in range(CH):
                            for f in range(2):
                                w = TPAD // 2 + f
                                a0 = f * (TPAD // 2)
                                for c in range(CH):
                                    last = pe.matmul(bank(2 + 2 * q + f, KC, 0, w), wr1[0:KC, c, q * KC:(q + 1) * KC],
                                                     xT[0:KC, c, a0:a0 + w], start=(c == 0), stop=(c == 1))
                                last.then_inc(r_psum, 1)
                        pe.wait_ge(r_ready, 4)
                        src = rT
                    for t in range(TILES):
                        for c in range(CH):
                            k = KC + c
                            last = pe.matmul(bank(7, TR, t * 16, t * 16 + E), src[0:k, c, t * TR:(t + 1) * TR],
                                             gw[0:k, c, :], start=(c == 0), stop=(c == 1))
                    last.then_inc(gate_psum, 1)

                def hidden(e, b):
                    pe.wait_ge(w1_low, e * P + (m["q0"] + P))
                    for u in range(U):
                        j, f = u // 2, u % 2
                        first = isinstance(e, int) and e == 0
                        if first and u < 2:
                            pe.wait_ge(x_low, TILES * L + (FIRST, TILES)[f])
                        if not (isinstance(e, int) and m["u0"] + e * U + u < 2):
                            pe.wait_ge(a_used, e * U + (m["u0"] + u - 1))
                            pe.wait_ge(b_used, e * U + (m["u0"] + u - 1))
                        for ab in range(2):
                            col = (2 * j + ab) * 128
                            for c in range(CH):
                                for q, (w, x) in enumerate(((W1h, xh), (W1h, xl), (W1l, xh))):
                                    last = pe.matmul(bank(2 * f + ab, 128, 0, HALF), w[0:KC, b, c, col:col + 128],
                                                     x[0:KC, c, f * HALF:(f + 1) * HALF],
                                                     start=(c == 0 and q == 0), stop=(c == 1 and q == 2))
                        last.then_inc(hid_psum, 1)
                        if first and u == 0:
                            if L in (1, 3):
                                transpose_x(n, FIRST, TILES)
                            gate_logits()

                def down(e, b, loads):
                    pe.wait_ge(w2_loaded[b], loads * 16)
                    if m["kind"] == "swiglu":
                        pe.wait_ge(act_ready, (e + 1) * U + m["s0"])
                    else:
                        pe.wait_ge(a_used, (e + 1) * U + m["u0"])
                        pe.wait_ge(b_used, (e + 1) * U + m["u0"])
                    for k in range(3):
                        if not (isinstance(e, int) and e == 0):
                            pe.wait_ge(y_added, (e - 1) * 3 + (m["y0"] + k + 1))
                        for t in range(2 * k, min(2 * k + 2, TILES)):
                            r = rows(t)
                            for q in range(Bk):
                                last = pe.matmul(bank(4 + k, r, (t % 2) * D, (t % 2 + 1) * D),
                                                 act[:, b, q, t * TR:t * TR + r], W2[:, b, q, :],
                                                 start=(q == 0), stop=(q == Bk - 1))
                        last.then_inc(y_psum, 1)

                hidden(0, 1)
                hidden(1, 0)
                down(0, 1, m["w1"] + 1)
                hidden(2, 1)
                down(1, 0, m["w0"] + 1)
                with pe.Fori(1, m["loops"]) as i:
                    hidden(2 * i + 1, 0)
                    down(2 * i, 1, i + (m["w1"] + 1))
                    hidden(2 * i + 2, 1)
                    down(2 * i + 1, 0, i + (m["w0"] + 1))
                if m["tail"]:
                    hidden(m["n"] - 1, 0)
                    down(m["n"] - 2, 1, m["w1"] + m["n"] // 2)
                if m["bias"]:
                    G = m["n"]
                    at = sum(1 for x in MOE[:L] if x["bias"])
                    pe.wait_ge(cw_ready, L + 1)
                    for t in range(4):
                        last = pe.transpose(bank(7, G, t * TR, (t + 1) * TR), cw[0:TR, t, 0:G], V["ident"][0:TR, 0:TR])
                    last.then_inc(cwT_psum, 1)
                    pe.wait_ge(cwT_ready, 2 * at + 1)
                    pe.transpose(bank(7, G, 0, TR), cw[0:TR, 4, 0:G], V["ident"][0:TR, 0:TR]).then_inc(cwT_psum, 1)
                    pe.wait_ge(cwT_ready, 2 * at + 2)
                    pe.wait_ge(a_used, m["u0"] + m["n"] * U)
                    pe.wait_ge(b_used, m["u0"] + m["n"] * U)
                    for t in range(TILES):
                        last = pe.matmul(bank(t // 2, rows(t), (t % 2) * D, (t % 2 + 1) * D),
                                         cwT[0:G, t * TR:t * TR + rows(t)], V[f"b2_{L}"][0:G, :], start=True, stop=True)
                    last.then_inc(bias_psum, 1)
                e = m["n"] - 1
                down(e, (e + 1) % 2, m[f"w{(e + 1) % 2}"] + e // 2 + 1)

            tokens()
            pe.wait_ge(packed["p_l0"], 16)
            pe.wait_ge(filled, 5)
            attention(0, 0)
            mixture(0, 1)
            trilinear(2)
            transpose_x(3, 0, FIRST)
            mixture(1, 3)
            pe.wait_ge(packed["p_l2"], 16)
            attention(1, 4)
            mixture(2, 5)
            convolution(6)
            transpose_x(7, 0, FIRST)
            pe.wait_ge(shift_used, TAP_BANKS * TILES)
            mixture(3, 7)

        @block.scalar
        def _(sc_):
            act_ = sc_.activation

            def take_tile(n, t, b):
                sc_.wait_ge(xT_psum, TILES * n + t + 1)
                src = ps[0:KC, b, 0:CH * TR].rearrange("p (c r) -> p c r", c=CH)
                r = rows(t)
                a0 = t * TR
                if n == 5:
                    for c in range(CH):
                        scale = V["nscale"][0:KC, c:c + 1]
                        act_(xh[0:KC, c, a0:a0 + r], src[:, c, 0:r], ACT.Copy, scale=scale)
                        last = act_(xT[0:KC, c, a0:a0 + TR], src[:, c, :], ACT.Copy, scale=scale)
                else:
                    if n % 2:
                        act_(xh[0:KC, :, a0:a0 + r], src[:, :, 0:r], ACT.Copy)
                    if n == 2:
                        for c in range(CH):
                            act_(uT[0:KC, c, a0:a0 + TR], src[:, c, :], ACT.Identity,
                                 scale=V["w3v"][0:KC, c:c + 1], bias=V["w1v"][0:KC, c:c + 1])
                            act_(aT[0:KC, c, a0:a0 + TR], src[:, c, :], ACT.Copy, scale=V["w2v"][0:KC, c:c + 1])
                    if n == 6:
                        for c in range(CH):
                            act_(xpad[0:KC, c, t * PER_TILE:(t + 1) * PER_TILE, PAD:PAD + SEQ],
                                 src[:, c, :].rearrange("p (i s) -> p i s", i=PER_TILE), ACT.Copy).then_inc(pad_ready, 1)
                    last = act_(xT[0:KC, :, a0:a0 + TR], src, ACT.Copy)
                last.then_inc(xT_ready, 1)

            def take_x(n):
                for t in range(TILES):
                    take_tile(n, t, x_bank(n, t))

            def attention(a, n):
                g0 = TILES * a

                def take_qk(t):
                    sc_.wait_ge(qkT_psum, g0 + t + 1)
                    need(sc_, s_psum, g0 + t - 1)
                    act_(qkT[0:KC, t % 2, :, :], ps[0:KC, 2, 0:2 * CH * TR].rearrange("p (c r) -> p c r", c=2 * CH),
                         ACT.Copy).then_inc(qkT_ready, 1)

                def take_v(t):
                    sc_.wait_ge(v_psum, g0 + t + 1)
                    need(sc_, o_psum, g0 + t - 1)
                    for c in range(CH):
                        w = HPC * (KC + HD)
                        v0 = ((t % 2) * HEADS + c * HPC) * KC
                        last = act_(vpad_all[0:TR, v0:v0 + w].rearrange("p (h d) -> p h d", h=HPC)[:, :, 0:HD],
                                    ps[0:TR, 1, c * KC:(c + 1) * KC].rearrange("p (h d) -> p h d", h=HPC), ACT.Copy)
                    last.then_inc(v_ready, 1)

                def exps(t, g):
                    sc_.wait_ge(smax_ready, g0 + t + 1)
                    need(sc_, pT_psum, 3 * (g0 + t - 1))
                    for i in range(4):
                        hh = 4 * g + i
                        last = act_(prob[0:TR, t % 2, hh, :], ps[0:TR, 3 + g, i * TR:(i + 1) * TR], ACT.Exp,
                                    bias=nbias[0:TR, t % 2, hh:hh + 1], scale=HD ** -0.5,
                                    accum_out=rowsum[0:TR, t % 2, hh:hh + 1])
                    last.then_inc(exp_ready, 1)

                take_qk(0)
                for s in range(TILES + 3):
                    if s == TILES:
                        first_splits(a * 2)
                    if s >= 3:
                        take_tile(n + 1, s - 3, 7)
                    if s < TILES:
                        exps(s, 0)
                        take_v(s)
                        exps(s, 1)
                        exps(s, 2)
                    if s + 1 < TILES:
                        take_qk(s + 1)

            def trilinear():
                for s in range(TILES + 1):
                    if s < TILES:
                        sc_.wait_ge(tri_max, s + 1)
                        need(sc_, triT_psum, s - 1)
                        act_(prob[0:TR, s % 2, 0, :], ps[0:TR, 3 + s % 2, 0:TR], ACT.Exp,
                             bias=nmax[0:TR, s:s + 1], accum_out=psumr[0:TR, s:s + 1]).then_inc(tri_exp, 1)
                    if s >= 1:
                        t = s - 1
                        sc_.wait_ge(triT_psum, t + 1)
                        need(sc_, trio_psum, t - 1)
                        act_(probT[0:TR, t % 2, 0, :], ps[0:TR, (5, 2)[t % 2], 0:TR], ACT.Copy).then_inc(triT_ready, 1)

            def convolution():
                for t in range(TILES):
                    sc_.wait_ge(vt_psum, t + 1)
                    act_(vtok[0:TR, t, :], ps[0:TR, 6 + t % 2, 0:D], ACT.Copy).then_inc(vt_ready, 1)
                sc_.wait_ge(kern_sub, 1)
                act_(kexp[0:TR, :, :], kexp[0:TR, :, :], ACT.Exp).then_inc(kern_exp, 1)

            def split(L, e, b, j, loads):
                m = MOE[L]
                cols = slice(j * 256, (j + 1) * 256)
                sc_.wait_ge(w1_loaded[b], loads * 16)
                if isinstance(e, int) and e < 2:
                    need(sc_, hid_psum, m["u0"])
                else:
                    sc_.wait_ge(hid_psum, (e - 2) * m["units"] + (m["u0"] + 2 * j + 2))
                act_(W1h[0:KC, b, :, cols], W1[0:KC, b, :, cols], ACT.Copy).then_inc(w1_high, 1)

            def first_splits(L):
                for e in range(2):
                    for j in range(MOE[L]["pairs"]):
                        split(L, e, 1 - e, j, MOE[L][f"w{1 - e}"] + 1)

            def mixture(L):
                m = MOE[L]
                P, U, E = m["pairs"], m["units"], m["routed"]
                if L == 3:
                    for q in range(CH):
                        for f in range(2):
                            w = TPAD // 2 + f
                            a0 = f * (TPAD // 2)
                            sc_.wait_ge(r_psum, 2 * q + f + 1)
                            act_(rT[0:KC, q, a0:a0 + w], ps[0:KC, 2 + 2 * q + f, 0:w], ACT.Relu,
                                 bias=V["br1"][0:KC, q:q + 1]).then_inc(r_ready, 1)
                sc_.wait_ge(gate_in, L + 1)
                act_(sc[0:TR, :, 0:E], sc[0:TR, :, 0:E] if L != 1 else lg[0:TR, :, 0:E],
                     ACT.Sigmoid if L == 1 else ACT.Exp).then_inc(gate_out, 1)

                def units(e, b, loads, ahead=True):
                    if m["bias"] and m["kind"] != "swiglu":
                        sc_.wait_ge(biases_loaded[b], (loads + m[f"b{b}"]) * 16)
                    for u in range(U):
                        j, f = u // 2, u % 2
                        U0 = m["u0"] + u
                        if m["kind"] == "silu":
                            sc_.wait_ge(hid_psum, e * U + (U0 + 1))
                            if not (isinstance(e, int) and U0 + e * U < 2):
                                sc_.wait_ge(b_used, e * U + (U0 - 1))
                            bias = biases[:, b, 2 * j:2 * j + 1] if m["bias"] else 0.0
                            act_(gate[:, f, :], ps[:, 2 * f, 0:HALF], ACT.Silu, bias=bias).then_inc(a_used, 1)
                        elif m["kind"] == "relu":
                            sc_.wait_ge(hid_psum, e * U + (U0 + 1))
                            act_(act[:, b, 2 * j, f * HALF:(f + 1) * HALF], ps[:, 2 * f, 0:HALF], ACT.Relu,
                                 bias=biases[:, b, 2 * j:2 * j + 1]).then_inc(a_used, 1)
                        else:
                            sc_.wait_ge(a_used, e * U + (U0 + 1))
                            if not (isinstance(e, int) and u + e * U < 2):
                                sc_.wait_ge(glu_ready, e * U + (u - 1))
                            act_(gsig[:, f, :], gate[:, f, :], ACT.Sigmoid, scale=1.702).then_inc(sig_ready, 1)
                        if f and ahead:
                            split(L, e + 2, b, j, loads + (m[f"w{b}"] + 1))

                units(0, 1, 1)
                with sc_.Fori(0, m["loops"] - 1) as i:
                    units(2 * i + 1, 0, i + 1)
                    units(2 * i + 2, 1, i + 2)
                i = m["loops"] - 1
                units(2 * i + 1, 0, i + 1, ahead=m["tail"])
                units(2 * i + 2, 1, i + 2, ahead=False)
                if m["tail"]:
                    units(m["n"] - 1, 0, m["n"] // 2, ahead=False)
                if m["bias"]:
                    G = m["n"]
                    at = sum(1 for x in MOE[:L] if x["bias"])
                    sc_.wait_ge(cwT_psum, 2 * at + 1)
                    act_(cwT[0:G, 0:4 * TR], ps[0:G, 7, 0:4 * TR], ACT.Copy).then_inc(cwT_ready, 1)
                    sc_.wait_ge(cwT_psum, 2 * at + 2)
                    act_(cwT[0:G, 4 * TR:5 * TR], ps[0:G, 7, 0:TR], ACT.Copy).then_inc(cwT_ready, 1)

            take_x(0)
            attention(0, 0)
            mixture(0)
            sc_.wait_ge(packed["p_l1"], 16)
            take_x(2)
            trilinear()
            first_splits(1)
            take_x(3)
            mixture(1)
            take_x(4)
            attention(1, 4)
            mixture(2)
            take_x(6)
            convolution()
            first_splits(3)
            take_x(7)
            mixture(3)

        @block.gpsimd
        def _(pool):
            pool.memset(vpad_all[:, :], 0.0).then_inc(filled, 1)
            pool.memset(xpad[:, :, :, :], 0.0).then_inc(filled, 1)

            def attention(a):
                g0 = TILES * a

                def mask_keys(t):
                    pool.wait_ge(qkT_ready, g0 + t + 1)
                    pool.tensor_tensor(kmask[0:KC, t % 2, HPC:, :],
                                       qkT[0:KC, t % 2, CH + 1, :].unsqueeze(1).broadcast_to([KC, HPC, TR]),
                                       V["hmask"][0:KC, :].unsqueeze(2).broadcast_to([KC, HPC, TR]),
                                       ALU.mult).then_inc(kmask_ready[1], 1)

                def normalise(t):
                    pool.wait_ge(rowsum_ready, g0 + t + 1)
                    p = prob[0:TR, t % 2, :, :]
                    pool.tensor_tensor(p, p, rowsum[0:TR, t % 2, :].unsqueeze(2).broadcast_to([TR, HEADS, TR]),
                                       ALU.mult).then_inc(prob_ready, 1)

                mask_keys(0)
                for t in range(TILES):
                    if t + 1 < TILES:
                        mask_keys(t + 1)
                    normalise(t)

            def mixture(L):
                m = MOE[L]
                P, U = m["pairs"], m["units"]

                def split(e, b, j):
                    cols = slice(j * 256, (j + 1) * 256)
                    pool.wait_ge(w1_high, e * P + (m["q0"] + j + 1))
                    pool.tensor_tensor(W1l[0:KC, b, :, cols], W1[0:KC, b, :, cols],
                                       W1h[0:KC, b, :, cols].bitcast(F32), ALU.subtract).then_inc(w1_low, 1)

                def units(e, b, ahead=True):
                    for u in range(U):
                        j, f = u // 2, u % 2
                        if m["kind"] == "swiglu":
                            pool.wait_ge(sig_ready, e * U + (u + 1))
                            pool.tensor_tensor(gsig[:, f, :], gate[:, f, :], gsig[:, f, :],
                                               ALU.mult).then_inc(glu_ready, 1)
                        if f and ahead:
                            split(e + 2, b, j)

                for e in range(2):
                    for j in range(P):
                        split(e, 1 - e, j)
                units(0, 1)
                with pool.Fori(0, m["loops"] - 1) as i:
                    units(2 * i + 1, 0)
                    units(2 * i + 2, 1)
                i = m["loops"] - 1
                units(2 * i + 1, 0, ahead=m["tail"])
                units(2 * i + 2, 1, ahead=False)
                if m["tail"]:
                    units(m["n"] - 1, 0, ahead=False)

            pool.wait_ge(packed["p_l0"], 16)
            pool.tensor_copy(maskA[:, :], V["same_q"]).then_inc(masks_in, 1)
            pool.tensor_copy(maskB[:, :], V["same_k"]).then_inc(masks_in, 1)
            attention(0)
            mixture(0)
            mixture(1)
            attention(1)
            mixture(2)
            pool.wait_ge(packed["p_l3"], 16)
            pool.tensor_tensor(fold[0:KC, :, :], v3("pww", CH)[0:KC, 1, :].unsqueeze(1).broadcast_to([KC, TAPS, KC]),
                               v3("dww", CH)[0:KC, 1, :].unsqueeze(2).broadcast_to([KC, TAPS, KC]),
                               ALU.mult).then_inc(folded, 1)
            mixture(3)

        @block.vector
        def _(dve):
            steps = [0]

            def link(ins):
                steps[0] += 1
                ins.then_inc(vec, 1)
                dve.wait_ge(vec, steps[0])

            tt, ts, stt = dve.tensor_tensor, dve.tensor_scalar, dve.scalar_tensor_tensor

            def rsqrt(dst, x, t0, t1):
                y, a = nt[0:TR, 0, t0:t1], nt[0:TR, 1, t0:t1]
                link(ts(nti[0:TR, t0:t1], x.bitcast(I32), 1, None, ALU.logical_shift_right))
                link(ts(y.bitcast(I32), nti[0:TR, t0:t1], -1.0, float(0x5F3759DF + 2 ** 30 - 2 ** 22), ALU.mult, ALU.add))
                for k in range(3):
                    if t1 - t0 == 1:
                        link(stt(out=a, in0=y, scalar=x, in1=y, op0=ALU.mult, op1=ALU.mult))
                    else:
                        link(tt(a, y, y, ALU.mult))
                        link(tt(a, a, x, ALU.mult))
                    link(stt(out=dst if k == 2 else y, in0=a, scalar=1.5, in1=y, op0=ALU.add, op1=ALU.mult))

            def statistics(t0, t1):
                for t in range(t0, t1):
                    last = dve.bn_stats(st[0:TR, t, :], h[0:TR, t, :])
                link(last)
                for t in range(t0, t1):
                    dve.bn_aggr(mv[0:TR, t, :], st[0:TR, t, :]).then_inc(vec, 1)
                    steps[0] += 1

            def low_tokens(L, t0, t1):
                for t in range(t0, t1):
                    dve.wait_ge(xT_ready, TILES * (2 * L + 1) + t + 1)
                    a0, a1 = t * TR, t * TR + rows(t)
                    tt(xl[0:KC, :, a0:a1], xT[0:KC, :, a0:a1], xh[0:KC, :, a0:a1].bitcast(F32),
                       ALU.subtract).then_inc(x_low, 1)

            def layernorm(n, t0, t1):
                dve.wait_ge(vec, steps[0])
                x, rstd = nt[0:TR, 2, t0:t1], nt[0:TR, 3, t0:t1]
                link(ts(x, mv[0:TR, t0:t1, 1], EPS, -0.5, ALU.add, ALU.mult))
                rsqrt(rstd, x, t0, t1)
                for t in range(t0, t1):
                    ins = ts(xhat[0:TR, t, :], h[0:TR, t, :], mv[0:TR, t, 0:1], rstd[:, t - t0:t - t0 + 1],
                             ALU.subtract, ALU.mult)
                    if n == 5:
                        last = ins
                    else:
                        ins.then_inc(ln_ready, 1)
                if n == 5:
                    link(last)
                    for t in range(t0, t1):
                        last = dve.tensor_tensor_reduce(xrms[0:TR, t, :], xhat[0:TR, t, :], xhat[0:TR, t, :],
                                                        1.0, 0.0, ALU.mult, ALU.add, s5[0:TR, 0, t:t + 1])
                    link(last)
                    link(ts(x, s5[0:TR, 0, t0:t1], -0.5 / D, -0.5 * EPS, ALU.mult, ALU.add))
                    rsqrt(rstd, x, t0, t1)
                    for t in range(t0, t1):
                        ts(xrms[0:TR, t, :], xhat[0:TR, t, :], rstd[:, t - t0:t - t0 + 1], None,
                           ALU.mult).then_inc(ln_ready, 1)
                    link(tt(h[0:TR, t0:t1, :], h[0:TR, t0:t1, :], xhat[0:TR, t0:t1, :], ALU.add))

            def attention(a, n):
                g0 = TILES * a
                cos = V[f"cos{a}"][0:TR, :].unsqueeze(1).broadcast_to([TR, 2 * HEADS, HD])
                sin = V[f"sin{a}"][0:TR, :]

                def rotate(t):
                    src = ps[0:TR, 0, 0:2 * D].rearrange("p (g d) -> p g d", d=HD)
                    r0 = rope[0:TR, 0, :].rearrange("p (g d) -> p g d", d=HD)
                    r1 = rope[0:TR, 1, :].rearrange("p (g d) -> p g d", d=HD)
                    dve.wait_ge(qk_psum, g0 + t + 1)
                    tt(r0, src, cos, ALU.mult)
                    for f in range(2):
                        w = HD // 2
                        last = tt(r1[:, :, f * w:(f + 1) * w], src[:, :, (1 - f) * w:(2 - f) * w],
                                  sin[:, f * w:(f + 1) * w].unsqueeze(1).broadcast_to([TR, 2 * HEADS, w]), ALU.mult)
                    last.then_inc(rope_used, 1)
                    dve.wait_ge(rope_used, g0 + t + 1)
                    need(dve, qkT_psum, g0 + t - 1)
                    tt(qk[0:TR, t % 2, :], rope[0:TR, 0, :], rope[0:TR, 1, :], ALU.add).then_inc(rope_ready, 1)
                    dve.wait_ge(rope_ready, g0 + t + 1)

                def mask_keys(t):
                    dve.wait_ge(qkT_ready, g0 + t + 1)
                    tt(kmask[0:KC, t % 2, 0:HPC, :],
                       qkT[0:KC, t % 2, CH, :].unsqueeze(1).broadcast_to([KC, HPC, TR]),
                       V["hmask"][0:KC, :].unsqueeze(2).broadcast_to([KC, HPC, TR]), ALU.mult).then_inc(kmask_ready[0], 1)

                def maxima(t):
                    dve.wait_ge(s_psum, g0 + t + 1)
                    s3 = ps[0:TR, 3:6, 0:4 * TR].rearrange("p b (i k) -> p b i k", i=4)
                    link(dve.tensor_reduce(smax[0:TR, :].rearrange("p (b i) -> p b i", b=3), s3, AX, ALU.max))
                    ts(nbias[0:TR, t % 2, :], smax[0:TR, :], -HD ** -0.5, None, ALU.mult).then_inc(smax_ready, 1)

                def invert_sums(t):
                    dve.wait_ge(exp_ready, 3 * (g0 + t + 1))
                    dve.reciprocal(rowsum[0:TR, t % 2, :], rowsum[0:TR, t % 2, :]).then_inc(rowsum_ready, 1)

                def take_p(t):
                    need(dve, o_psum, g0 + t - 1)
                    for g in range(3):
                        dve.wait_ge(pT_psum, 3 * (g0 + t) + g + 1)
                        dve.tensor_copy(probT[0:TR, t % 2, 4 * g:4 * g + 4, :],
                                        ps[0:TR, 6 + g % 2, 0:4 * TR].rearrange("p (c r) -> p c r", c=4)).then_inc(pT_ready, 1)

                def take_o(t):
                    dve.wait_ge(o_psum, g0 + t + 1)
                    need(dve, proj_psum, g0 + t)
                    dve.tensor_copy(oT[0:KC, :, :],
                                    ps[0:KC, 1, 0:CH * TR].rearrange("p (c r) -> p c r", c=CH)).then_inc(o_ready, 1)

                def add(t):
                    dve.wait_ge(proj_psum, g0 + t + 1)
                    tt(h[0:TR, t, :], ps[0:TR, 2, 0:D], h[0:TR, t, :], ALU.add).then_inc(h_added, 1)

                rotate(0)
                layernorm(n, 2, TILES)
                mask_keys(0)
                for s in range(TILES + 3):
                    if s < TILES:
                        maxima(s)
                    if 0 <= s - 2 < TILES:
                        add(s - 2)
                    if s + 1 < TILES:
                        rotate(s + 1)
                    if 0 <= s - 1 < TILES:
                        take_p(s - 1)
                    if s + 1 < TILES:
                        mask_keys(s + 1)
                    if 0 <= s - 2 < TILES:
                        dve.wait_ge(h_added, 2 * TILES * a + s - 1)
                        statistics(s - 2, s - 1)
                        layernorm(n + 1, s - 2, s - 1)
                    if s >= 3:
                        low_tokens(2 * a, s - 3, s - 2)
                    if s < TILES:
                        invert_sums(s)
                    if 0 <= s - 1 < TILES:
                        take_o(s - 1)

            def trilinear():
                def add(t):
                    dve.wait_ge(trio_psum, t + 1)
                    link(dve.reciprocal(rsum[0:TR, t:t + 1], psumr[0:TR, t:t + 1]))
                    stt(out=h[0:TR, t, :], in0=ps[0:TR, t % 2, 0:D], scalar=rsum[0:TR, t:t + 1],
                        in1=h[0:TR, t, :], op0=ALU.mult, op1=ALU.add).then_inc(h_added, 1)
                    dve.wait_ge(h_added, TILES + t + 1)

                for s in range(TILES + 2):
                    if s < TILES:
                        dve.wait_ge(tri_psum, s + 1)
                        dve.tensor_reduce(nmax[0:TR, s:s + 1], ps[0:TR, 3 + s % 2, 0:TR], AX, ALU.max,
                                          negate=True).then_inc(tri_max, 1)
                    if s >= 2:
                        add(s - 2)
                        statistics(s - 2, s - 1)
                    if s - 2 == FIRST - 1:
                        layernorm(3, 0, FIRST)
                low_tokens(1, 0, FIRST)
                layernorm(3, FIRST, TILES)
                low_tokens(1, FIRST, TILES)

            def convolution():
                dve.wait_ge(pad_ready, CH * TILES)
                dst = dwc[0:KC, 0, :].rearrange("p (i s) -> p i s", s=SEQ)
                w = v3("dww", CH)[0:KC, 0, :]
                link(ts(dst, xpad[0:KC, 0, :, 0:SEQ], w[:, 0:1], None, ALU.mult))
                for k in range(1, TAPS):
                    ins = stt(out=dst, in0=xpad[0:KC, 0, :, k:k + SEQ], scalar=w[:, k:k + 1], in1=dst,
                              op0=ALU.mult, op1=ALU.add)
                    if k < TAPS - 1:
                        link(ins)
                ins.then_inc(dw_ready, 1)
                dve.wait_ge(xT_ready, 7 * TILES)
                for i, (c, f) in enumerate(((1, 0), (1, 1), (0, 0), (0, 1))):
                    a0, a1 = image_half(f)
                    dve.wait_ge(pw_psum, i + 1)
                    stt(out=ca[0:KC, c, a0:a1], in0=ps[0:KC, 2 * c + f, 0:a1 - a0], scalar=V["pwb"][0:KC, c:c + 1],
                        in1=xT[0:KC, c, a0:a1], op0=ALU.add, op1=ALU.mult).then_inc(ca_ready, 1)
                N = TAPS * HEADS
                dve.wait_ge(kern_psum, 1)
                dve.tensor_copy(kern[0:TR, 0:4, :], ps[0:TR, 4, 0:4 * N].rearrange("p (t n) -> p t n", t=4))
                link(dve.tensor_copy(kern[0:TR, 4, :], ps[0:TR, 5, 0:N]))

                def by_tap(x):
                    return x[0:TR, :, :].rearrange("p t (k h) -> p t k h", k=TAPS)

                def over(x):
                    return x[0:TR, :, :].rearrange("p t (k h) -> p t h k", k=TAPS)

                def spread(x, t):
                    return x[0:TR, t, :].unsqueeze(1).broadcast_to([TR, TAPS, HEADS])

                for t in range(TILES):
                    last = dve.tensor_reduce(kmx[0:TR, t, :], over(kern)[:, t, :, :], AX, ALU.max)
                link(last)
                for t in range(TILES):
                    last = tt(by_tap(kexp)[:, t, :, :], by_tap(kern)[:, t, :, :], spread(kmx, t), ALU.subtract)
                last.then_inc(kern_sub, 1)
                dve.wait_ge(kern_exp, 1)
                for t in range(TILES):
                    last = dve.tensor_reduce(kmx[0:TR, t, :], over(kexp)[:, t, :, :], AX, ALU.add)
                link(last)
                link(dve.reciprocal(kmx[0:TR, :, :], kmx[0:TR, :, :]))
                for t in range(TILES):
                    last = tt(by_tap(kern)[:, t, :, :], by_tap(kexp)[:, t, :, :], spread(kmx, t), ALU.mult)
                link(last)
                for t in range(TILES):
                    w = kern[0:TR, t, :].unsqueeze(2)
                    for b in range(TAP_BANKS):
                        k0, k1 = 2 * b, min(2 * b + 2, TAPS)
                        G = (k1 - k0) * HEADS
                        dve.wait_ge(shift_psum, TAP_BANKS * t + b + 1)
                        tt(prod[0:TR, k0:k1, :].rearrange("p k (h d) -> p (k h) d", d=HD),
                           ps[0:TR, b, 0:G * HD].rearrange("p (h d) -> p h d", d=HD),
                           w[:, k0 * HEADS:k1 * HEADS, :].broadcast_to([TR, G, HD]), ALU.mult).then_inc(shift_used, 1)
                    dve.wait_ge(shift_used, TAP_BANKS * (t + 1))
                    link(dve.tensor_reduce(conv[0:TR, :], prod[0:TR, :, :].rearrange("p k d -> p d k"), AX, ALU.add))
                    link(tt(h[0:TR, t, :], h[0:TR, t, :], conv[0:TR, :], ALU.add))
                    statistics(t, t + 1)
                    if t == FIRST - 1:
                        layernorm(7, 0, FIRST)
                    if t == FIRST:
                        low_tokens(3, 0, FIRST)
                layernorm(7, FIRST, TILES)
                low_tokens(3, FIRST, TILES)

            def choose(s, N, top, dst):
                Z = 8 - top
                field = chosen[0:TR, :, 0:N + Z]
                dve.tensor_copy(field[:, :, 0:N], s)
                link(dve.memset(field[:, :, N:], NEVER))
                for t in range(TILES):
                    last = dve.max(largest[0:TR, t, :], field[:, t, :])
                link(last)
                link(dve.memset(largest[0:TR, :, top:8], NEVER))
                for t in range(TILES):
                    last = dve.match_replace(field[:, t, :], largest[0:TR, t, :], field[:, t, :], MARK)
                link(last)
                link(ts(dst, field[:, :, 0:N], MARK, None, ALU.is_equal))

            def wide(x, N):
                return x.unsqueeze(2).broadcast_to([TR, TILES, N])

            def gating(L, meanwhile):
                m = MOE[L]
                E = m["routed"]
                c0 = m["shared"]
                dve.wait_ge(gate_psum, L + 1)
                l, s, r, p = lg[0:TR, :, 0:E], sc[0:TR, :, 0:E], sr[0:TR, :, 0:E], pick[0:TR, :, 0:E]
                mx, sm = s5[0:TR, 0, :], s5[0:TR, 1, :]
                ins = dve.tensor_copy(l, ps[0:TR, 7, 0:16 * TILES].rearrange("p (t e) -> p t e", e=16)[:, :, 0:E])
                if L == 1:
                    ins.then_inc(gate_in, 1)
                else:
                    link(ins)
                    link(dve.tensor_reduce(mx, l, AX, ALU.max))
                    tt(s, l, wide(mx, E), ALU.subtract).then_inc(gate_in, 1)
                meanwhile()
                if L >= 2:
                    choose(l, E, m["top"], p)
                    dve.wait_ge(gate_out, L + 1)
                    link(tt(r, s, p, ALU.mult))
                    link(dve.tensor_reduce(sm, r, AX, ALU.add))
                    link(dve.reciprocal(sm, sm))
                    tt(cw[0:TR, :, 0:E], r, wide(sm, E), ALU.mult).then_inc(cw_ready, 1)
                    dve.wait_ge(cw_ready, L + 1)
                    return
                dve.wait_ge(gate_out, L + 1)
                if L == 0:
                    link(dve.tensor_reduce(sm, s, AX, ALU.add))
                    link(dve.reciprocal(sm, sm))
                    link(tt(s, s, wide(sm, E), ALU.mult))
                link(tt(r, s, V[f"gb{L}"][0:TR, :].unsqueeze(1).broadcast_to([TR, TILES, E]), ALU.add))
                G = m["groups"]
                gs, gp = gsum[0:TR, :, 0:G], gpick[0:TR, :, 0:G]
                link(tt(gs, r[:, :, 0::2], r[:, :, 1::2], ALU.add))
                choose(gs, G, m["top_groups"], gp)
                for f in range(2):
                    last = tt(r[:, :, f::2], r[:, :, f::2], gp, ALU.mult)
                link(last)
                link(ts(gs, gp, 1e30, -1e30, ALU.mult, ALU.add))
                for f in range(2):
                    last = tt(r[:, :, f::2], r[:, :, f::2], gs, ALU.add)
                link(last)
                choose(r, E, m["top"], p)
                out_ = cw[0:TR, :, c0:c0 + E]
                if L == 0:
                    stt(out=out_, in0=p, scalar=2.5, in1=s, op0=ALU.mult, op1=ALU.mult).then_inc(cw_ready, 1)
                else:
                    link(tt(r, s, p, ALU.mult))
                    link(dve.tensor_reduce(sm, r, AX, ALU.add))
                    link(ts(sm, sm, 1e-6, None, ALU.add))
                    link(dve.reciprocal(sm, sm))
                    tt(out_, r, wide(sm, E), ALU.mult).then_inc(cw_ready, 1)
                dve.wait_ge(cw_ready, L + 1)

            def mixture(L):
                m = MOE[L]
                P, U = m["pairs"], m["units"]
                if m["shared"]:
                    link(dve.memset(cw[:, :, 0:1], 1.0))

                def units(e, b, loads):
                    if m["bias"]:
                        dve.wait_ge(biases_loaded[b], (loads + m[f"b{b}"]) * 16)
                    if m["kind"] == "swiglu":
                        ts(lin_bias[:, b, :], biases[:, b, 1::2], 1.0, None, ALU.add).then_inc(lin_bias_ready, 1)
                        dve.wait_ge(lin_bias_ready, e + 1)

                    def last_factor(u):
                        j, f = u // 2, u % 2
                        dve.wait_ge(glu_ready, e * U + (u + 1))
                        stt(out=act[:, b, j, f * HALF:(f + 1) * HALF], in0=lin[:, f, :], scalar=-6.0,
                            in1=gsig[:, f, :], op0=ALU.max, op1=ALU.mult).then_inc(act_ready, 1)

                    for u in range(U):
                        j, f = u // 2, u % 2
                        U0 = m["u0"] + u
                        if m["kind"] == "silu":
                            dve.wait_ge(a_used, e * U + (U0 + 1))
                            bias = biases[:, b, 2 * j + 1:2 * j + 2] if m["bias"] else 0.0
                            stt(out=act[:, b, j, f * HALF:(f + 1) * HALF], in0=ps[:, 2 * f + 1, 0:HALF], scalar=bias,
                                in1=gate[:, f, :], op0=ALU.add, op1=ALU.mult).then_inc(b_used, 1)
                        elif m["kind"] == "relu":
                            dve.wait_ge(hid_psum, e * U + (U0 + 1))
                            ts(act[:, b, 2 * j + 1, f * HALF:(f + 1) * HALF], ps[:, 2 * f + 1, 0:HALF],
                               biases[:, b, 2 * j + 1:2 * j + 2], 0.0, ALU.add, ALU.max).then_inc(b_used, 1)
                        else:
                            if u >= 2:
                                dve.wait_ge(act_ready, e * U + (u - 1))
                            elif not (isinstance(e, int) and e == 0):
                                dve.wait_ge(act_ready, e * U + (u - 1))
                            dve.wait_ge(hid_psum, e * U + (U0 + 1))
                            ts(gate[:, f, :], ps[:, 2 * f, 0:HALF], biases[:, b, 2 * j:2 * j + 1], 7.0,
                               ALU.add, ALU.min).then_inc(a_used, 1)
                            ts(lin[:, f, :], ps[:, 2 * f + 1, 0:HALF], lin_bias[:, b, j:j + 1], 8.0,
                               ALU.add, ALU.min).then_inc(b_used, 1)
                            if u >= 1:
                                dve.wait_ge(b_used, e * U + U0)
                                last_factor(u - 1)
                    if m["kind"] == "swiglu":
                        dve.wait_ge(b_used, e * U + (m["u0"] + U))
                        last_factor(U - 1)

                def add(e, first=False, final=False):
                    for k in range(3):
                        dve.wait_ge(y_psum, e * 3 + (m["y0"] + k + 1))
                        if not first:
                            dve.wait_ge(y_added, e * 3 + (m["y0"] + k - 2))
                        for t in range(2 * k, min(2 * k + 2, TILES)):
                            r = rows(t)
                            last = stt(out=h[0:r, t, :], in0=ps[0:r, 4 + k, (t % 2) * D:(t % 2 + 1) * D],
                                       scalar=cw[0:r, t, bass.ds(e, 1)], in1=h[0:r, t, :], op0=ALU.mult, op1=ALU.add)
                        last.then_inc(y_added, 1)
                        if final and L < 3 and k == 0:
                            dve.wait_ge(y_added, e * 3 + (m["y0"] + 1))
                            statistics(0, 2)
                            layernorm(2 * L + 2, 0, 2)
                    if final and L < 3:
                        dve.wait_ge(y_added, e * 3 + (m["y0"] + 3))
                        statistics(2, TILES)

                gating(L, lambda: units(0, 1, 1))
                units(1, 0, 1)
                add(0, True)
                units(2, 1, 2)
                add(1)
                with dve.Fori(1, m["loops"]) as i:
                    units(2 * i + 1, 0, i + 1)
                    add(2 * i)
                    units(2 * i + 2, 1, i + 2)
                    add(2 * i + 1)
                n = m["n"]
                if m["tail"]:
                    units(n - 1, 0, n // 2)
                    add(n - 2)
                if m["bias"]:
                    at = sum(1 for x in MOE[:L] if x["bias"])
                    dve.wait_ge(bias_psum, at + 1)
                    dve.wait_ge(y_added, m["y0"] + 3 * (n - 1))
                    for t in range(TILES):
                        r = rows(t)
                        last = tt(h[0:r, t, :], ps[0:r, t // 2, (t % 2) * D:(t % 2 + 1) * D], h[0:r, t, :], ALU.add)
                    link(last)
                add(n - 1, final=True)
                dve.wait_ge(y_added, m["y0"] + 3 * n)

            dve.memset(xT[96:97, :, :], 1.0).then_inc(filled, 1)
            dve.memset(oT[96:97, :, :], 1.0).then_inc(filled, 1)
            dve.memset(rT[96:97, :, :], 1.0).then_inc(filled, 1)
            link(dve.memset(ca[96:97, :, :], 1.0))
            for t0, t1 in ((0, 2), (2, TILES)):
                for t in range(t0, t1):
                    dve.wait_ge(tok_psum, t + 1)
                    last = dve.tensor_copy(h[0:TR, t, :], ps[0:TR, t, 0:D])
                link(last)
                statistics(t0, t1)
                if t0 == 0:
                    layernorm(0, 0, 2)
            dve.wait_ge(packed["p_l0"], 16)
            attention(0, 0)
            mixture(0)
            layernorm(2, 2, TILES)
            dve.wait_ge(packed["p_l1"], 16)
            trilinear()
            mixture(1)
            dve.wait_ge(packed["p_l2"], 16)
            attention(1, 4)
            mixture(2)
            layernorm(6, 2, TILES)
            dve.wait_ge(packed["p_l3"], 16)
            convolution()
            mixture(3)
            dve.nop().then_inc(h_done, TILES)


def chunks(w, bias=None):
    n = w.shape[1]
    o = np.zeros((97, CH, n), w.dtype)
    o[0:KC] = w.reshape(CH, KC, n).transpose(1, 0, 2)
    if bias is not None:
        o[KC, CH - 1] = bias
    return o.reshape(97, CH * n)


def rope_table(inv):
    pos = (np.arange(128) % SEQ).astype(np.float32)
    ang = (pos[:, None] * inv[None, :].astype(np.float32)).astype(np.float32)
    cos, sin = np.cos(ang).astype(np.float32), np.sin(ang).astype(np.float32)
    return np.concatenate([cos, cos], 1), np.concatenate([-sin, sin], 1)


def layout(I):
    f = np.float32
    S = {}
    x = I["x"].reshape(IMAGES, 3, 4, 16, 4, 16).transpose(1, 3, 5, 0, 2, 4).reshape(768, IMAGES, PATCHES)
    pt = np.zeros((768, TILES * PER_TILE, SEQ), f)
    pt[:, :IMAGES, 1:] = x
    w = I["L0_tok_W"].reshape(D, 16, 16, 3).transpose(3, 1, 2, 0).reshape(IN_CH, 128, D)
    patches = np.ascontiguousarray(np.concatenate([w, pt.reshape(IN_CH, 128, TPAD)], 2).transpose(1, 0, 2))
    ind = np.zeros((128, TILES * PER_TILE, SEQ), f)
    ind[0, :IMAGES, 1:] = 1
    ind[1, :IMAGES, 0] = 1
    S["ind"] = ind.reshape(128, TPAD)
    S["tokb"] = np.zeros((128, D), f)
    S["tokb"][0] = I["L0_tok_b"]
    S["tokb"][1] = I["cls_tok"].reshape(D)
    S["ident"] = np.eye(128, dtype=f)

    S["wqkv0"] = chunks(np.concatenate([I["L0_attn_wq"].T, I["L0_attn_wk"].T, I["L0_attn_wv"].T], 1),
                        np.concatenate([I["L0_attn_bq"], I["L0_attn_bk"], I["L0_attn_bv"]]))
    S["wo0"] = chunks(I["L0_attn_wo"].T, I["L0_attn_bo"])
    frac = 2.0 * np.arange(4, dtype=f) / HD
    inv0 = np.concatenate([1.0 / (f(10000.0) ** frac), np.zeros(4, f)]).astype(f)
    S["cos0"], S["sin0"] = rope_table(inv0)
    S["hmask"] = np.repeat(np.eye(HPC, dtype=f), HD, 0)
    S["gw0"] = chunks(I["L0_ffn_gate_w"], I["L0_ffn_gate_b"])
    S["gb0"] = np.broadcast_to(I["L0_ffn_bias"], (128, 16))
    S["b2_0"] = np.concatenate([I["L0_ffn_sbd"][None], I["L0_ffn_bd"]])

    for i, name in enumerate(["w1v", "w2v", "w3v"]):
        S[name] = I["L1_attn_w"][0, i * D:(i + 1) * D].reshape(CH, KC).T
    S["ones"] = np.ones((KC, TR), f)
    S["gw1"] = chunks(I["L1_ffn_gate_weight"].T)
    S["gb1"] = np.broadcast_to(I["L1_ffn_gate_bias"], (128, 8))

    S["wqkv1"] = chunks(I["L2_attn_w_qkv"].T, I["L2_attn_b_qkv"])
    S["wo1"] = chunks(I["L2_attn_w_proj"].T, I["L2_attn_b_proj"])
    inv1 = (1.0 / f(10000.0) ** (np.arange(0, HD, 2, dtype=f) / HD)).astype(f)
    S["cos1"], S["sin1"] = rope_table(inv1)
    S["nscale"] = I["L2_ffn_norm_scale"].reshape(CH, KC).T
    S["gw2"] = chunks(I["L2_ffn_gate_w"].T, I["L2_ffn_gate_b"])
    S["b2_2"] = I["L2_ffn_mlp2_b"]

    S["dww"] = I["L3_attn_dw_w"].reshape(CH, KC, TAPS).transpose(1, 0, 2).reshape(KC, CH * TAPS)
    pw = np.zeros((KC, CH, KC), f)
    ak = np.zeros((97, CH, TAPS, HPC), f)
    for c in range(CH):
        for i in range(HPC):
            hh = c * HPC + i
            pw[i * HD:(i + 1) * HD, c, i * HD:(i + 1) * HD] = I["L3_attn_pw_w"][hh].T
            ak[i * HD:(i + 1) * HD, c, :, i] = I["L3_attn_ak_w"][hh].T
            ak[KC, c, :, i] = I["L3_attn_ak_b"].reshape(HEADS, TAPS)[hh]
    S["pww"] = pw.reshape(KC, CH * KC)
    S["akw"] = ak.reshape(97, CH * TAPS * HPC)
    S["pwb"] = I["L3_attn_pw_b"].reshape(CH, KC).T
    S["ptw"] = chunks(I["L3_attn_pt_w"].T, I["L3_attn_pt_b"])
    l = np.arange(TR)
    sh = np.stack([(l[:, None] == l[None, :] + k - PAD) & (l[:, None] // SEQ == l[None, :] // SEQ)
                   for k in range(TAPS)], 1)
    S["shift"] = sh.astype(f).reshape(TR, TAPS * TR)
    S["wr1"] = chunks(I["L3_ffn_Wr1"].T)[0:KC]
    S["br1"] = I["L3_ffn_br1"].reshape(CH, KC).T
    S["gw3"] = chunks(I["L3_ffn_Wr2"].T, I["L3_ffn_br2"])
    S["b2_3"] = I["L3_ffn_b2"]

    same = (l[None, :] // SEQ == np.arange(PER_TILE)[:, None]).astype(f)
    mA, mB = np.zeros((128, TR), f), np.zeros((128, TR), f)
    mA[0:PER_TILE], mA[PER_TILE] = same, 1
    mB[0:PER_TILE], mB[PER_TILE] = same * BIG, -BIG
    S["same_q"], S["same_k"] = mA, np.tile(mB, (1, 4))



    O = {"patches": patches}
    for p, items in PACKS.items():
        blob = np.zeros((128, sum(c for _, _, c in items)), f)
        at = 0
        for name, rows, cols in items:
            blob[0:rows, at:at + cols] = S[name]
            at += cols
        O[p] = blob

    def up(pairs):
        e, p = pairs.shape[:2]
        return np.ascontiguousarray(pairs.reshape(e, p * 256, CH, KC).transpose(0, 3, 2, 1))

    def down(w):
        return np.ascontiguousarray(w.reshape(w.shape[0], -1, 128, D).transpose(0, 2, 1, 3))

    def with_shared(s, w):
        return np.concatenate([s[None], w])

    a0 = with_shared(I["L0_ffn_sWu"], I["L0_ffn_Wu"]).transpose(0, 2, 1)
    g0 = with_shared(I["L0_ffn_sWg"], I["L0_ffn_Wg"]).transpose(0, 2, 1)
    O["W1_0"] = up(np.stack([a0, g0], 1)[:, None])
    O["W2_0"] = down(with_shared(I["L0_ffn_sWd"], I["L0_ffn_Wd"]))
    a1 = with_shared(I["L1_ffn_sw1"], I["L1_ffn_w1"])
    g1 = with_shared(I["L1_ffn_sw3"], I["L1_ffn_w3"])
    O["W1_1"] = up(np.stack([a1, g1], 1)[:, None])
    O["W2_1"] = down(with_shared(I["L1_ffn_sw2"], I["L1_ffn_w2"]).transpose(0, 2, 1))
    w = I["L2_ffn_mlp1_w"].reshape(16, 3, 128, 2, D).transpose(0, 1, 3, 2, 4)
    O["W1_2"] = up(w)
    O["W2_2"] = down(I["L2_ffn_mlp2_w"].transpose(0, 2, 1))
    O["W1_3"] = up(I["L3_ffn_W1"].reshape(8, 3, 2, 128, D))
    O["bias_0"] = np.ascontiguousarray(np.stack([with_shared(I["L0_ffn_sbu"], I["L0_ffn_bu"]),
                                                 with_shared(I["L0_ffn_sbg"], I["L0_ffn_bg"])], 2))
    b = I["L2_ffn_mlp1_b"].reshape(16, 3, 128, 2).transpose(0, 2, 1, 3)
    O["bias_2"] = np.ascontiguousarray(b.reshape(16, 128, 6))
    O["bias_3"] = np.ascontiguousarray(I["L3_ffn_b1"].reshape(8, 6, 128).transpose(0, 2, 1))
    O["W2_3"] = down(I["L3_ffn_W2"].transpose(0, 2, 1))
    return O


def kernel(**inputs):
    import concourse.bacc as bacc
    from concourse.bass_utils import run_bass_kernel_spmd

    arrays = layout({k: np.asarray(v) for k, v in inputs.items()})
    nc = bacc.Bacc("TRN2", target_bir_lowering=False, num_devices=1)
    A = {k: nc.dram_tensor(k + "_dram", a.shape, mybir.dt.from_np(a.dtype), kind="ExternalInput").ap()
         for k, a in arrays.items()}
    out = nc.dram_tensor("out_dram", (TOKENS, D), F32, kind="ExternalOutput").ap()
    vit_tower(nc, A, out)
    r = run_bass_kernel_spmd(nc, [{k + "_dram": a for k, a in arrays.items()}], core_ids=[0])
    return r.results[0]["out_dram"].reshape(IMAGES, SEQ, D)
```

```python
from contextlib import ExitStack

import numpy as np

import concourse.bass as bass
from concourse import mybir

F32 = mybir.dt.float32
F32R = mybir.dt.float32r
BF16 = mybir.dt.bfloat16
I32 = mybir.dt.int32
ALU = mybir.AluOpType
ACT = mybir.ActivationFunctionType
AX = mybir.AxisListType.X

IMAGES, PATCHES = 32, 16
SEQ = PATCHES + 1
TOKENS = IMAGES * SEQ
D = 192
KC = 96
CH = D // KC
PER_TILE = 7
TR = PER_TILE * SEQ
TILES = -(-IMAGES // PER_TILE)
TPAD = TILES * TR
LAST = TOKENS - (TILES - 1) * TR
HALF = TOKENS // 2
FIRST = -(-HALF // TR)
HEADS, HD = 12, 16
HPC = HEADS // CH
TAPS = 9
PAD = (TAPS - 1) // 2
LPAD = SEQ + TAPS - 1
FILLS = 6
TAPS_A = 5
IN_CH = 768 // 128
EPS = 1e-5
BIG = 2.0 ** 60
GMAX = 17
NEVER, MARK = -3.0e38, 3.0e38

MOE = [
    dict(kind="silu", n=17, pairs=1, routed=16, top=4, groups=8, top_groups=4, shared=1, bias=True),
    dict(kind="silu", n=9, pairs=1, routed=8, top=2, groups=4, top_groups=2, shared=1, bias=False),
    dict(kind="swiglu", n=16, pairs=3, routed=16, top=4, groups=0, top_groups=0, shared=0, bias=True),
    dict(kind="relu", n=8, pairs=3, routed=8, top=2, groups=0, top_groups=0, shared=0, bias=True),
]
for _m in MOE:
    _m["units"] = 2 * _m["pairs"]
    _m["blocks"] = _m["pairs"] * (2 if _m["kind"] == "relu" else 1)
    _m["tail"] = _m["n"] % 2 == 0
    _m["loops"] = (_m["n"] - 1) // 2
MAXP, MAXB = 3, 6

PACKS = {
    "p_tok": [("ind", 128, TPAD), ("tokb", 128, D), ("ident", 128, 128)],
    "p_l0": [("wqkv0", 97, CH * 3 * D), ("wo0", 97, CH * D), ("cos0", 128, HD), ("sin0", 128, HD),
             ("same_q", 128, TR), ("same_k", 128, 4 * TR), ("hmask", KC, HPC), ("gw0", 128, CH * 16), ("gwb0", 128, 16), ("gb0", 128, 16),
             ("b2_0", 17, D)],
    "p_l1": [("w1v", KC, CH), ("w2v", KC, CH * TR), ("w3v", KC, CH), ("gw1", 128, CH * 8), ("gb1", 128, 8)],
    "p_l2": [("wqkv1", 97, CH * 3 * D), ("wo1", 97, CH * D), ("cos1", 128, HD), ("sin1", 128, HD),
             ("nscale", 128, CH), ("gw2", 128, CH * 16), ("gwb2", 128, 16), ("b2_2", 16, D)],
    "p_l3": [("dww", KC, CH * TAPS), ("pww", KC, CH * KC), ("pwb", KC, CH), ("akw", 97, CH * TAPS * HPC),
             ("ptw", 97, CH * D), ("shift", TR, TAPS * TR), ("wr1", 128, CH * D), ("br1", KC, CH),
             ("gw3", 97, CH * 8), ("b2_3", 8, D)],
}


def vit_tower(nc, A, out):
    with ExitStack() as ctx:
        def sb(name, shape, dt=F32):
            return ctx.enter_context(nc.sbuf_tensor(name, shape, dt))

        def sem(name):
            return ctx.enter_context(nc.semaphore(name))

        V = {}
        packs = {}
        for p, items in PACKS.items():
            packs[p] = sb(p, [128, sum(c for _, _, c in items)])
            at = 0
            for name, rows, cols in items:
                V[name] = packs[p][:, at:at + cols]
                at += cols

        def v3(name, a):
            return V[name].rearrange("p (a b) -> p a b", a=a)

        maskA = sb("maskA", [128, TR], BF16)
        maskB = sb("maskB", [128, 4 * TR], BF16)
        h = sb("h", [128, TILES, D])
        xhat = sb("xhat", [128, TILES, 256])
        xrms = sb("xrms", [128, TILES, 256])
        xT = sb("xT", [128, CH, TPAD])
        st = sb("st", [128, TILES, 6])
        mv = sb("mv", [128, TILES, 2])
        nt = sb("nt", [128, 4, 2 * TILES])
        nti = sb("nti", [128, 2 * TILES], I32)
        rope = sb("rope", [128, 2, 2 * D])
        qk = sb("qk", [128, 2, 2 * D])
        qkT = sb("qkT", [128, 2, 2 * CH, TR])
        hidden_or_scores = sb("hidden_or_scores", [128, 2 * MAXB * TOKENS])
        patches = hidden_or_scores[:, 0:IN_CH * (D + TPAD)].rearrange("p (c r) -> p c r", c=IN_CH)
        n = 2 * HEADS * TR
        kmask = hidden_or_scores[:, 0:n].rearrange("p (b h r) -> p b h r", b=2, h=HEADS)
        prob = hidden_or_scores[:, n:2 * n].rearrange("p (b h r) -> p b h r", b=2, h=HEADS)
        probT = sb("probT", [128, 2, HEADS, TR])
        prod = hidden_or_scores[:, 0:2 * TAPS * D].rearrange("p (b k d) -> p b k d", b=2, k=TAPS)
        vpad_all = sb("vpad", [128, 2 * HEADS * KC + KC])
        vpad = vpad_all[:, 0:2 * HEADS * KC].rearrange("p (b h c) -> p b h c", b=2, h=HEADS)
        smax = sb("smax", [128, HEADS])
        nbias = sb("nbias", [128, 2, HEADS])
        rowsum = sb("rowsum", [128, 2, HEADS])
        oT = sb("oT", [128, CH, TR])
        uT = sb("uT", [128, CH, TPAD])
        nmax = sb("nmax", [128, TILES])
        psumr = sb("psumr", [128, TILES])
        rsum = sb("rsum", [128, TILES])
        xpad = sb("xpad", [128, CH, TILES * PER_TILE, LPAD])
        dwc = uT
        fold = sb("fold", [128, TAPS, KC])
        ca = sb("ca", [128, CH, TPAD])
        moved = sb("moved", [128, TAPS, TILES, HEADS])
        rtap = sb("rtap", [128, TILES, HEADS])
        kexp = sb("kexp", [128, TILES, TAPS * HEADS])
        kmx = sb("kmx", [128, TILES, HEADS])
        vtok = sb("vtok", [128, TILES, D])
        conv = sb("conv", [128, D])
        W1 = sb("W1", [128, 2, CH, MAXP * 256])
        W1h = sb("W1h", [128, 2, CH, MAXP * 256], F32R)
        W1l = sb("W1l", [128, 2, CH, MAXP * 256], F32R)
        xh = sb("xh", [128, CH, TOKENS], F32R)
        xl = sb("xl", [128, TOKENS], F32R)
        xm = sb("xm", [128, CH, TPAD])
        W2 = sb("W2", [128, 2, MAXB, D])
        act = hidden_or_scores[:, :].rearrange("p (b q r) -> p b q r", b=2, q=MAXB)
        gate = sb("gate", [128, 2, HALF])
        gsig = sb("gsig", [128, 2, HALF])
        lin = sb("lin", [128, 2, HALF])
        cw = sb("cw", [128, TILES, GMAX])
        lg = sb("lg", [128, TILES, 16])
        sc = sb("sc", [128, TILES, 16])
        sr = sb("sr", [128, TILES, 16])
        gsum = sb("gsum", [128, TILES, 8])
        pick = sb("pick", [128, TILES, 16])
        gpick = sb("gpick", [128, TILES, 8])
        chosen = sb("chosen", [128, TILES, 24])
        largest = sb("largest", [128, TILES, 8])
        s5 = sb("s5", [128, 2, TILES])
        biases = sb("biases", [128, 2, 2 * MAXP])
        lin_bias = sb("lin_bias", [128, 2, MAXP])
        rT = sb("rT", [128, CH, TPAD])
        cwT = uT[:, 0, :]
        spare = sb("spare", [128, 1])

        ps = ctx.enter_context(nc.psum_tensor("ps", [128, 8, 512], F32))

        packed = {p: sem("loaded_" + p) for p in PACKS}
        patches_in = [sem(f"patches_in{c}") for c in range(IN_CH)]
        masks_in = sem("masks_in")
        vec = sem("vec_step")
        filled = sem("filled")
        tok_psum = sem("tok_psum")
        ln_ready = sem("ln_ready")
        xT_psum = sem("xT_psum")
        xT_ready = sem("xT_ready")
        qk_psum = sem("qk_psum")
        v_psum = sem("v_psum")
        rope_ready = sem("rope_ready")
        rope_used = sem("rope_used")
        qkT_psum = sem("qkT_psum")
        qkT_ready = sem("qkT_ready")
        kmask_ready = [sem("kmask0_ready"), sem("kmask1_ready")]
        v_ready = sem("v_ready")
        s_psum = sem("s_psum")
        smax_ready = sem("smax_ready")
        exp_ready = sem("exp_ready")
        rowsum_ready = sem("rowsum_ready")
        prob_ready = sem("prob_ready")
        pT_psum = sem("pT_psum")
        pT0_ready = sem("pT0_ready")
        pT_ready = sem("pT_ready")
        o_psum = sem("o_psum")
        o_ready = sem("o_ready")
        proj_psum = sem("proj_psum")
        h_added = sem("h_added")
        tri_psum = sem("tri_psum")
        tri_max = sem("tri_max")
        tri_exp = sem("tri_exp")
        triT_psum = sem("triT_psum")
        triT_ready = sem("triT_ready")
        trio_psum = sem("trio_psum")
        pad_ready = sem("pad_ready")
        dw_ready = sem("dw_ready")
        folded = sem("folded")
        pw_psum = sem("pw_psum")
        ca_ready = sem("ca_ready")
        vt_psum = sem("vt_psum")
        vt_ready = sem("vt_ready")
        kern_psum = sem("kern_psum")
        kern_sub = sem("kern_sub")
        kern_exp = sem("kern_exp")
        moved_psum = sem("moved_psum")
        moved_ready = sem("moved_ready")
        prod_ready = [sem("prod0_ready"), sem("prod1_ready")]
        shift_psum = sem("shift_psum")
        conv_used = sem("conv_used")
        r_psum = sem("r_psum")
        r_ready = sem("r_ready")
        gate_psum = sem("gate_psum")
        gate_in = sem("gate_in")
        gate_out = sem("gate_out")
        cw_ready = sem("cw_ready")
        cwT_psum = sem("cwT_psum")
        cwT_ready = sem("cwT_ready")
        bias_psum = sem("bias_psum")
        w1_loaded = [sem("w1_loaded0"), sem("w1_loaded1")]
        w1_high = sem("w1_high")
        w1_low = sem("w1_low")
        x_low = sem("x_low")
        w2_loaded = [sem("w2_loaded0"), sem("w2_loaded1")]
        biases_loaded = [sem("biases_loaded0"), sem("biases_loaded1")]
        lin_bias_ready = sem("lin_bias_ready")
        hid_psum = sem("hid_psum")
        a_used = sem("a_used")
        b_used = sem("b_used")
        sig_ready = sem("sig_ready")
        glu_ready = sem("glu_ready")
        act_ready = sem("act_ready")
        y_psum = sem("y_psum")
        y_added = sem("y_added")
        stored = sem("stored")

        for L, m in enumerate(MOE):
            prev = MOE[:L]
            m["u0"] = sum(p["n"] * p["units"] for p in prev)
            m["y0"] = sum(p["n"] * 3 for p in prev)
            m["q0"] = sum(p["n"] * p["pairs"] for p in prev)
            m["s0"] = sum(p["n"] * p["units"] for p in prev if p["kind"] == "swiglu")
            for b in range(2):
                m[f"w{b}"] = sum((p["n"] + b) // 2 for p in prev)
                m[f"b{b}"] = sum((p["n"] + b) // 2 for p in prev if p["bias"])

        def x_bank(n, t):
            return (7, 3, 6, 7, 6)[t] if n in (2, 4, 6) else 6 + t % 2

        def weigh(eng, t, part):
            k0, k1 = ((0, TAPS_A), (TAPS_A, TAPS))[part]
            shape = [TR, k1 - k0, HEADS, HD]
            eng.tensor_tensor(prod[0:TR, t % 2, k0:k1, :].rearrange("p k (h d) -> p k h d", d=HD),
                              vtok[0:TR, t, :].rearrange("p (h d) -> p h d", d=HD).unsqueeze(1).broadcast_to(shape),
                              moved[0:TR, k0:k1, t, :].unsqueeze(3).broadcast_to(shape),
                              ALU.mult).then_inc(prod_ready[part], 1)

        def image_half(f):
            mid = TILES * PER_TILE // 2 * SEQ
            return (0, mid) if f == 0 else (mid, TPAD)

        def rows(t):
            return TR if t < TILES - 1 else LAST

        def need(eng, s, n):
            if n > 0:
                eng.wait_ge(s, n)

        block = ctx.enter_context(nc.Block())

        @block.sync
        def _(sp):
            for c in range(IN_CH):
                sp.dma_start(patches[:, c, :], A["patches"][:, c, :]).then_inc(patches_in[c], 16)
            sp.dma_start(packs["p_tok"][:, :], A["p_tok"][:, :]).then_inc(packed["p_tok"], 16)
            sp.dma_start(packs["p_l0"][:, :], A["p_l0"][:, :]).then_inc(packed["p_l0"], 16)

            def load_first(L, e, b):
                m = MOE[L]
                P = m["pairs"]
                if isinstance(e, int) and e < 2:
                    need(sp, w1_low, m["q0"])
                else:
                    sp.wait_ge(w1_low, (e - 1) * P + m["q0"])
                sp.dma_start(W1[:, b, :, 0:P * 256], A[f"W1_{L}"][e, :, :, :]).then_inc(w1_loaded[b], 16)

            def load_rest(L, e, b):
                m = MOE[L]
                early = isinstance(e, int) and e < 2
                if m["bias"]:
                    for used in (a_used, b_used):
                        if early:
                            need(sp, used, m["u0"])
                        else:
                            sp.wait_ge(used, (e - 1) * m["units"] + m["u0"])
                    sp.dma_start(biases[:, b, 0:2 * m["pairs"]], A[f"bias_{L}"][e, :, :]).then_inc(biases_loaded[b], 16)
                if early:
                    need(sp, y_psum, m["y0"])
                else:
                    sp.wait_ge(y_psum, (e - 1) * 3 + m["y0"])
                sp.dma_start(W2[:, b, 0:m["blocks"], :], A[f"W2_{L}"][e, :, :, :]).then_inc(w2_loaded[b], 16)

            for L, m in enumerate(MOE):
                load_first(L, 0, 1)
                load_first(L, 1, 0)
                load_rest(L, 0, 1)
                load_rest(L, 1, 0)
                if L < 3:
                    p = f"p_l{L + 1}"
                    sp.dma_start(packs[p][:, :], A[p][:, :]).then_inc(packed[p], 16)
                load_first(L, 2, 1)
                load_first(L, 3, 0)
                load_first(L, 4, 1)
                load_rest(L, 2, 1)
                with sp.Fori(1, m["loops"] - 1) as i:
                    load_first(L, 2 * i + 3, 0)
                    load_rest(L, 2 * i + 1, 0)
                    load_first(L, 2 * i + 4, 1)
                    load_rest(L, 2 * i + 2, 1)
                n = m["n"]
                if m["tail"]:
                    load_first(L, n - 1, 0)
                for e in range(2 * m["loops"] - 1, n):
                    load_rest(L, e, (e + 1) % 2)
            for t in range(TILES):
                sp.wait_ge(y_added, MOE[3]["y0"] + 3 * (MOE[3]["n"] - 1) + t // 2 + 1)
                sp.dma_start(out[t * TR:t * TR + rows(t), :], h[0:rows(t), t, :]).then_inc(stored, 16)
            sp.wait_ge(stored, 16 * TILES)

        @block.tensor
        def _(pe):
            def bank(i, r=TR, c0=0, c1=512):
                return ps[0:r, i, c0:c1]

            def tokens():
                for c in range(IN_CH):
                    pe.wait_ge(patches_in[c], 16)
                    for t in range(TILES):
                        pe.matmul(bank(t, TR, 0, D), patches[:, c, D + t * TR:D + (t + 1) * TR],
                                  patches[:, c, 0:D], start=(c == 0), stop=False)
                pe.wait_ge(packed["p_tok"], 16)
                for t in range(TILES):
                    pe.matmul(bank(t, TR, 0, D), V["ind"][:, t * TR:(t + 1) * TR], V["tokb"],
                              start=False, stop=True).then_inc(tok_psum, 1)

            def xhat_of(n):
                return xrms if n == 5 else xhat

            def transpose_x(n, t0, t1):
                for t in range(t0, t1):
                    pe.wait_ge(ln_ready, TILES * n + t + 1)
                    before = [p for p in range(t) if x_bank(n, p) == x_bank(n, t)]
                    if before:
                        pe.wait_ge(xT_ready, TILES * n + before[-1] + 1)
                    transpose_tile(n, t, x_bank(n, t))

            def transpose_tile(n, t, b):
                x = xhat_of(n)[0:TR, t, :]
                if n % 2:
                    pe.transpose(ps[:, b, 0:TR], x[:, 0:128], V["ident"][0:TR, 0:TR])
                    pe.transpose(ps[:, b, TR:2 * TR], x[:, 128:256], V["ident"][0:TR, 0:TR]).then_inc(xT_psum, 1)
                    return
                for c in range(CH):
                    last = pe.transpose(ps[0:KC, b, c * TR:(c + 1) * TR],
                                        xhat_of(n)[0:TR, t, c * KC:(c + 1) * KC], V["ident"][0:TR, 0:TR])
                last.then_inc(xT_psum, 1)

            def attention(a, n):
                wqkv, wo = v3(f"wqkv{a}", CH), v3(f"wo{a}", CH)
                g0 = TILES * a
                h0 = 2 * TILES * a

                def project_qk(t):
                    pe.wait_ge(xT_ready, TILES * n + t + 1)
                    need(pe, rope_used, g0 + t)
                    for c in range(CH):
                        k = KC + c
                        last = pe.matmul(bank(0, TR, 0, 2 * D), xT[0:k, c, t * TR:(t + 1) * TR],
                                         wqkv[0:k, c, 0:2 * D], start=(c == 0), stop=(c == 1))
                    last.then_inc(qk_psum, 1)

                def project_v(t):
                    need(pe, o_ready, g0 + t - 1)
                    for c in range(CH):
                        k = KC + c
                        last = pe.matmul(bank(1, TR, 0, D), xT[0:k, c, t * TR:(t + 1) * TR],
                                         wqkv[0:k, c, 2 * D:3 * D], start=(c == 0), stop=(c == 1))
                    last.then_inc(v_psum, 1)

                def transpose_qk(t):
                    pe.wait_ge(rope_ready, g0 + t + 1)
                    need(pe, h_added, h0 + max(t - 2, 0))
                    need(pe, qkT_ready, g0 + t)
                    for c in range(2 * CH):
                        last = pe.transpose(ps[0:KC, 2, c * TR:(c + 1) * TR],
                                            qk[0:TR, t % 2, c * KC:(c + 1) * KC], V["ident"][0:TR, 0:TR])
                    last.then_inc(qkT_psum, 1)

                def scores(t):
                    pe.wait_ge(masks_in, 2)
                    pe.wait_ge(qkT_ready, g0 + t + 1)
                    pe.wait_ge(kmask_ready[0], g0 + t + 1)
                    pe.wait_ge(kmask_ready[1], g0 + t + 1)
                    for g in range(3):
                        need(pe, exp_ready, 3 * (g0 + t - 1) + g + 1)
                        for c in range(CH):
                            a0, a1 = max(4 * g, HPC * c), min(4 * g + 4, HPC * c + HPC)
                            if a0 < a1:
                                o = bank(3 + g, TR, (a0 - 4 * g) * TR, (a1 - 4 * g) * TR)
                                pe.matmul(o, maskA[:, :], maskB[:, 0:(a1 - a0) * TR], start=True, stop=False)
                                last = pe.matmul(o, qkT[0:KC, t % 2, c, :], kmask[0:KC, t % 2, a0:a1, :],
                                                 start=False, stop=True)
                        last.then_inc(s_psum, 1)

                def transpose_p(t):
                    pe.wait_ge(prob_ready, g0 + t + 1)
                    for g in range(3):
                        if g == 1:
                            pe.wait_ge(xT_ready, TILES * (n + 1) + max(t - 1, 0))
                        if g == 0:
                            pe.wait_ge(xT_ready, TILES * (n + 1))
                        if g == 2:
                            pe.wait_ge(pT0_ready, g0 + t + 1)
                        else:
                            need(pe, pT_ready, 2 * (g0 + t))
                        for i in range(4):
                            last = pe.transpose(ps[0:TR, 6 + g % 2, i * TR:(i + 1) * TR],
                                                prob[0:TR, t % 2, 4 * g + i, :], V["ident"][0:TR, 0:TR])
                        last.then_inc(pT_psum, 1)

                def outputs(t):
                    pe.wait_ge(pT_ready, 2 * (g0 + t + 1))
                    pe.wait_ge(v_ready, g0 + min(t + 2, TILES))
                    for c in range(CH):
                        for i in range(HPC):
                            last = pe.matmul(ps[0:KC, 1, c * TR:(c + 1) * TR], vpad[0:TR, t % 2, HPC * c + i, :],
                                             probT[0:TR, t % 2, HPC * c + i, :], start=(i == 0), stop=(i == HPC - 1))
                    last.then_inc(o_psum, 1)

                def output_projection(t):
                    pe.wait_ge(o_ready, g0 + t + 1)
                    pe.wait_ge(qkT_ready, g0 + min(t + 3, TILES))
                    need(pe, h_added, h0 + t)
                    for c in range(CH):
                        k = KC + c
                        last = pe.matmul(bank(2, TR, 0, D), oT[0:k, c, :], wo[0:k, c, :],
                                         start=(c == 0), stop=(c == 1))
                    last.then_inc(proj_psum, 1)

                def transpose_result(t):
                    pe.wait_ge(ln_ready, TILES * (n + 1) + t + 1)
                    pe.wait_ge(xT_ready, TILES * (n + 1) + t)
                    pe.wait_ge(pT_ready, 2 * (g0 + min(t + 2, TILES)))
                    transpose_tile(n + 1, t, 7)

                transpose_x(n, 0, 2)
                project_qk(0)
                transpose_x(n, 2, TILES)
                transpose_qk(0)
                project_qk(1)
                for s in range(TILES + 3):
                    if s < TILES:
                        scores(s)
                    if s >= 3:
                        transpose_result(s - 3)
                    if 0 <= s - 2 < TILES:
                        output_projection(s - 2)
                    if 0 < s < TILES - 1:
                        project_qk(s + 1)
                    if s < TILES:
                        project_v(s)
                    if 0 <= s - 1 < TILES:
                        transpose_p(s - 1)
                    if s + 1 < TILES:
                        transpose_qk(s + 1)
                    if 0 <= s - 1 < TILES:
                        outputs(s - 1)

            def trilinear(n):
                def scores(t):
                    pe.wait_ge(xT_ready, TILES * n + t + 1)
                    need(pe, tri_exp, t - 1)
                    o = bank(4 - t % 2, TR, 0, TR)
                    pe.matmul(o, maskA[:, :], maskB[:, 0:TR], start=True, stop=False)
                    for c in range(CH):
                        pe.matmul(o, uT[0:KC, c, t * TR:(t + 1) * TR], xT[0:KC, c, t * TR:(t + 1) * TR],
                                  start=False, stop=False)
                    for c in range(CH):
                        last = pe.matmul(o, xT[0:KC, c, t * TR:(t + 1) * TR], v3("w2v", CH)[0:KC, c, :],
                                         start=False, stop=(c == 1))
                    last.then_inc(tri_psum, 1)

                def transpose_p(t):
                    pe.wait_ge(tri_exp, t + 1)
                    need(pe, triT_ready, t - 1)
                    pe.transpose(ps[0:TR, (5, 2)[t % 2], 0:TR], prob[0:TR, t % 2, 0, :],
                                 V["ident"][0:TR, 0:TR]).then_inc(triT_psum, 1)

                def outputs(t):
                    pe.wait_ge(triT_ready, t + 1)
                    need(pe, h_added, TILES + t - 1)
                    pe.matmul(bank(t % 2, TR, 0, D), probT[0:TR, t % 2, 0, :], xhat[0:TR, t, 0:D],
                              start=True, stop=True).then_inc(trio_psum, 1)

                transpose_x(n, 0, 2)
                pe.wait_ge(packed["p_l1"], 16)
                scores(0)
                scores(1)
                transpose_x(n, 2, TILES)
                transpose_p(0)
                scores(2)
                for t in range(1, TILES):
                    transpose_p(t)
                    outputs(t - 1)
                    if t + 2 < TILES:
                        scores(t + 2)
                outputs(TILES - 1)

            def convolution(n):
                pe.wait_ge(packed["p_l3"], 16)
                ptw = v3("ptw", CH)
                transpose_x(n, 0, TILES)
                pe.wait_ge(pad_ready, CH * TILES)
                pe.wait_ge(folded, 1)
                for f in range(2):
                    a0, a1 = image_half(f)
                    for k in range(TAPS):
                        last = pe.matmul(bank(2 + f, KC, 0, a1 - a0), fold[0:KC, k, :],
                                         xpad[0:KC, 1, a0 // SEQ:a1 // SEQ, k:k + SEQ],
                                         start=(k == 0), stop=(k == TAPS - 1))
                    last.then_inc(pw_psum, 1)
                pe.wait_ge(dw_ready, 1)
                for f in range(2):
                    a0, a1 = image_half(f)
                    pe.matmul(bank(f, KC, 0, a1 - a0), v3("pww", CH)[0:KC, 0, :], dwc[0:KC, 0, a0:a1],
                              start=True, stop=True).then_inc(pw_psum, 1)

                def values(t):
                    pe.wait_ge(xT_ready, TILES * (n + 1))
                    need(pe, vt_ready, t - 1)
                    for c in range(CH):
                        k = KC + c
                        last = pe.matmul(bank(6 + t % 2, TR, 0, D), xT[0:k, c, t * TR:(t + 1) * TR],
                                         ptw[0:k, c, :], start=(c == 0), stop=(c == 1))
                    last.then_inc(vt_psum, 1)

                values(0)
                values(1)
                pe.wait_ge(ca_ready, 4)
                akw = v3("akw", CH)
                for t in range(TILES):
                    base = (t % 4) * TAPS * HEADS
                    o = ps[0:TR, 4 + t // 4, base:base + TAPS * HEADS].rearrange("p (k h) -> p k h", k=TAPS)
                    for c in range(CH):
                        last = pe.matmul(o[:, :, c * HPC:(c + 1) * HPC], ca[0:97, c, t * TR:(t + 1) * TR],
                                         akw[0:97, c, :], start=True, stop=True)
                last.then_inc(kern_psum, 1)
                for t in range(2, TILES):
                    values(t)
                sh = v3("shift", TAPS)
                by_tap = kexp[0:TR, :, :].rearrange("p t (k h) -> p k t h", k=TAPS)
                pe.wait_ge(kern_exp, 1)
                for k in range(TAPS):
                    b, j = (0, k) if k < TAPS_A else (1, k - TAPS_A)
                    last = pe.matmul(bank(b, TR, j * TILES * HEADS, (j + 1) * TILES * HEADS), sh[0:TR, TAPS - 1 - k, :],
                                     by_tap[:, k, :, :], start=True, stop=True)
                    if k in (TAPS_A - 1, TAPS - 1):
                        last.then_inc(moved_psum, 1)
                for t in range(TILES):
                    need(pe, conv_used, t - 1)
                    for k in range(TAPS):
                        if k == 0:
                            pe.wait_ge(prod_ready[0], t + 1)
                        if k == TAPS_A:
                            pe.wait_ge(prod_ready[1], t + 1)
                        last = pe.matmul(bank(2 + t % 2, TR, 0, D), sh[0:TR, k, :], prod[0:TR, t % 2, k, :],
                                         start=(k == 0), stop=(k == TAPS - 1))
                    last.then_inc(shift_psum, 1)

            def mixture(L, n):
                m = MOE[L]
                P, U, Bk, E = m["pairs"], m["units"], m["blocks"], m["routed"]
                gw = v3(f"gw{L}", CH)
                pe.wait_ge(packed[f"p_l{L}"], 16)
                def gate_logits():
                    src, depth = xm, (128, D - 128)
                    pe.wait_ge(xT_ready, TILES * (n + 1))
                    if L == 3:
                        wr1 = v3("wr1", CH)
                        for q in range(CH):
                            for f in range(2):
                                w = TPAD // 2 + f
                                a0 = f * (TPAD // 2)
                                for c in range(CH):
                                    last = pe.matmul(bank(2 + 2 * q + f, KC, 0, w), wr1[0:depth[c], c, q * KC:(q + 1) * KC],
                                                     xm[0:depth[c], c, a0:a0 + w], start=(c == 0), stop=(c == 1))
                                last.then_inc(r_psum, 1)
                        pe.wait_ge(r_ready, 4)
                        src, depth = rT, (KC, KC + 1)
                    for t in range(TILES):
                        for c in range(CH):
                            k = depth[c]
                            last = pe.matmul(bank(7, TR, t * 16, t * 16 + E), src[0:k, c, t * TR:(t + 1) * TR],
                                             gw[0:k, c, :], start=(c == 0), stop=(c == 1))
                    last.then_inc(gate_psum, 1)

                def hidden(e, b):
                    pe.wait_ge(w1_low, e * P + (m["q0"] + P))
                    for u in range(U):
                        j, f = u // 2, u % 2
                        first = isinstance(e, int) and e == 0
                        if first and u < 2:
                            pe.wait_ge(x_low, TILES * L + (FIRST, TILES)[f])
                        if not (isinstance(e, int) and m["u0"] + e * U + u < 2):
                            pe.wait_ge(a_used, e * U + (m["u0"] + u - 1))
                            pe.wait_ge(b_used, e * U + (m["u0"] + u - 1))
                        for ab in range(2):
                            col = (2 * j + ab) * 128
                            passes = ((W1h, 0, 128, xh[:, 0, :]), (W1h, 0, 128, xl[:, :]), (W1l, 0, 128, xh[:, 0, :]),
                                      (W1h, 1, 128, xh[:, 1, :]), (W1l, 1, 64, xh[:, 1, :]))
                            for q, (w, c, k, x) in enumerate(passes):
                                last = pe.matmul(bank(2 * f + ab, 128, 0, HALF), w[0:k, b, c, col:col + 128],
                                                 x[0:k, f * HALF:(f + 1) * HALF],
                                                 start=(q == 0), stop=(q == len(passes) - 1))
                        last.then_inc(hid_psum, 1)
                        if first and u == 0:
                            if L == 3:
                                pe.wait_ge(conv_used, TILES)
                            if L in (1, 3):
                                transpose_x(n, FIRST, TILES)
                            gate_logits()

                def down(e, b, loads):
                    pe.wait_ge(w2_loaded[b], loads * 16)
                    if m["kind"] == "swiglu":
                        pe.wait_ge(act_ready, (e + 1) * U + m["s0"])
                    else:
                        pe.wait_ge(a_used, (e + 1) * U + m["u0"])
                        pe.wait_ge(b_used, (e + 1) * U + m["u0"])
                    for k in range(3):
                        if not (isinstance(e, int) and e == 0):
                            pe.wait_ge(y_added, (e - 1) * 3 + (m["y0"] + k + 1))
                        for t in range(2 * k, min(2 * k + 2, TILES)):
                            r = rows(t)
                            for q in range(Bk):
                                last = pe.matmul(bank(4 + k, r, (t % 2) * D, (t % 2 + 1) * D),
                                                 act[:, b, q, t * TR:t * TR + r], W2[:, b, q, :],
                                                 start=(q == 0), stop=(q == Bk - 1))
                        last.then_inc(y_psum, 1)

                hidden(0, 1)
                hidden(1, 0)
                down(0, 1, m["w1"] + 1)
                hidden(2, 1)
                down(1, 0, m["w0"] + 1)
                with pe.Fori(1, m["loops"]) as i:
                    hidden(2 * i + 1, 0)
                    down(2 * i, 1, i + (m["w1"] + 1))
                    hidden(2 * i + 2, 1)
                    down(2 * i + 1, 0, i + (m["w0"] + 1))
                if m["tail"]:
                    hidden(m["n"] - 1, 0)
                    down(m["n"] - 2, 1, m["w1"] + m["n"] // 2)
                if m["bias"]:
                    G = m["n"]
                    at = sum(1 for x in MOE[:L] if x["bias"])
                    pe.wait_ge(cw_ready, L + 1)
                    for t in range(4):
                        last = pe.transpose(bank(7, G, t * TR, (t + 1) * TR), cw[0:TR, t, 0:G], V["ident"][0:TR, 0:TR])
                    last.then_inc(cwT_psum, 1)
                    pe.wait_ge(cwT_ready, 2 * at + 1)
                    pe.transpose(bank(7, G, 0, TR), cw[0:TR, 4, 0:G], V["ident"][0:TR, 0:TR]).then_inc(cwT_psum, 1)
                    pe.wait_ge(cwT_ready, 2 * at + 2)
                    pe.wait_ge(a_used, m["u0"] + m["n"] * U)
                    pe.wait_ge(b_used, m["u0"] + m["n"] * U)
                    for t in range(TILES):
                        last = pe.matmul(bank(t // 2, rows(t), (t % 2) * D, (t % 2 + 1) * D),
                                         cwT[0:G, t * TR:t * TR + rows(t)], V[f"b2_{L}"][0:G, :], start=True, stop=True)
                    last.then_inc(bias_psum, 1)
                e = m["n"] - 1
                down(e, (e + 1) % 2, m[f"w{(e + 1) % 2}"] + e // 2 + 1)

            tokens()
            pe.wait_ge(packed["p_l0"], 16)
            pe.wait_ge(filled, FILLS)
            attention(0, 0)
            mixture(0, 1)
            trilinear(2)
            transpose_x(3, 0, FIRST)
            mixture(1, 3)
            pe.wait_ge(packed["p_l2"], 16)
            attention(1, 4)
            mixture(2, 5)
            convolution(6)
            transpose_x(7, 0, FIRST)
            mixture(3, 7)

        @block.scalar
        def _(sc_):
            act_ = sc_.activation

            def take_tile(n, t, b):
                sc_.wait_ge(xT_psum, TILES * n + t + 1)
                src = ps[0:128 if n % 2 else KC, b, 0:CH * TR].rearrange("p (c r) -> p c r", c=CH)
                r = rows(t)
                a0 = t * TR
                if n == 5:
                    for c in range(CH):
                        scale = V["nscale"][:, c:c + 1]
                        act_(xh[:, c, a0:a0 + r], src[:, c, 0:r], ACT.Copy, scale=scale)
                        last = act_(xm[:, c, a0:a0 + TR], src[:, c, :], ACT.Copy, scale=scale)
                elif n % 2:
                    act_(xh[:, :, a0:a0 + r], src[:, :, 0:r], ACT.Copy)
                    last = act_(xm[:, :, a0:a0 + TR], src, ACT.Copy)
                else:
                    if n == 2:
                        for c in range(CH):
                            act_(uT[0:KC, c, a0:a0 + TR], src[:, c, :], ACT.Identity,
                                 scale=V["w3v"][0:KC, c:c + 1], bias=V["w1v"][0:KC, c:c + 1])
                    if n == 6:
                        for c in range(CH):
                            act_(xpad[0:KC, c, t * PER_TILE:(t + 1) * PER_TILE, PAD:PAD + SEQ],
                                 src[:, c, :].rearrange("p (i s) -> p i s", i=PER_TILE), ACT.Copy).then_inc(pad_ready, 1)
                    last = act_(xT[0:KC, :, a0:a0 + TR], src, ACT.Copy)
                last.then_inc(xT_ready, 1)

            def take_x(n):
                for t in range(TILES):
                    take_tile(n, t, x_bank(n, t))

            def fetch_exp():
                act_(spare[:, :], spare[:, :], ACT.Exp)

            def attention(a, n):
                g0 = TILES * a

                def take_qk(t):
                    sc_.wait_ge(qkT_psum, g0 + t + 1)
                    need(sc_, s_psum, 3 * (g0 + t - 1))
                    act_(qkT[0:KC, t % 2, :, :], ps[0:KC, 2, 0:2 * CH * TR].rearrange("p (c r) -> p c r", c=2 * CH),
                         ACT.Copy).then_inc(qkT_ready, 1)

                def take_v(t):
                    sc_.wait_ge(v_psum, g0 + t + 1)
                    need(sc_, o_psum, g0 + t - 1)
                    for c in range(CH):
                        w = HPC * (KC + HD)
                        v0 = ((t % 2) * HEADS + c * HPC) * KC
                        last = act_(vpad_all[0:TR, v0:v0 + w].rearrange("p (h d) -> p h d", h=HPC)[:, :, 0:HD],
                                    ps[0:TR, 1, c * KC:(c + 1) * KC].rearrange("p (h d) -> p h d", h=HPC), ACT.Copy)
                    last.then_inc(v_ready, 1)

                def exps(t, g):
                    sc_.wait_ge(smax_ready, 3 * (g0 + t) + g + 1)
                    need(sc_, pT_psum, 3 * (g0 + t - 1))
                    for i in range(4):
                        hh = 4 * g + i
                        last = act_(prob[0:TR, t % 2, hh, :], ps[0:TR, 3 + g, i * TR:(i + 1) * TR], ACT.Exp,
                                    bias=nbias[0:TR, t % 2, hh:hh + 1], scale=HD ** -0.5,
                                    accum_out=rowsum[0:TR, t % 2, hh:hh + 1])
                    last.then_inc(exp_ready, 1)

                def take_p(t):
                    need(sc_, o_psum, g0 + t - 1)
                    sc_.wait_ge(pT_psum, 3 * (g0 + t) + 1)
                    act_(probT[0:TR, t % 2, 0:4, :], ps[0:TR, 6, 0:4 * TR].rearrange("p (c r) -> p c r", c=4),
                         ACT.Copy).then_inc(pT0_ready, 1)

                take_qk(0)
                for s in range(TILES + 3):
                    if s == TILES:
                        first_splits(a * 2)
                    if s >= 3:
                        take_tile(n + 1, s - 3, 7)
                    if s == 0:
                        take_v(0)
                        take_qk(1)
                    if s < TILES:
                        exps(s, 0)
                    if 0 < s < TILES:
                        take_v(s)
                    if 0 <= s - 1 < TILES:
                        take_p(s - 1)
                    if s < TILES:
                        exps(s, 1)
                    if 0 < s < TILES - 1:
                        take_qk(s + 1)
                    if s < TILES:
                        exps(s, 2)

            def trilinear():
                for s in range(TILES + 1):
                    if s < TILES:
                        sc_.wait_ge(tri_max, s + 1)
                        need(sc_, triT_psum, s - 1)
                        act_(prob[0:TR, s % 2, 0, :], ps[0:TR, 4 - s % 2, 0:TR], ACT.Exp,
                             bias=nmax[0:TR, s:s + 1], accum_out=psumr[0:TR, s:s + 1]).then_inc(tri_exp, 1)
                    if s >= 1:
                        t = s - 1
                        sc_.wait_ge(triT_psum, t + 1)
                        need(sc_, trio_psum, t - 1)
                        act_(probT[0:TR, t % 2, 0, :], ps[0:TR, (5, 2)[t % 2], 0:TR], ACT.Copy).then_inc(triT_ready, 1)

            def convolution():
                for t in range(TILES):
                    sc_.wait_ge(vt_psum, t + 1)
                    act_(vtok[0:TR, t, :], ps[0:TR, 6 + t % 2, 0:D], ACT.Copy).then_inc(vt_ready, 1)
                sc_.wait_ge(kern_sub, 1)
                act_(kexp[0:TR, :, :], kexp[0:TR, :, :], ACT.Exp).then_inc(kern_exp, 1)
                for b, (k0, k1) in enumerate(((0, TAPS_A), (TAPS_A, TAPS))):
                    sc_.wait_ge(moved_psum, b + 1)
                    n = (k1 - k0) * TILES * HEADS
                    act_(moved[0:TR, k0:k1, :, :].rearrange("p k t h -> p (k t h)"), ps[0:TR, b, 0:n],
                         ACT.Copy).then_inc(moved_ready, 1)

            def split(L, e, b, j, loads):
                m = MOE[L]
                cols = slice(j * 256, (j + 1) * 256)
                sc_.wait_ge(w1_loaded[b], loads * 16)
                if isinstance(e, int) and e < 2:
                    need(sc_, hid_psum, m["u0"])
                else:
                    sc_.wait_ge(hid_psum, (e - 2) * m["units"] + (m["u0"] + 2 * j + 2))
                act_(W1h[:, b, :, cols], W1[:, b, :, cols], ACT.Copy).then_inc(w1_high, 1)

            def first_splits(L):
                for e in range(2):
                    for j in range(MOE[L]["pairs"]):
                        split(L, e, 1 - e, j, MOE[L][f"w{1 - e}"] + 1)

            def mixture(L):
                m = MOE[L]
                P, U, E = m["pairs"], m["units"], m["routed"]
                if L == 3:
                    for q in range(CH):
                        for f in range(2):
                            w = TPAD // 2 + f
                            a0 = f * (TPAD // 2)
                            sc_.wait_ge(r_psum, 2 * q + f + 1)
                            act_(rT[0:KC, q, a0:a0 + w], ps[0:KC, 2 + 2 * q + f, 0:w], ACT.Relu,
                                 bias=V["br1"][0:KC, q:q + 1]).then_inc(r_ready, 1)
                sc_.wait_ge(gate_in, L + 1)
                act_(sc[0:TR, :, 0:E], sc[0:TR, :, 0:E] if L != 1 else lg[0:TR, :, 0:E],
                     ACT.Sigmoid if L == 1 else ACT.Exp).then_inc(gate_out, 1)

                def units(e, b, loads, ahead=True):
                    if m["bias"] and m["kind"] != "swiglu":
                        sc_.wait_ge(biases_loaded[b], (loads + m[f"b{b}"]) * 16)
                    for u in range(U):
                        j, f = u // 2, u % 2
                        U0 = m["u0"] + u
                        if m["kind"] == "silu":
                            sc_.wait_ge(hid_psum, e * U + (U0 + 1))
                            if not (isinstance(e, int) and U0 + e * U < 2):
                                sc_.wait_ge(b_used, e * U + (U0 - 1))
                            bias = biases[:, b, 2 * j:2 * j + 1] if m["bias"] else 0.0
                            act_(gate[:, f, :], ps[:, 2 * f, 0:HALF], ACT.Silu, bias=bias).then_inc(a_used, 1)
                        elif m["kind"] == "relu":
                            sc_.wait_ge(hid_psum, e * U + (U0 + 1))
                            act_(act[:, b, 2 * j, f * HALF:(f + 1) * HALF], ps[:, 2 * f, 0:HALF], ACT.Relu,
                                 bias=biases[:, b, 2 * j:2 * j + 1]).then_inc(a_used, 1)
                        else:
                            sc_.wait_ge(a_used, e * U + (U0 + 1))
                            if not (isinstance(e, int) and u + e * U < 2):
                                sc_.wait_ge(glu_ready, e * U + (u - 1))
                            act_(gsig[:, f, :], gate[:, f, :], ACT.Sigmoid, scale=1.702).then_inc(sig_ready, 1)
                        if f and ahead:
                            split(L, e + 2, b, j, loads + (m[f"w{b}"] + 1))

                units(0, 1, 1)
                with sc_.Fori(0, m["loops"] - 1) as i:
                    units(2 * i + 1, 0, i + 1)
                    units(2 * i + 2, 1, i + 2)
                i = m["loops"] - 1
                units(2 * i + 1, 0, i + 1, ahead=m["tail"])
                units(2 * i + 2, 1, i + 2, ahead=False)
                if m["tail"]:
                    units(m["n"] - 1, 0, m["n"] // 2, ahead=False)
                if m["bias"]:
                    G = m["n"]
                    at = sum(1 for x in MOE[:L] if x["bias"])
                    sc_.wait_ge(cwT_psum, 2 * at + 1)
                    act_(cwT[0:G, 0:4 * TR], ps[0:G, 7, 0:4 * TR], ACT.Copy).then_inc(cwT_ready, 1)
                    sc_.wait_ge(cwT_psum, 2 * at + 2)
                    act_(cwT[0:G, 4 * TR:5 * TR], ps[0:G, 7, 0:TR], ACT.Copy).then_inc(cwT_ready, 1)

            take_x(0)
            attention(0, 0)
            mixture(0)
            sc_.wait_ge(packed["p_l1"], 16)
            sc_.wait_ge(filled, FILLS)
            fetch_exp()
            take_x(2)
            trilinear()
            first_splits(1)
            take_x(3)
            mixture(1)
            fetch_exp()
            take_x(4)
            attention(1, 4)
            mixture(2)
            fetch_exp()
            take_x(6)
            first_splits(3)
            convolution()
            take_x(7)
            mixture(3)

        @block.gpsimd
        def _(pool):
            pool.memset(vpad_all[:, :], 0.0).then_inc(filled, 1)
            pool.memset(xpad[:, :, :, :], 0.0).then_inc(filled, 1)

            def attention(a):
                g0 = TILES * a

                def mask_keys(t):
                    pool.wait_ge(qkT_ready, g0 + t + 1)
                    pool.tensor_tensor(kmask[0:KC, t % 2, HPC:, :],
                                       qkT[0:KC, t % 2, CH + 1, :].unsqueeze(1).broadcast_to([KC, HPC, TR]),
                                       V["hmask"][0:KC, :].unsqueeze(2).broadcast_to([KC, HPC, TR]),
                                       ALU.mult).then_inc(kmask_ready[1], 1)

                def normalise(t):
                    pool.wait_ge(rowsum_ready, g0 + t + 1)
                    p = prob[0:TR, t % 2, :, :]
                    pool.tensor_tensor(p, p, rowsum[0:TR, t % 2, :].unsqueeze(2).broadcast_to([TR, HEADS, TR]),
                                       ALU.mult).then_inc(prob_ready, 1)

                mask_keys(0)
                for t in range(TILES):
                    if t + 1 < TILES:
                        mask_keys(t + 1)
                    normalise(t)

            def convolution():
                for t in range(TILES):
                    if t == 0:
                        pool.wait_ge(vt_ready, TILES)
                        pool.wait_ge(moved_ready, 2)
                    need(pool, shift_psum, t - 1)
                    weigh(pool, t, 1)

            def split(L, e, b, j):
                m = MOE[L]
                cols = slice(j * 256, (j + 1) * 256)
                pool.wait_ge(w1_high, e * m["pairs"] + (m["q0"] + j + 1))
                pool.tensor_tensor(W1l[:, b, :, cols], W1[:, b, :, cols],
                                   W1h[:, b, :, cols].bitcast(F32), ALU.subtract).then_inc(w1_low, 1)

            def first_splits(L):
                for e in range(2):
                    for j in range(MOE[L]["pairs"]):
                        split(L, e, 1 - e, j)

            def mixture(L):
                m = MOE[L]
                P, U = m["pairs"], m["units"]

                def units(e, b, ahead=True):
                    for u in range(U):
                        j, f = u // 2, u % 2
                        if m["kind"] == "swiglu":
                            pool.wait_ge(sig_ready, e * U + (u + 1))
                            pool.tensor_tensor(gsig[:, f, :], gate[:, f, :], gsig[:, f, :],
                                               ALU.mult).then_inc(glu_ready, 1)
                        if f and ahead:
                            split(L, e + 2, b, j)

                units(0, 1)
                with pool.Fori(0, m["loops"] - 1) as i:
                    units(2 * i + 1, 0)
                    units(2 * i + 2, 1)
                i = m["loops"] - 1
                units(2 * i + 1, 0, ahead=m["tail"])
                units(2 * i + 2, 1, ahead=False)
                if m["tail"]:
                    units(m["n"] - 1, 0, ahead=False)

            pool.wait_ge(packed["p_l0"], 16)
            pool.tensor_copy(maskA[:, :], V["same_q"]).then_inc(masks_in, 1)
            pool.tensor_copy(maskB[:, :], V["same_k"]).then_inc(masks_in, 1)
            attention(0)
            first_splits(0)
            mixture(0)
            first_splits(1)
            mixture(1)
            attention(1)
            first_splits(2)
            mixture(2)
            pool.wait_ge(packed["p_l3"], 16)
            pool.tensor_tensor(fold[0:KC, :, :], v3("pww", CH)[0:KC, 1, :].unsqueeze(1).broadcast_to([KC, TAPS, KC]),
                               v3("dww", CH)[0:KC, 1, :].unsqueeze(2).broadcast_to([KC, TAPS, KC]),
                               ALU.mult).then_inc(folded, 1)
            first_splits(3)
            convolution()
            mixture(3)

        @block.vector
        def _(dve):
            steps = [0]

            def link(ins):
                steps[0] += 1
                ins.then_inc(vec, 1)
                dve.wait_ge(vec, steps[0])

            tt, ts, stt = dve.tensor_tensor, dve.tensor_scalar, dve.scalar_tensor_tensor

            def rsqrt(dst, x, t0, t1):
                y, a = nt[0:TR, 0, t0:t1], nt[0:TR, 1, t0:t1]
                link(ts(nti[0:TR, t0:t1], x.bitcast(I32), 1, None, ALU.logical_shift_right))
                link(ts(y.bitcast(I32), nti[0:TR, t0:t1], -1.0, float(0x5F3759DF + 2 ** 30 - 2 ** 22), ALU.mult, ALU.add))
                for k in range(3):
                    if t1 - t0 == 1:
                        link(stt(out=a, in0=y, scalar=x, in1=y, op0=ALU.mult, op1=ALU.mult))
                    else:
                        link(tt(a, y, y, ALU.mult))
                        link(tt(a, a, x, ALU.mult))
                    link(stt(out=dst if k == 2 else y, in0=a, scalar=1.5, in1=y, op0=ALU.add, op1=ALU.mult))

            def statistics(t0, t1):
                for t in range(t0, t1):
                    last = dve.bn_stats(st[0:TR, t, :], h[0:TR, t, :])
                link(last)
                for t in range(t0, t1):
                    dve.bn_aggr(mv[0:TR, t, :], st[0:TR, t, :]).then_inc(vec, 1)
                    steps[0] += 1

            def low_tokens(L, t0, t1):
                for t in range(t0, t1):
                    dve.wait_ge(xT_ready, TILES * (2 * L + 1) + t + 1)
                    a0, a1 = t * TR, t * TR + rows(t)
                    tt(xl[:, a0:a1], xm[:, 0, a0:a1], xh[:, 0, a0:a1].bitcast(F32), ALU.subtract)
                    low = xh[64:128, 1, a0:a1]
                    tt(low, xm[64:128, 1, a0:a1], low.bitcast(F32), ALU.subtract).then_inc(x_low, 1)

            def normalise(dst, t, rstd, twice):
                mean = mv[0:TR, t, 0:1]
                if not twice:
                    return ts(dst[0:TR, t, 0:D], h[0:TR, t, :], mean, rstd, ALU.subtract, ALU.mult)
                ts(dst[0:TR, t, 0:128], h[0:TR, t, 0:128], mean, rstd, ALU.subtract, ALU.mult)
                w = D - 128
                return ts(dst[0:TR, t, 128:256].rearrange("p (a w) -> p a w", a=2),
                          h[0:TR, t, 128:D].unsqueeze(1).broadcast_to([TR, 2, w]), mean, rstd, ALU.subtract, ALU.mult)

            def layernorm(n, t0, t1):
                dve.wait_ge(vec, steps[0])
                x, rstd = nt[0:TR, 2, t0:t1], nt[0:TR, 3, t0:t1]
                if n == 5:
                    x, rstd = nt[0:TR, 2, 0:2], nt[0:TR, 3, 0:2]
                    ts(x[:, 0:1], mv[0:TR, t0:t1, 1], EPS, -0.5, ALU.add, ALU.mult)
                    link(ts(x[:, 1:2], mv[0:TR, t0:t1, 1], -0.5 * (1 + EPS), -0.5 * EPS * EPS, ALU.mult, ALU.add))
                    rsqrt(rstd, x, 0, 2)
                    normalise(xrms, t0, rstd[:, 1:2], True).then_inc(ln_ready, 1)
                    link(ts(xhat[0:TR, t0, 0:D], h[0:TR, t0, :], mv[0:TR, t0, 0:1], rstd[:, 0:1],
                            ALU.subtract, ALU.mult))
                    link(tt(h[0:TR, t0, :], h[0:TR, t0, :], xhat[0:TR, t0, 0:D], ALU.add))
                    return
                link(ts(x, mv[0:TR, t0:t1, 1], EPS, -0.5, ALU.add, ALU.mult))
                rsqrt(rstd, x, t0, t1)
                for t in range(t0, t1):
                    normalise(xhat, t, rstd[:, t - t0:t - t0 + 1], n % 2).then_inc(ln_ready, 1)

            def attention(a, n):
                g0 = TILES * a
                cos = V[f"cos{a}"][0:TR, :].unsqueeze(1).broadcast_to([TR, 2 * HEADS, HD])
                sin = V[f"sin{a}"][0:TR, :]

                def rotate(t):
                    src = ps[0:TR, 0, 0:2 * D].rearrange("p (g d) -> p g d", d=HD)
                    r0 = rope[0:TR, 0, :].rearrange("p (g d) -> p g d", d=HD)
                    r1 = rope[0:TR, 1, :].rearrange("p (g d) -> p g d", d=HD)
                    dve.wait_ge(qk_psum, g0 + t + 1)
                    tt(r0, src, cos, ALU.mult)
                    for f in range(2):
                        w = HD // 2
                        last = tt(r1[:, :, f * w:(f + 1) * w], src[:, :, (1 - f) * w:(2 - f) * w],
                                  sin[:, f * w:(f + 1) * w].unsqueeze(1).broadcast_to([TR, 2 * HEADS, w]), ALU.mult)
                    last.then_inc(rope_used, 1)
                    dve.wait_ge(rope_used, g0 + t + 1)
                    need(dve, qkT_psum, g0 + t - 1)
                    tt(qk[0:TR, t % 2, :], rope[0:TR, 0, :], rope[0:TR, 1, :], ALU.add).then_inc(rope_ready, 1)
                    dve.wait_ge(rope_ready, g0 + t + 1)

                def mask_keys(t):
                    dve.wait_ge(qkT_ready, g0 + t + 1)
                    tt(kmask[0:KC, t % 2, 0:HPC, :],
                       qkT[0:KC, t % 2, CH, :].unsqueeze(1).broadcast_to([KC, HPC, TR]),
                       V["hmask"][0:KC, :].unsqueeze(2).broadcast_to([KC, HPC, TR]), ALU.mult).then_inc(kmask_ready[0], 1)

                def maxima(t):
                    for g in range(4):
                        if g < 3:
                            dve.wait_ge(s_psum, 3 * (g0 + t) + g + 1)
                            dve.tensor_reduce(smax[0:TR, 4 * g:4 * g + 4],
                                              ps[0:TR, 3 + g, 0:4 * TR].rearrange("p (i k) -> p i k", i=4),
                                              AX, ALU.max).then_inc(vec, 1)
                            steps[0] += 1
                        if g >= 1:
                            dve.wait_ge(vec, steps[0] - (g < 3))
                            ts(nbias[0:TR, t % 2, 4 * g - 4:4 * g], smax[0:TR, 4 * g - 4:4 * g], -HD ** -0.5, None,
                               ALU.mult).then_inc(smax_ready, 1)

                def invert_sums(t):
                    dve.wait_ge(exp_ready, 3 * (g0 + t + 1))
                    dve.reciprocal(rowsum[0:TR, t % 2, :], rowsum[0:TR, t % 2, :]).then_inc(rowsum_ready, 1)

                def take_p(t):
                    need(dve, o_psum, g0 + t - 1)
                    for g in (1, 2):
                        dve.wait_ge(pT_psum, 3 * (g0 + t) + g + 1)
                        dve.tensor_copy(probT[0:TR, t % 2, 4 * g:4 * g + 4, :],
                                        ps[0:TR, 6 + g % 2, 0:4 * TR].rearrange("p (c r) -> p c r", c=4)).then_inc(pT_ready, 1)

                def take_o(t):
                    dve.wait_ge(o_psum, g0 + t + 1)
                    need(dve, proj_psum, g0 + t)
                    dve.tensor_copy(oT[0:KC, :, :],
                                    ps[0:KC, 1, 0:CH * TR].rearrange("p (c r) -> p c r", c=CH)).then_inc(o_ready, 1)

                def add(t):
                    dve.wait_ge(proj_psum, g0 + t + 1)
                    tt(h[0:TR, t, :], ps[0:TR, 2, 0:D], h[0:TR, t, :], ALU.add).then_inc(h_added, 1)

                layernorm(n, 2, TILES)
                rotate(0)
                mask_keys(0)
                rotate(1)
                for s in range(TILES + 3):
                    if s < TILES:
                        maxima(s)
                    if 0 <= s - 2 < TILES:
                        add(s - 2)
                    if 0 < s < TILES - 1:
                        rotate(s + 1)
                    if 0 <= s - 1 < TILES:
                        take_p(s - 1)
                    if s + 1 < TILES:
                        mask_keys(s + 1)
                    if 0 <= s - 2 < TILES:
                        dve.wait_ge(h_added, 2 * TILES * a + s - 1)
                        statistics(s - 2, s - 1)
                        layernorm(n + 1, s - 2, s - 1)
                    if s >= 3:
                        low_tokens(2 * a, s - 3, s - 2)
                    if s < TILES:
                        invert_sums(s)
                    if 0 <= s - 1 < TILES:
                        take_o(s - 1)

            def trilinear():
                def add(t):
                    dve.wait_ge(trio_psum, t + 1)
                    link(dve.reciprocal(rsum[0:TR, t:t + 1], psumr[0:TR, t:t + 1]))
                    stt(out=h[0:TR, t, :], in0=ps[0:TR, t % 2, 0:D], scalar=rsum[0:TR, t:t + 1],
                        in1=h[0:TR, t, :], op0=ALU.mult, op1=ALU.add).then_inc(h_added, 1)
                    dve.wait_ge(h_added, TILES + t + 1)

                for s in range(TILES + 2):
                    if s < TILES:
                        dve.wait_ge(tri_psum, s + 1)
                        dve.tensor_reduce(nmax[0:TR, s:s + 1], ps[0:TR, 4 - s % 2, 0:TR], AX, ALU.max,
                                          negate=True).then_inc(tri_max, 1)
                    if s >= 2:
                        add(s - 2)
                        statistics(s - 2, s - 1)
                    if s - 2 == FIRST - 1:
                        layernorm(3, 0, FIRST)
                low_tokens(1, 0, FIRST)
                layernorm(3, FIRST, TILES)
                low_tokens(1, FIRST, TILES)

            def convolution():
                dve.wait_ge(pad_ready, CH * TILES)
                dst = dwc[0:KC, 0, :].rearrange("p (i s) -> p i s", s=SEQ)
                w = v3("dww", CH)[0:KC, 0, :]
                link(ts(dst, xpad[0:KC, 0, :, 0:SEQ], w[:, 0:1], None, ALU.mult))
                for k in range(1, TAPS):
                    ins = stt(out=dst, in0=xpad[0:KC, 0, :, k:k + SEQ], scalar=w[:, k:k + 1], in1=dst,
                              op0=ALU.mult, op1=ALU.add)
                    if k < TAPS - 1:
                        link(ins)
                ins.then_inc(dw_ready, 1)
                dve.wait_ge(xT_ready, 7 * TILES)
                for i, (c, f) in enumerate(((1, 0), (1, 1), (0, 0), (0, 1))):
                    a0, a1 = image_half(f)
                    dve.wait_ge(pw_psum, i + 1)
                    stt(out=ca[0:KC, c, a0:a1], in0=ps[0:KC, 2 * c + f, 0:a1 - a0], scalar=V["pwb"][0:KC, c:c + 1],
                        in1=xT[0:KC, c, a0:a1], op0=ALU.add, op1=ALU.mult).then_inc(ca_ready, 1)
                dve.wait_ge(kern_psum, 1)

                def logits(t):
                    base = (t % 4) * TAPS * HEADS
                    return ps[0:TR, 4 + t // 4, base:base + TAPS * HEADS]

                for t in range(TILES):
                    last = dve.tensor_reduce(kmx[0:TR, t, :], logits(t).rearrange("p (k h) -> p h k", k=TAPS), AX, ALU.max)
                link(last)
                for t in range(TILES):
                    last = tt(kexp[0:TR, t, :].rearrange("p (k h) -> p k h", k=TAPS),
                              logits(t).rearrange("p (k h) -> p k h", k=TAPS),
                              kmx[0:TR, t, :].unsqueeze(1).broadcast_to([TR, TAPS, HEADS]), ALU.subtract)
                last.then_inc(kern_sub, 1)
                dve.wait_ge(kern_exp, 1)
                for t in range(TILES):
                    last = dve.tensor_reduce(kmx[0:TR, t, :], kexp[0:TR, t, :].rearrange("p (k h) -> p h k", k=TAPS),
                                             AX, ALU.add)
                link(last)
                link(dve.reciprocal(rtap[0:TR, :, :], kmx[0:TR, :, :]))

                def add(t):
                    dve.wait_ge(shift_psum, t + 1)
                    tt(conv[0:TR, :].rearrange("p (h d) -> p h d", d=HD),
                       ps[0:TR, 2 + t % 2, 0:D].rearrange("p (h d) -> p h d", d=HD),
                       rtap[0:TR, t, :].unsqueeze(2).broadcast_to([TR, HEADS, HD]), ALU.mult).then_inc(conv_used, 1)
                    dve.wait_ge(conv_used, t + 1)
                    link(tt(h[0:TR, t, :], h[0:TR, t, :], conv[0:TR, :], ALU.add))
                    statistics(t, t + 1)

                for s in range(TILES + 1):
                    if s < TILES:
                        if s == 0:
                            dve.wait_ge(vt_ready, TILES)
                            dve.wait_ge(moved_ready, 1)
                        need(dve, shift_psum, s - 1)
                        weigh(dve, s, 0)
                    if s == TILES - 1:
                        layernorm(7, 0, FIRST)
                    if s >= 1:
                        add(s - 1)
                low_tokens(3, 0, FIRST)
                layernorm(7, FIRST, TILES)
                low_tokens(3, FIRST, TILES)

            def choose(s, N, top, dst):
                Z = 8 - top
                field = chosen[0:TR, :, 0:N + Z]
                dve.tensor_copy(field[:, :, 0:N], s)
                link(dve.memset(field[:, :, N:], NEVER))
                for t in range(TILES):
                    last = dve.max(largest[0:TR, t, :], field[:, t, :])
                link(last)
                link(dve.memset(largest[0:TR, :, top:8], NEVER))
                for t in range(TILES):
                    last = dve.match_replace(field[:, t, :], largest[0:TR, t, :], field[:, t, :], MARK)
                link(last)
                link(ts(dst, field[:, :, 0:N], MARK, None, ALU.is_equal))

            def wide(x, N):
                return x.unsqueeze(2).broadcast_to([TR, TILES, N])

            def gating(L, meanwhile):
                m = MOE[L]
                E = m["routed"]
                c0 = m["shared"]
                dve.wait_ge(gate_psum, L + 1)
                l, s, r, p = lg[0:TR, :, 0:E], sc[0:TR, :, 0:E], sr[0:TR, :, 0:E], pick[0:TR, :, 0:E]
                mx, sm = s5[0:TR, 0, :], s5[0:TR, 1, :]
                logits = ps[0:TR, 7, 0:16 * TILES].rearrange("p (t e) -> p t e", e=16)[:, :, 0:E]
                if L in (0, 2):
                    ins = tt(l, logits, V[f"gwb{L}"][0:TR, :].unsqueeze(1).broadcast_to([TR, TILES, E]), ALU.add)
                else:
                    ins = dve.tensor_copy(l, logits)
                if L == 1:
                    ins.then_inc(gate_in, 1)
                else:
                    link(ins)
                    link(dve.tensor_reduce(mx, l, AX, ALU.max))
                    tt(s, l, wide(mx, E), ALU.subtract).then_inc(gate_in, 1)
                meanwhile()
                if L >= 2:
                    choose(l, E, m["top"], p)
                    dve.wait_ge(gate_out, L + 1)
                    link(tt(r, s, p, ALU.mult))
                    link(dve.tensor_reduce(sm, r, AX, ALU.add))
                    link(dve.reciprocal(sm, sm))
                    tt(cw[0:TR, :, 0:E], r, wide(sm, E), ALU.mult).then_inc(cw_ready, 1)
                    dve.wait_ge(cw_ready, L + 1)
                    return
                dve.wait_ge(gate_out, L + 1)
                if L == 0:
                    link(dve.tensor_reduce(sm, s, AX, ALU.add))
                    link(dve.reciprocal(sm, sm))
                    link(tt(s, s, wide(sm, E), ALU.mult))
                link(tt(r, s, V[f"gb{L}"][0:TR, :].unsqueeze(1).broadcast_to([TR, TILES, E]), ALU.add))
                G = m["groups"]
                gs, gp = gsum[0:TR, :, 0:G], gpick[0:TR, :, 0:G]
                link(tt(gs, r[:, :, 0::2], r[:, :, 1::2], ALU.add))
                choose(gs, G, m["top_groups"], gp)
                for f in range(2):
                    last = tt(r[:, :, f::2], r[:, :, f::2], gp, ALU.mult)
                link(last)
                link(ts(gs, gp, 1e30, -1e30, ALU.mult, ALU.add))
                for f in range(2):
                    last = tt(r[:, :, f::2], r[:, :, f::2], gs, ALU.add)
                link(last)
                choose(r, E, m["top"], p)
                out_ = cw[0:TR, :, c0:c0 + E]
                if L == 0:
                    stt(out=out_, in0=p, scalar=2.5, in1=s, op0=ALU.mult, op1=ALU.mult).then_inc(cw_ready, 1)
                else:
                    link(tt(r, s, p, ALU.mult))
                    link(dve.tensor_reduce(sm, r, AX, ALU.add))
                    link(ts(sm, sm, 1e-6, None, ALU.add))
                    link(dve.reciprocal(sm, sm))
                    tt(out_, r, wide(sm, E), ALU.mult).then_inc(cw_ready, 1)
                dve.wait_ge(cw_ready, L + 1)

            def mixture(L):
                m = MOE[L]
                P, U = m["pairs"], m["units"]
                if m["shared"]:
                    link(dve.memset(cw[:, :, 0:1], 1.0))

                def units(e, b, loads):
                    if m["bias"]:
                        dve.wait_ge(biases_loaded[b], (loads + m[f"b{b}"]) * 16)
                    if m["kind"] == "swiglu":
                        ts(lin_bias[:, b, :], biases[:, b, 1::2], 1.0, None, ALU.add).then_inc(lin_bias_ready, 1)
                        dve.wait_ge(lin_bias_ready, e + 1)

                    def last_factor(u):
                        j, f = u // 2, u % 2
                        dve.wait_ge(glu_ready, e * U + (u + 1))
                        stt(out=act[:, b, j, f * HALF:(f + 1) * HALF], in0=lin[:, f, :], scalar=-6.0,
                            in1=gsig[:, f, :], op0=ALU.max, op1=ALU.mult).then_inc(act_ready, 1)

                    for u in range(U):
                        j, f = u // 2, u % 2
                        U0 = m["u0"] + u
                        if m["kind"] == "silu":
                            dve.wait_ge(a_used, e * U + (U0 + 1))
                            bias = biases[:, b, 2 * j + 1:2 * j + 2] if m["bias"] else 0.0
                            stt(out=act[:, b, j, f * HALF:(f + 1) * HALF], in0=ps[:, 2 * f + 1, 0:HALF], scalar=bias,
                                in1=gate[:, f, :], op0=ALU.add, op1=ALU.mult).then_inc(b_used, 1)
                        elif m["kind"] == "relu":
                            dve.wait_ge(hid_psum, e * U + (U0 + 1))
                            ts(act[:, b, 2 * j + 1, f * HALF:(f + 1) * HALF], ps[:, 2 * f + 1, 0:HALF],
                               biases[:, b, 2 * j + 1:2 * j + 2], 0.0, ALU.add, ALU.max).then_inc(b_used, 1)
                        else:
                            if u >= 2:
                                dve.wait_ge(act_ready, e * U + (u - 1))
                            elif not (isinstance(e, int) and e == 0):
                                dve.wait_ge(act_ready, e * U + (u - 1))
                            dve.wait_ge(hid_psum, e * U + (U0 + 1))
                            ts(gate[:, f, :], ps[:, 2 * f, 0:HALF], biases[:, b, 2 * j:2 * j + 1], 7.0,
                               ALU.add, ALU.min).then_inc(a_used, 1)
                            ts(lin[:, f, :], ps[:, 2 * f + 1, 0:HALF], lin_bias[:, b, j:j + 1], 8.0,
                               ALU.add, ALU.min).then_inc(b_used, 1)
                            if u >= 1:
                                dve.wait_ge(b_used, e * U + U0)
                                last_factor(u - 1)
                    if m["kind"] == "swiglu":
                        dve.wait_ge(b_used, e * U + (m["u0"] + U))
                        last_factor(U - 1)

                def add(e, first=False, final=False):
                    for k in range(3):
                        if not first:
                            dve.wait_ge(y_added, e * 3 + (m["y0"] + k - 2))
                        if final and m["bias"]:
                            for t in range(2 * k, min(2 * k + 2, TILES)):
                                r = rows(t)
                                last = tt(h[0:r, t, :], ps[0:r, k, (t % 2) * D:(t % 2 + 1) * D], h[0:r, t, :], ALU.add)
                            link(last)
                        dve.wait_ge(y_psum, e * 3 + (m["y0"] + k + 1))
                        for t in range(2 * k, min(2 * k + 2, TILES)):
                            r = rows(t)
                            last = stt(out=h[0:r, t, :], in0=ps[0:r, 4 + k, (t % 2) * D:(t % 2 + 1) * D],
                                       scalar=cw[0:r, t, bass.ds(e, 1)], in1=h[0:r, t, :], op0=ALU.mult, op1=ALU.add)
                        last.then_inc(y_added, 1)
                        if final and L < 2 and k == 0:
                            dve.wait_ge(y_added, e * 3 + (m["y0"] + 1))
                            statistics(0, 2)
                            layernorm(2 * L + 2, 0, 2)
                    if final and L < 3:
                        dve.wait_ge(y_added, e * 3 + (m["y0"] + 3))
                        statistics(2 if L < 2 else 0, TILES)

                long = m["blocks"] > 1
                gating(L, lambda: (units(0, 1, 1), units(1, 0, 1) if long else None))
                if not long:
                    units(1, 0, 1)
                add(0, True)
                units(2, 1, 2)
                add(1)
                with dve.Fori(1, m["loops"]) as i:
                    units(2 * i + 1, 0, i + 1)
                    add(2 * i)
                    units(2 * i + 2, 1, i + 2)
                    add(2 * i + 1)
                n = m["n"]
                if m["tail"]:
                    units(n - 1, 0, n // 2)
                    add(n - 2)
                if m["bias"]:
                    dve.wait_ge(bias_psum, 1 + sum(1 for x in MOE[:L] if x["bias"]))
                add(n - 1, final=True)
                dve.wait_ge(y_added, m["y0"] + 3 * n)

            dve.memset(spare[:, :], 0.0).then_inc(filled, 1)
            dve.memset(xT[96:97, :, :], 1.0).then_inc(filled, 1)
            dve.memset(oT[96:97, :, :], 1.0).then_inc(filled, 1)
            dve.memset(rT[96:97, :, :], 1.0).then_inc(filled, 1)
            link(dve.memset(ca[96:97, :, :], 1.0))
            for t0, t1 in ((0, 2), (2, TILES)):
                for t in range(t0, t1):
                    dve.wait_ge(tok_psum, t + 1)
                    last = dve.tensor_copy(h[0:TR, t, :], ps[0:TR, t, 0:D])
                link(last)
                statistics(t0, t1)
                if t0 == 0:
                    layernorm(0, 0, 2)
            dve.wait_ge(packed["p_l0"], 16)
            attention(0, 0)
            mixture(0)
            layernorm(2, 2, TILES)
            dve.wait_ge(packed["p_l1"], 16)
            trilinear()
            mixture(1)
            dve.wait_ge(packed["p_l2"], 16)
            attention(1, 4)
            mixture(2)
            layernorm(6, 0, TILES)
            dve.wait_ge(packed["p_l3"], 16)
            convolution()
            mixture(3)


def chunks(w, bias=None):
    n = w.shape[1]
    o = np.zeros((97, CH, n), w.dtype)
    o[0:KC] = w.reshape(CH, KC, n).transpose(1, 0, 2)
    if bias is not None:
        o[KC, CH - 1] = bias
    return o.reshape(97, CH * n)


def mixed(w):
    return np.stack([w[0:128], np.concatenate([w[128:D], w[128:D]])], 1)


def rope_table(inv):
    pos = (np.arange(128) % SEQ).astype(np.float32)
    ang = (pos[:, None] * inv[None, :].astype(np.float32)).astype(np.float32)
    cos, sin = np.cos(ang).astype(np.float32), np.sin(ang).astype(np.float32)
    return np.concatenate([cos, cos], 1), np.concatenate([-sin, sin], 1)


def layout(I):
    f = np.float32
    S = {}
    x = I["x"].reshape(IMAGES, 3, 4, 16, 4, 16).transpose(1, 3, 5, 0, 2, 4).reshape(768, IMAGES, PATCHES)
    pt = np.zeros((768, TILES * PER_TILE, SEQ), f)
    pt[:, :IMAGES, 1:] = x
    w = I["L0_tok_W"].reshape(D, 16, 16, 3).transpose(3, 1, 2, 0).reshape(IN_CH, 128, D)
    patches = np.ascontiguousarray(np.concatenate([w, pt.reshape(IN_CH, 128, TPAD)], 2).transpose(1, 0, 2))
    ind = np.zeros((128, TILES * PER_TILE, SEQ), f)
    ind[0, :IMAGES, 1:] = 1
    ind[1, :IMAGES, 0] = 1
    S["ind"] = ind.reshape(128, TPAD)
    S["tokb"] = np.zeros((128, D), f)
    S["tokb"][0] = I["L0_tok_b"]
    S["tokb"][1] = I["cls_tok"].reshape(D)
    S["ident"] = np.eye(128, dtype=f)

    S["wqkv0"] = chunks(np.concatenate([I["L0_attn_wq"].T, I["L0_attn_wk"].T, I["L0_attn_wv"].T], 1),
                        np.concatenate([I["L0_attn_bq"], I["L0_attn_bk"], I["L0_attn_bv"]]))
    S["wo0"] = chunks(I["L0_attn_wo"].T, I["L0_attn_bo"])
    frac = 2.0 * np.arange(4, dtype=f) / HD
    inv0 = np.concatenate([1.0 / (f(10000.0) ** frac), np.zeros(4, f)]).astype(f)
    S["cos0"], S["sin0"] = rope_table(inv0)
    S["hmask"] = np.repeat(np.eye(HPC, dtype=f), HD, 0)
    S["gw0"] = mixed(I["L0_ffn_gate_w"]).reshape(128, CH * 16)
    S["gwb0"] = np.broadcast_to(I["L0_ffn_gate_b"], (128, 16))
    S["gb0"] = np.broadcast_to(I["L0_ffn_bias"], (128, 16))
    S["b2_0"] = np.concatenate([I["L0_ffn_sbd"][None], I["L0_ffn_bd"]])

    for i, name in enumerate(["w1v", "w2v", "w3v"]):
        S[name] = I["L1_attn_w"][0, i * D:(i + 1) * D].reshape(CH, KC).T
    S["w2v"] = np.repeat(S["w2v"], TR, 1)
    S["gw1"] = mixed(I["L1_ffn_gate_weight"].T).reshape(128, CH * 8)
    S["gb1"] = np.broadcast_to(I["L1_ffn_gate_bias"], (128, 8))

    S["wqkv1"] = chunks(I["L2_attn_w_qkv"].T, I["L2_attn_b_qkv"])
    S["wo1"] = chunks(I["L2_attn_w_proj"].T, I["L2_attn_b_proj"])
    inv1 = (1.0 / f(10000.0) ** (np.arange(0, HD, 2, dtype=f) / HD)).astype(f)
    S["cos1"], S["sin1"] = rope_table(inv1)
    S["nscale"] = mixed(I["L2_ffn_norm_scale"])
    S["gw2"] = mixed(I["L2_ffn_gate_w"].T).reshape(128, CH * 16)
    S["gwb2"] = np.broadcast_to(I["L2_ffn_gate_b"], (128, 16))
    S["b2_2"] = I["L2_ffn_mlp2_b"]

    S["dww"] = I["L3_attn_dw_w"].reshape(CH, KC, TAPS).transpose(1, 0, 2).reshape(KC, CH * TAPS)
    pw = np.zeros((KC, CH, KC), f)
    ak = np.zeros((97, CH, TAPS, HPC), f)
    for c in range(CH):
        for i in range(HPC):
            hh = c * HPC + i
            pw[i * HD:(i + 1) * HD, c, i * HD:(i + 1) * HD] = I["L3_attn_pw_w"][hh].T
            ak[i * HD:(i + 1) * HD, c, :, i] = I["L3_attn_ak_w"][hh].T
            ak[KC, c, :, i] = I["L3_attn_ak_b"].reshape(HEADS, TAPS)[hh]
    S["pww"] = pw.reshape(KC, CH * KC)
    S["akw"] = ak.reshape(97, CH * TAPS * HPC)
    S["pwb"] = I["L3_attn_pw_b"].reshape(CH, KC).T
    S["ptw"] = chunks(I["L3_attn_pt_w"].T, I["L3_attn_pt_b"])
    l = np.arange(TR)
    sh = np.stack([(l[:, None] == l[None, :] + k - PAD) & (l[:, None] // SEQ == l[None, :] // SEQ)
                   for k in range(TAPS)], 1)
    S["shift"] = sh.astype(f).reshape(TR, TAPS * TR)
    S["wr1"] = mixed(I["L3_ffn_Wr1"].T).reshape(128, CH * D)
    S["br1"] = I["L3_ffn_br1"].reshape(CH, KC).T
    S["gw3"] = chunks(I["L3_ffn_Wr2"].T, I["L3_ffn_br2"])
    S["b2_3"] = I["L3_ffn_b2"]

    same = (l[None, :] // SEQ == np.arange(PER_TILE)[:, None]).astype(f)
    mA, mB = np.zeros((128, TR), f), np.zeros((128, TR), f)
    mA[0:PER_TILE], mA[PER_TILE] = same, 1
    mB[0:PER_TILE], mB[PER_TILE] = same * BIG, -BIG
    S["same_q"], S["same_k"] = mA, np.tile(mB, (1, 4))

    O = {"patches": patches}
    for p, items in PACKS.items():
        blob = np.zeros((128, sum(c for _, _, c in items)), f)
        at = 0
        for name, rows, cols in items:
            blob[0:rows, at:at + cols] = S[name]
            at += cols
        O[p] = blob

    def up(pairs):
        e, p = pairs.shape[:2]
        return np.ascontiguousarray(mixed(pairs.reshape(e, p * 256, D).transpose(2, 0, 1)).transpose(2, 0, 1, 3))

    def down(w):
        return np.ascontiguousarray(w.reshape(w.shape[0], -1, 128, D).transpose(0, 2, 1, 3))

    def with_shared(s, w):
        return np.concatenate([s[None], w])

    a0 = with_shared(I["L0_ffn_sWu"], I["L0_ffn_Wu"]).transpose(0, 2, 1)
    g0 = with_shared(I["L0_ffn_sWg"], I["L0_ffn_Wg"]).transpose(0, 2, 1)
    O["W1_0"] = up(np.stack([a0, g0], 1)[:, None])
    O["W2_0"] = down(with_shared(I["L0_ffn_sWd"], I["L0_ffn_Wd"]))
    a1 = with_shared(I["L1_ffn_sw1"], I["L1_ffn_w1"])
    g1 = with_shared(I["L1_ffn_sw3"], I["L1_ffn_w3"])
    O["W1_1"] = up(np.stack([a1, g1], 1)[:, None])
    O["W2_1"] = down(with_shared(I["L1_ffn_sw2"], I["L1_ffn_w2"]).transpose(0, 2, 1))
    w = I["L2_ffn_mlp1_w"].reshape(16, 3, 128, 2, D).transpose(0, 1, 3, 2, 4)
    O["W1_2"] = up(w)
    O["W2_2"] = down(I["L2_ffn_mlp2_w"].transpose(0, 2, 1))
    O["W1_3"] = up(I["L3_ffn_W1"].reshape(8, 3, 2, 128, D))
    O["bias_0"] = np.ascontiguousarray(np.stack([with_shared(I["L0_ffn_sbu"], I["L0_ffn_bu"]),
                                                 with_shared(I["L0_ffn_sbg"], I["L0_ffn_bg"])], 2))
    b = I["L2_ffn_mlp1_b"].reshape(16, 3, 128, 2).transpose(0, 2, 1, 3)
    O["bias_2"] = np.ascontiguousarray(b.reshape(16, 128, 6))
    O["bias_3"] = np.ascontiguousarray(I["L3_ffn_b1"].reshape(8, 6, 128).transpose(0, 2, 1))
    O["W2_3"] = down(I["L3_ffn_W2"].transpose(0, 2, 1))
    return O


def kernel(**inputs):
    import concourse.bacc as bacc
    from concourse.bass_utils import run_bass_kernel_spmd

    arrays = layout({k: np.asarray(v) for k, v in inputs.items()})
    nc = bacc.Bacc("TRN2", target_bir_lowering=False, num_devices=1)
    A = {k: nc.dram_tensor(k + "_dram", a.shape, mybir.dt.from_np(a.dtype), kind="ExternalInput").ap()
         for k, a in arrays.items()}
    out = nc.dram_tensor("out_dram", (TOKENS, D), F32, kind="ExternalOutput").ap()
    vit_tower(nc, A, out)
    r = run_bass_kernel_spmd(nc, [{k + "_dram": a for k, a in arrays.items()}], core_ids=[0])
    return r.results[0]["out_dram"].reshape(IMAGES, SEQ, D)
```
